# Optimizing a Trainium2 kernel written in Bass

```python
import numpy as np
import jax
import jax.numpy as jnp

def _softmax(x, axis=-1):
    return jax.nn.softmax(x, axis=axis)

def _gelu(x):
    return jax.nn.gelu(x, approximate=True)

def _silu(x):
    return jax.nn.silu(x)

def _sigmoid(x):
    return jax.nn.sigmoid(x)

def _layernorm(x, axis=-1, eps=1e-05):
    m = jnp.mean(x, axis=axis, keepdims=True)
    v = jnp.var(x, axis=axis, keepdims=True)
    return (x - m) / jnp.sqrt(v + eps)

def _scatter_add(tgt, idx, src, axis=0):
    return tgt.at[idx].add(src)

def _segment_sum(src, seg, n):
    return jax.ops.segment_sum(src, seg, n)
kernel_name = 'mk_perceiver_d1_seqx_r8_071ef0'

def setup_inputs(seed: int=0):
    np.random.seed(seed)
    _w = jnp.asarray

    def _rec_inputs():
        import jax
        import jax.numpy as jnp
        _rk = jax.random.key(seed)
        x = -0.0003929 + 0.9999 * jax.random.normal(jax.random.fold_in(_rk, 1), (16, 64, 256), jnp.float32)
        _lenS = 64 - jax.random.randint(jax.random.fold_in(_rk, 7), (16,), 0, max(1, 64 // 4) + 1, jnp.int32)
        _lenS2 = 1601 - jax.random.randint(jax.random.fold_in(_rk, 8), (16,), 0, max(1, 1601 // 4) + 1, jnp.int32)
        _ctx_2048P = jax.random.normal(jax.random.fold_in(_rk, 11), (16, 16, 256), jnp.float32)
        _ctx_2048c = jax.random.dirichlet(jax.random.fold_in(_rk, 511), 0.3 * jnp.ones((16,), jnp.float32), (16, 1601))
        _ctx_2048t = jnp.einsum('bsk,bkd->bsd', _ctx_2048c, _ctx_2048P)
        _ctx_2048t = _ctx_2048t * jax.lax.rsqrt(jnp.mean(jnp.square(_ctx_2048t)) + 1e-12) * 0.953939
        ctx_2048 = -0.000514642 + 1.00011 * (_ctx_2048t + 0.3 * jax.random.normal(jax.random.fold_in(_rk, 611), (16, 1601, 256), jnp.float32))
        _validS = jnp.arange(64)[None, :] < _lenS[:, None]
        _validS2 = jnp.arange(1601)[None, :] < _lenS2[:, None]
        _causal = jnp.tril(jnp.ones((64, 64), dtype=bool))
        mask_BxSxS2_ff0 = jnp.where(jnp.ones((16, 64, 1601), dtype=bool), 0.0, -1000000000.0).astype(jnp.float32)
        return (x, ctx_2048, mask_BxSxS2_ff0)
    x, ctx_2048, mask_BxSxS2_ff0 = _rec_inputs()

    def _L0_xattn_setup():
        import jax, jax.numpy as jnp
        import numpy as np
        NUM_HEADS = 16
        EPS = 1e-08

        def _dyn_quant(x):
            s = jnp.maximum(jnp.max(jnp.abs(x), axis=-1, keepdims=True) / 127.0, EPS)
            q = jnp.clip(jnp.round(x / s), -127.0, 127.0)
            return (q, s)

        def _quant_weight(w):
            s = jnp.maximum(jnp.max(jnp.abs(w), axis=1, keepdims=True) / 127.0, EPS)
            q = jnp.clip(jnp.round(w / s), -127.0, 127.0)
            return (q, s)

        def _w8a8_linear(x, w, b):
            qx, sx = _dyn_quant(x)
            qw, sw = _quant_weight(w)
            y = jnp.einsum('bnc,oc->bno', qx, qw) * (sx * sw[:, 0])
            return y + b
        key = jax.random.key(seed)
        ks = jax.random.split(key, 9)
        B, N, L, C = (2, 512, 64, 256)
        sc = 0.02
        return {'x': jax.random.normal(ks[0], (B, N, C), jnp.float32), 'cond': jax.random.normal(ks[1], (B, L, C), jnp.float32), 'mask': jnp.zeros((B, N, L), jnp.float32), 'wq': jax.random.normal(ks[2], (C, C), jnp.float32) * sc, 'bq': jnp.zeros((C,), jnp.float32), 'wk': jax.random.normal(ks[3], (C, C), jnp.float32) * sc, 'bk': jnp.zeros((C,), jnp.float32), 'wv': jax.random.normal(ks[4], (C, C), jnp.float32) * sc, 'bv': jnp.zeros((C,), jnp.float32), 'wo': jax.random.normal(ks[5], (C, C), jnp.float32) * sc, 'bo': jnp.zeros((C,), jnp.float32)}
    _L0_xattn_all = _L0_xattn_setup()
    _L0_xattn_in = {k: v for k, v in _L0_xattn_all.items() if k in ('wq', 'bq', 'wk', 'bk', 'wv', 'bv', 'wo', 'bo')}
    del _L0_xattn_all

    def _L0_attn_setup():
        import jax, jax.numpy as jnp
        import numpy as np
        SCALE_BASE = 64
        EPS = 1e-05

        def _xpos_terms(seq_len, d):
            half = d // 2
            xscale = (jnp.arange(0, d, 2, dtype=jnp.float32) + 0.4 * d) / (1.4 * d)
            pos = jnp.arange(seq_len, dtype=jnp.float32)
            scale = xscale[None, :] ** (pos[:, None] / SCALE_BASE)
            inv_freq = 1.0 / 10000.0 ** (jnp.arange(half, dtype=jnp.float32) / half)
            sinu = pos[:, None] * inv_freq[None, :]
            return (jnp.sin(sinu), jnp.cos(sinu), scale)

        def _dup(t):
            return jnp.repeat(t, 2, axis=-1)

        def _rot(x):
            x1 = x[..., ::2]
            x2 = x[..., 1::2]
            return jnp.stack((-x2, x1), axis=-1).reshape(x.shape)

        def _apply_xpos(x, sin, cos, scale):
            c = _dup(cos * scale)
            s = _dup(sin * scale)
            return x * c + _rot(x) * s
        key = jax.random.key(seed)
        ks = jax.random.split(key, 6)
        B, S, H, nheads = (2, 128, 256, 16)
        d = H // nheads
        X = jax.random.normal(ks[0], (B, S, H), dtype=jnp.float32)
        W_Q = jax.random.normal(ks[1], (nheads, H, d), dtype=jnp.float32) / H
        W_K = jax.random.normal(ks[2], (nheads, H, d), dtype=jnp.float32) / H
        W_V = jax.random.normal(ks[3], (nheads, H, d), dtype=jnp.float32) / H
        W_G = jax.random.normal(ks[4], (H, H), dtype=jnp.float32) / H
        W_O = jax.random.normal(ks[5], (H, H), dtype=jnp.float32) / H
        gn_weight = jnp.ones((H,), dtype=jnp.float32)
        gn_bias = jnp.zeros((H,), dtype=jnp.float32)
        return {'X': X, 'W_Q': W_Q, 'W_K': W_K, 'W_V': W_V, 'W_G': W_G, 'W_O': W_O, 'gn_weight': gn_weight, 'gn_bias': gn_bias}
    _L0_attn_all = _L0_attn_setup()
    _L0_attn_in = {k: v for k, v in _L0_attn_all.items() if k in ('W_Q', 'W_K', 'W_V', 'W_G', 'W_O', 'gn_weight', 'gn_bias')}
    del _L0_attn_all

    def _L0_ffn_setup():
        import jax, jax.numpy as jnp
        import numpy as np
        H = 256
        E = 16
        K = 4
        I = 176
        IS = 176 * 2
        B, S = (1, 128)
        key = jax.random.key(seed)
        ks = jax.random.split(key, 9)
        scale = 0.02
        return {'hidden_states': jax.random.normal(ks[0], (B, S, H), dtype=jnp.float32), 'gate_w': jax.random.normal(ks[1], (E, H), dtype=jnp.float32) * scale, 'w_gate': jax.random.normal(ks[2], (E, H, I), dtype=jnp.float32) * scale, 'w_up': jax.random.normal(ks[3], (E, H, I), dtype=jnp.float32) * scale, 'w_down': jax.random.normal(ks[4], (E, I, H), dtype=jnp.float32) * scale, 'sw_gate': jax.random.normal(ks[5], (H, IS), dtype=jnp.float32) * scale, 'sw_up': jax.random.normal(ks[6], (H, IS), dtype=jnp.float32) * scale, 'sw_down': jax.random.normal(ks[7], (IS, H), dtype=jnp.float32) * scale}
    _L0_ffn_all = _L0_ffn_setup()
    _L0_ffn_in = {k: v for k, v in _L0_ffn_all.items() if k in ('gate_w', 'w_gate', 'w_up', 'w_down', 'sw_gate', 'sw_up', 'sw_down')}
    del _L0_ffn_all
    return {'x': x, 'ctx_2048': ctx_2048, 'mask_BxSxS2_ff0': mask_BxSxS2_ff0, 'L0_xattn_wq': _L0_xattn_in['wq'], 'L0_xattn_bq': _L0_xattn_in['bq'], 'L0_xattn_wk': _L0_xattn_in['wk'], 'L0_xattn_bk': _L0_xattn_in['bk'], 'L0_xattn_wv': _L0_xattn_in['wv'], 'L0_xattn_bv': _L0_xattn_in['bv'], 'L0_xattn_wo': _L0_xattn_in['wo'], 'L0_xattn_bo': _L0_xattn_in['bo'], 'L0_attn_W_Q': _L0_attn_in['W_Q'], 'L0_attn_W_K': _L0_attn_in['W_K'], 'L0_attn_W_V': _L0_attn_in['W_V'], 'L0_attn_W_G': _L0_attn_in['W_G'], 'L0_attn_W_O': _L0_attn_in['W_O'], 'L0_attn_gn_weight': _L0_attn_in['gn_weight'], 'L0_attn_gn_bias': _L0_attn_in['gn_bias'], 'L0_ffn_gate_w': _L0_ffn_in['gate_w'], 'L0_ffn_w_gate': _L0_ffn_in['w_gate'], 'L0_ffn_w_up': _L0_ffn_in['w_up'], 'L0_ffn_w_down': _L0_ffn_in['w_down'], 'L0_ffn_sw_gate': _L0_ffn_in['sw_gate'], 'L0_ffn_sw_up': _L0_ffn_in['sw_up'], 'L0_ffn_sw_down': _L0_ffn_in['sw_down']}

def reference(x, ctx_2048, mask_BxSxS2_ff0, L0_xattn_wq, L0_xattn_bq, L0_xattn_wk, L0_xattn_bk, L0_xattn_wv, L0_xattn_bv, L0_xattn_wo, L0_xattn_bo, L0_attn_W_Q, L0_attn_W_K, L0_attn_W_V, L0_attn_W_G, L0_attn_W_O, L0_attn_gn_weight, L0_attn_gn_bias, L0_ffn_gate_w, L0_ffn_w_gate, L0_ffn_w_up, L0_ffn_w_down, L0_ffn_sw_gate, L0_ffn_sw_up, L0_ffn_sw_down):
    import jax
    import jax.numpy as jnp

    def _L0_xattn_ref(x, cond, mask, wq, bq, wk, bk, wv, bv, wo, bo):
        import jax, jax.numpy as jnp
        import numpy as np
        NUM_HEADS = 16
        EPS = 1e-08

        def _dyn_quant(x):
            s = jnp.maximum(jnp.max(jnp.abs(x), axis=-1, keepdims=True) / 127.0, EPS)
            q = jnp.clip(jnp.round(x / s), -127.0, 127.0)
            return (q, s)

        def _quant_weight(w):
            s = jnp.maximum(jnp.max(jnp.abs(w), axis=1, keepdims=True) / 127.0, EPS)
            q = jnp.clip(jnp.round(w / s), -127.0, 127.0)
            return (q, s)

        def _w8a8_linear(x, w, b):
            qx, sx = _dyn_quant(x)
            qw, sw = _quant_weight(w)
            y = jnp.einsum('bnc,oc->bno', qx, qw) * (sx * sw[:, 0])
            return y + b
        B, N, C = x.shape
        L = cond.shape[1]
        H = NUM_HEADS
        D = C // H
        inv_sqrt_d = np.float32(1.0 / np.sqrt(D))
        q = _w8a8_linear(x, wq, bq).reshape(B, N, H, D).transpose(0, 2, 1, 3)
        k = (cond @ wk.T + bk).reshape(B, L, H, D).transpose(0, 2, 1, 3)
        v = (cond @ wv.T + bv).reshape(B, L, H, D).transpose(0, 2, 1, 3)
        scores = jnp.einsum('bhnd,bhld->bhnl', q, k) * inv_sqrt_d + mask[:, None]
        attn = jax.nn.softmax(scores, axis=-1)
        o = jnp.einsum('bhnl,bhld->bhnd', attn, v)
        o = o.transpose(0, 2, 1, 3).reshape(B, N, C)
        return _w8a8_linear(o, wo, bo)

    def _L0_attn_ref(X, W_Q, W_K, W_V, W_G, W_O, gn_weight, gn_bias):
        import jax, jax.numpy as jnp
        import numpy as np
        SCALE_BASE = 64
        EPS = 1e-05

        def _xpos_terms(seq_len, d):
            half = d // 2
            xscale = (jnp.arange(0, d, 2, dtype=jnp.float32) + 0.4 * d) / (1.4 * d)
            pos = jnp.arange(seq_len, dtype=jnp.float32)
            scale = xscale[None, :] ** (pos[:, None] / SCALE_BASE)
            inv_freq = 1.0 / 10000.0 ** (jnp.arange(half, dtype=jnp.float32) / half)
            sinu = pos[:, None] * inv_freq[None, :]
            return (jnp.sin(sinu), jnp.cos(sinu), scale)

        def _dup(t):
            return jnp.repeat(t, 2, axis=-1)

        def _rot(x):
            x1 = x[..., ::2]
            x2 = x[..., 1::2]
            return jnp.stack((-x2, x1), axis=-1).reshape(x.shape)

        def _apply_xpos(x, sin, cos, scale):
            c = _dup(cos * scale)
            s = _dup(sin * scale)
            return x * c + _rot(x) * s
        B, S, H = X.shape
        nheads, _, d = W_Q.shape
        gammas = 1.0 - jnp.exp(jnp.linspace(np.log(1.0 / 32), np.log(1.0 / 64), nheads)).astype(jnp.float32)
        sin, cos, scale = _xpos_terms(S, d)
        Q = jnp.einsum('bsh,nhd->bnsd', X, W_Q)
        K = jnp.einsum('bsh,nhd->bnsd', X, W_K)
        V = jnp.einsum('bsh,nhd->bnsd', X, W_V)
        Q = _apply_xpos(Q, sin, cos, scale)
        K = _apply_xpos(K, sin, cos, 1.0 / scale)
        n = jnp.arange(S)[:, None]
        m = jnp.arange(S)[None, :]
        D = jnp.where(n >= m, gammas[:, None, None] ** (n - m).astype(jnp.float32), 0.0)
        ret = jnp.einsum('bnsd,bntd->bnst', Q, K) * D[None]
        Y = jnp.einsum('bnst,bntv->bnsv', ret, V)
        Y = jnp.transpose(Y, (0, 2, 1, 3)).reshape(B, S, nheads * d)
        Yg = Y.reshape(B, S, nheads, d)
        mu = Yg.mean(-1, keepdims=True)
        var = Yg.var(-1, keepdims=True)
        Yn = ((Yg - mu) / jnp.sqrt(var + EPS)).reshape(B, S, nheads * d)
        Yn = Yn * gn_weight + gn_bias
        G = X @ W_G
        gate = G * jax.nn.sigmoid(G)
        return gate * Yn @ W_O

    def _L0_ffn_ref(hidden_states, gate_w, w_gate, w_up, w_down, sw_gate, sw_up, sw_down):
        import jax, jax.numpy as jnp
        import numpy as np
        H = 256
        E = 16
        K = 4
        I = 176
        IS = 176 * 2
        B, S = (1, 128)
        orig_shape = hidden_states.shape
        x = hidden_states.reshape(-1, H)
        T = x.shape[0]
        logits = jnp.einsum('th,eh->te', x, gate_w)
        scores = jax.nn.softmax(logits, axis=-1)
        topk_w, topk_idx = jax.lax.top_k(scores, K)
        topk_w = topk_w / jnp.sum(topk_w, axis=-1, keepdims=True)
        combine = jnp.zeros((T, E), dtype=x.dtype)
        combine = combine.at[jnp.arange(T)[:, None], topk_idx].add(topk_w)
        g = jnp.einsum('th,ehi->tei', x, w_gate)
        u = jnp.einsum('th,ehi->tei', x, w_up)
        a = jax.nn.silu(g) * u
        a = a * combine[:, :, None]
        y = jnp.einsum('tei,eih->th', a, w_down)
        sg = x @ sw_gate
        su = x @ sw_up
        y = y + jax.nn.silu(sg) * su @ sw_down
        return y.reshape(orig_shape)
    x = x + _L0_xattn_ref(_layernorm(x, axis=-1), ctx_2048, mask_BxSxS2_ff0, L0_xattn_wq, L0_xattn_bq, L0_xattn_wk, L0_xattn_bk, L0_xattn_wv, L0_xattn_bv, L0_xattn_wo, L0_xattn_bo)
    x = x + _L0_attn_ref(_layernorm(x, axis=-1), L0_attn_W_Q, L0_attn_W_K, L0_attn_W_V, L0_attn_W_G, L0_attn_W_O, L0_attn_gn_weight, L0_attn_gn_bias)
    x = x + _L0_ffn_ref(_layernorm(x, axis=-1), L0_ffn_gate_w, L0_ffn_w_gate, L0_ffn_w_up, L0_ffn_w_down, L0_ffn_sw_gate, L0_ffn_sw_up, L0_ffn_sw_down)
    return x

_drawn_inputs = setup_inputs


def setup_inputs(seed=0):
    import zlib

    import numpy as np

    out = dict(_drawn_inputs(seed))
    spreads = {'L0_xattn_bq': (0.0, 0.8),
     'L0_xattn_bk': (0.0, 0.8),
     'L0_xattn_bv': (0.0, 0.1),
     'L0_xattn_bo': (0.0, 0.1),
     'L0_attn_gn_weight': (1.0, 0.6),
     'L0_attn_gn_bias': (0.0, 0.8)}
    factors = {'L0_xattn_wq': 8.0,
     'L0_xattn_wk': 8.0,
     'L0_attn_W_Q': 8.0,
     'L0_attn_W_K': 8.0,
     'L0_attn_W_V': 8.0,
     'L0_attn_W_G': 8.0,
     'L0_attn_W_O': 8.0,
     'L0_ffn_gate_w': 8.0,
     'L0_ffn_w_gate': 7.9,
     'L0_ffn_w_up': 7.863,
     'L0_ffn_w_down': 7.823,
     'L0_ffn_sw_gate': 2.909,
     'L0_ffn_sw_up': 2.867,
     'L0_ffn_sw_down': 2.873}
    for name, (base, spread) in spreads.items():
        noise = np.random.default_rng([zlib.crc32(name.encode()), seed]).standard_normal(out[name].shape)
        drawn = base * np.exp(spread * noise) if base else spread * noise
        out[name] = jnp.asarray(drawn.astype(out[name].dtype))
    for name, factor in factors.items():
        out[name] = (out[name] * factor).astype(out[name].dtype)
    return out
```

```python
from contextlib import ExitStack

import concourse.bass as bass
from concourse import mybir
from concourse.alu_op_type import AluOpType as ALU

F32 = mybir.dt.float32
BF16 = mybir.dt.bfloat16
ACT = mybir.ActivationFunctionType
AX = mybir.AxisListType

P = 128
B, N, C = 16, 64, 256
L = 1601
H, D = 16, 16
KC = C // P
HH = H // KC
TILES = B * N // P
PAIRS = H // 2
UNITS = 2 * PAIRS
LT = -(-L // P)
LAST = L - (LT - 1) * P
CH = [401, 400, 400, 400]
CO = [0, 401, 801, 1201]
E, I, TOPK = 16, 176, 4
IS = 2 * I
MT = E * I // P
ST = -(-IS // P)
JT = MT + ST
ROUND = 12582912.0
BIG = 3.0e38
LN_EPS, Q_EPS, GN_EPS = 1e-5, 1e-8, 1e-5


def perceiver_program(nc, x, ctx_t, mask, wq, wk_t, wv_t, wo, bq, bo_b, bv_b, w_qkvg, w_o, gnw_b, gnb_b,
                      gate_t, w_gu, w_dn, ident, half_sel, group_sel, cos_t, sin_t, decay, tri, expand, bk, out):
    with ExitStack() as ctx:
        def sem(name):
            return ctx.enter_context(nc.semaphore(name))

        def sb(stack, name, shape, dt=F32):
            return stack.enter_context(nc.sbuf_tensor(name, shape, dt))

        events = {}

        def ev(name):
            if name not in events:
                events[name] = sem(name)
            return events[name]

        def need(e, name, t):
            e.wait_ge(ev(name), t + 1)

        def hold(e):
            e.nop(nofuse=True)

        bank_s = [ctx.enter_context(nc.psum_tensor(f"scores{n}", [P, 512], F32)) for n in range(3)]
        bank_t = [ctx.enter_context(nc.psum_tensor(f"turned{n}", [P, 512], F32)) for n in range(2)]
        bank_x = ctx.enter_context(nc.psum_tensor("kv_proj", [P, 512], F32))
        bank_c = ctx.enter_context(nc.psum_tensor("chain", [P, 512], F32))
        bank_o = ctx.enter_context(nc.psum_tensor("attn_out", [P, 512], F32))

        ident_f = sb(ctx, "ident_f", [P, P])
        ident_b = sb(ctx, "ident_b", [P, P], BF16)
        o_all = sb(ctx, "o_all", [P, TILES, C])
        qt_all = sb(ctx, "qt_all", [P, KC, TILES * P])
        wo_qt = sb(ctx, "wo_qt", [P, KC, C], BF16)
        swo_b = sb(ctx, "swo_b", [P, C])
        half = sb(ctx, "half", [P, HH])
        group = sb(ctx, "group", [P, 4])
        half_exp = sb(ctx, "power", [P, H])

        with ExitStack() as ph:
            xs = sb(ph, "xs", [P, TILES, C])
            w_in = sb(ph, "w_in", [P, 2, KC, C])
            w_q = sb(ph, "w_quant", [P, 2, KC, C])
            w_i = sb(ph, "w_int", [P, 2, KC, C], BF16)
            w_amax = sb(ph, "w_amax", [P, 2 * KC])
            w_s = sb(ph, "w_scale", [P, 2 * KC])
            w_r = sb(ph, "w_rscale", [P, 2 * KC])
            wq_qt = sb(ph, "wq_qt", [P, KC, C], BF16)
            diag = sb(ph, "diag", [P, KC, P])
            ones = sb(ph, "ones", [P, P])
            bq_s = sb(ph, "bq_s", [P, KC])
            bq4 = sb(ph, "bq4", [P, KC])
            swq4 = sb(ph, "swq4", [P, KC])
            stats = sb(ph, "q_stats", [P, 6])
            mv = sb(ph, "q_mv", [P, 2])
            rstd = sb(ph, "q_rstd", [P, 2])
            xn = sb(ph, "q_xn", [P, C])
            sc = sb(ph, "q_sc", [P, 4])
            xq = sb(ph, "q_xq", [P, C])
            xi = sb(ph, "q_xi", [P, C], BF16)
            xit = sb(ph, "q_xit", [P, KC, P], BF16)
            qtok = sb(ph, "q_tok", [P, C])
            s_in, s_w, s_wdve = sem("in_loaded"), sem("w_in_loaded"), sem("w_dve")
            s_link = sem("q_dve")
            blk = ph.enter_context(nc.Block())

            @blk.sync
            def _(sp):
                sp.dma_start(w_in[:, 0], wq.rearrange("(a p) c -> p a c", p=P)).then_inc(s_w, 16)
                sp.dma_start(w_in[:, 1], wo.rearrange("(a p) c -> p a c", p=P)).then_inc(s_w, 16)
                sp.dma_start(ident_f[:, :], ident).then_inc(s_w, 16)
                sp.dma_start(bq_s[:, :], bq).then_inc(s_w, 16)
                sp.dma_start(xs[:, :, :], x.rearrange("(t p) c -> p t c", p=P)).then_inc(s_in, 16)
                sp.dma_start(half[:, :], half_sel).then_inc(s_in, 16)
                sp.dma_start(group[:, :], group_sel).then_inc(s_in, 16)

            @blk.gpsimd
            def _(pool):
                pool.memset(half_exp[:, :], -0.5).then_inc(ev("consts_set"), 1)
                pool.memset(ones[:, :], 1.0).then_inc(ev("consts_set"), 1)
                pool.wait_ge(ev("consts_set"), 2)
                with pool.Fori(0, TILES) as t:
                    need(pool, "q_mv_ready", t)
                    hold(pool)
                    pool.tensor_scalar(rstd[:, 0:1], mv[:, 1:2], LN_EPS, None, ALU.add).then_inc(ev("q_veps"), 1)
                    need(pool, "q_veps", t)
                    pool.tensor_tensor(rstd[:, 1:2], rstd[:, 0:1], half_exp[:, 0:1], ALU.pow).then_inc(ev("q_rstd_ready"), 1)

            @blk.vector
            def _(dve):
                done = [0]

                def link(ins):
                    done[0] += 1
                    ins.then_inc(s_wdve, 1)
                    dve.wait_ge(s_wdve, done[0])

                dve.wait_ge(s_w, 64)
                link(dve.tensor_copy(ident_b[:, :], ident_f[:, :]))
                link(dve.tensor_reduce(w_amax[:, :], w_in[:, :, :, :].rearrange("p m a c -> p (m a) c"), AX.X, ALU.max,
                                       apply_absolute_value=True))
                link(dve.tensor_scalar(w_s[:, :], w_amax[:, :], 1.0 / 127.0, Q_EPS, ALU.mult, ALU.max))
                link(dve.reciprocal(w_r[:, :], w_s[:, :]))
                for m in range(2):
                    for a in range(KC):
                        link(dve.tensor_scalar(w_q[:, m, a], w_in[:, m, a], w_r[:, KC * m + a:KC * m + a + 1], 127.0,
                                               ALU.mult, ALU.min))
                link(dve.tensor_scalar(w_q[:, :, :, :], w_q[:, :, :, :], -127.0, ROUND, ALU.max, ALU.add))
                dve.tensor_scalar(w_i[:, :, :, :], w_q[:, :, :, :], -ROUND, None, ALU.add).then_inc(ev("w_int_ready"), 1)
                for a in range(KC):
                    link(dve.tensor_scalar(diag[:, a], ident_f[:, :], w_s[:, KC + a:KC + a + 1], None, ALU.mult))
                link(dve.tensor_scalar(swq4[:, :], w_s[:, 0:KC], float(D) ** -0.5, None, ALU.mult))
                dve.tensor_scalar(bq4[:, :], bq_s[:, :], float(D) ** -0.5, None, ALU.mult).then_inc(ev("diag_ready"), 1)
                for m, dst in enumerate((wq_qt, wo_qt)):
                    dve.wait_ge(ev("w_turned"), m + 1)
                    dve.tensor_copy(dst[:, :, :].rearrange("p k o -> p (k o)"),
                                    bank_t[m][:, :].bitcast(BF16)[:, 0:KC * C]).then_inc(ev("w_copied"), 1)
                dve.wait_ge(ev("swo_rows"), 1)
                dve.tensor_copy(swo_b[:, :], bank_x[:, 0:C]).then_inc(ev("w_copied"), 1)

                dve.wait_ge(s_in, 48)
                with dve.Fori(0, TILES) as t:
                    n = [0]
                    links = 9

                    def step(ins):
                        n[0] += 1
                        ins.then_inc(s_link, 1)
                        dve.wait_ge(s_link, t * links + n[0])

                    step(dve.bn_stats(stats[:, :], xs[:, t, :]))
                    hold(dve)
                    dve.bn_aggr(mv[:, :], stats[:, :]).then_inc(ev("q_mv_ready"), 1)
                    need(dve, "q_rstd_ready", t)
                    hold(dve)
                    step(dve.tensor_scalar(xn[:, :], xs[:, t, :], mv[:, 0:1], rstd[:, 1:2], ALU.subtract, ALU.mult))
                    step(dve.tensor_reduce(sc[:, 0:1], xn[:, :], AX.X, ALU.max, apply_absolute_value=True))
                    step(dve.tensor_scalar(sc[:, 1:2], sc[:, 0:1], 1.0 / 127.0, Q_EPS, ALU.mult, ALU.max))
                    step(dve.reciprocal(sc[:, 2:3], sc[:, 1:2]))
                    step(dve.tensor_scalar(xn[:, :], xn[:, :], sc[:, 2:3], 127.0, ALU.mult, ALU.min))
                    step(dve.tensor_scalar(xq[:, :], xn[:, :], -127.0, ROUND, ALU.max, ALU.add))
                    dve.tensor_scalar(xi[:, :], xq[:, :], -ROUND, None, ALU.add).then_inc(ev("q_int_ready"), 1)
                    need(dve, "q_proj_done", t)
                    dve.tensor_scalar(qtok[:, :], bank_c[:, 0:C], sc[:, 1:2], None, ALU.mult).then_inc(ev("q_tok_ready"), 1)
                    need(dve, "q_turned", t)
                    hold(dve)
                    for m in range(KC):
                        step(dve.tensor_scalar(qt_all[:, m, bass.ds(t * P, P)], bank_c[:, m * P:(m + 1) * P],
                                               swq4[:, m:m + 1], bq4[:, m:m + 1], ALU.mult, ALU.add))
                    assert n[0] == links

            @blk.scalar
            def _(act):
                with act.Fori(0, TILES) as t:
                    need(act, "q_int_turned", t)
                    act.activation(xit[:, :, :].rearrange("p k n -> p (k n)"), bank_c[:, :].bitcast(BF16)[:, 0:C],
                                   ACT.Copy).then_inc(ev("q_xit_ready"), 1)

            @blk.tensor
            def _(pe):
                pe.wait_ge(ev("w_int_ready"), 1)
                for m in range(2):
                    tb = bank_t[m][:, :].bitcast(BF16)
                    for k in range(KC):
                        for a in range(KC):
                            mm = pe.transpose(tb[:, k * C + a * P:k * C + a * P + P], w_i[:, m, a, k * P:(k + 1) * P], ident_b[:, :])
                    mm.then_inc(ev("w_turned"), 1)
                pe.wait_ge(ev("diag_ready"), 1)
                pe.wait_ge(ev("consts_set"), 2)
                pe.matmul(bank_x[:, 0:C], ones[:, :], diag[:, :, :].rearrange("p a o -> p (a o)"),
                          start=True, stop=True).then_inc(ev("swo_rows"), 1)
                pe.wait_ge(ev("w_copied"), 3)
                with pe.Fori(0, TILES) as t:
                    need(pe, "q_int_ready", t)
                    cb = bank_c[:, :].bitcast(BF16)
                    for k in range(KC):
                        mm = pe.transpose(cb[:, k * P:(k + 1) * P], xi[:, k * P:(k + 1) * P], ident_b[:, :])
                    mm.then_inc(ev("q_int_turned"), 1)
                    need(pe, "q_xit_ready", t)
                    for k in range(KC):
                        mm = pe.matmul(bank_c[:, 0:C], xit[:, k, :], wq_qt[:, k, :], start=(k == 0), stop=(k == KC - 1))
                    mm.then_inc(ev("q_proj_done"), 1)
                    need(pe, "q_tok_ready", t)
                    for m in range(KC):
                        mm = pe.transpose(bank_c[:, m * P:(m + 1) * P], qtok[:, m * P:(m + 1) * P], ident_f[:, :])
                    mm.then_inc(ev("q_turned"), 1)

        with ExitStack() as ph:
            ct = [sb(ph, f"ctx{s}", [P, KC, L]) for s in range(2)]
            mk = [sb(ph, f"mask{s}", [P, L]) for s in range(2)]
            kt = [sb(ph, f"keys{s}", [P, KC, L]) for s in range(2)]
            vt = [sb(ph, f"values{s}", [P, LT, C]) for s in range(2)]
            qb = [sb(ph, f"queries{s}", [P, KC, HH, N]) for s in range(2)]
            sm = [sb(ph, f"probs{s}", [P, L]) for s in range(2)]
            pt = [sb(ph, f"probs_t{n}", [P, LT, 2, P]) for n in range(4)]
            wk = sb(ph, "wk", [P, KC, C])
            wv = sb(ph, "wv", [P, KC, C])
            bks = sb(ph, "bks", [P, KC])
            nmax = sb(ph, "neg_max", [P, 2, 4])
            sums = [sb(ph, f"sums{s}", [P, PAIRS]) for s in range(2)]
            rsum = sb(ph, "rsum", [P, PAIRS])
            rtok = sb(ph, "rtok", [P, PAIRS, 2])
            ot4 = sb(ph, "ot4", [P, KC, 4, N])
            ot = sb(ph, "ot", [P, KC, P])
            s_wkv = sem("wkv_loaded")
            s_ct = [sem(f"ctx_loaded{s}") for s in range(2)]
            s_mk = [sem(f"mask_loaded{s}") for s in range(2)]
            s_item = sem("kv_item_done")
            s_keva, s_kevd = sem("kv_out_act"), sem("kv_out_dve")
            s_sc = sem("scores_done")
            s_ttr = sem("scores_masked")
            s_exp = sem("exp_done")
            s_t = sem("turned")
            s_ta, s_td = sem("turned_out_act"), sem("turned_out_dve")
            s_pv = sem("pv_done")
            s_of = sem("attn_out_read")
            s_qb = sem("queries_set")
            s_rs = sem("sums_read")
            s_fin = sem("attn_dve")
            blk = ph.enter_context(nc.Block())
            LASTI = TILES - 1
            FINS = 7
            ITEMS = 2 * PAIRS - 1

            def items(v):
                return [n for n in (2 * v, 2 * v + 1) if n < ITEMS]

            @blk.sync
            def _(sp):
                sp.dma_start(wk[:, :, :], wk_t.rearrange("(k p) o -> p k o", p=P)).then_inc(s_wkv, 16)
                sp.dma_start(wv[:, :, :], wv_t.rearrange("(k p) o -> p k o", p=P)).then_inc(s_wkv, 16)
                sp.dma_start(bks[:, :], bk).then_inc(s_wkv, 16)

                def load(b, s):
                    sp.dma_start(ct[s][:, :, :], ctx_t[b].rearrange("(k p) l -> p k l", p=P)).then_inc(s_ct[s], 16)

                def load_mask(b, s):
                    for j in range(2):
                        sp.dma_start(mk[s][j * N:(j + 1) * N, :], mask[b]).then_inc(s_mk[s], 16)

                for s in range(2):
                    load(s, s)
                    load_mask(s, s)
                with sp.Fori(0, LASTI) as i:
                    for s in range(2):
                        sp.wait_ge(s_item, ITEMS * (2 * i + s + 1))
                        load(2 * i + 2 + s, s)
                        sp.wait_ge(s_ttr, 4 * PAIRS * (2 * i + s + 1))
                        load_mask(2 * i + 2 + s, s)

            @blk.gpsimd
            def _(pool):
                def spread(b, s):
                    for m in range(KC):
                        q = qt_all[:, m, bass.ds(b * N, N)].unsqueeze(1).to_broadcast([P, HH, N])
                        mm = pool.tensor_tensor(qb[s][:, m], q, half[:, :].unsqueeze(2).to_broadcast([P, HH, N]), ALU.mult)
                    mm.then_inc(s_qb, 1)

                for s in range(2):
                    spread(s, s)
                with pool.Fori(0, LASTI) as i:
                    for s in range(2):
                        pool.wait_ge(s_sc, 4 * PAIRS * (2 * i + s + 1))
                        hold(pool)
                        spread(2 * i + 2 + s, s)

            @blk.tensor
            def _(pe):
                def item(s, n):
                    if n < 8:
                        m, c = n // 4, n % 4
                        for k in range(KC):
                            mm = pe.matmul(bank_x[:, 0:CH[c]], wk[:, k, m * P:(m + 1) * P],
                                           ct[s][:, k, CO[c]:CO[c] + CH[c]], start=(k == 0), stop=(k == KC - 1))
                    else:
                        for h, lt in enumerate(range(2 * (n - 8), min(2 * (n - 8) + 2, LT))):
                            rows = LAST if lt == LT - 1 else P
                            for k in range(KC):
                                mm = pe.matmul(bank_x[0:rows, h * C:(h + 1) * C], ct[s][:, k, lt * P:lt * P + rows],
                                               wv[:, k, :], start=(k == 0), stop=(k == KC - 1))
                    mm.then_inc(s_item, 1)

                def kv_step(b, s, loads, v, pos):
                    got = items(v)
                    if pos >= len(got):
                        return
                    first = isinstance(b, int) and b == 0
                    if v == 0 and pos == 0:
                        pe.wait_ge(s_ct[s], 16 * loads)
                    if pos == 1:
                        pe.wait_ge(s_keva, 8 * b + v + 1)
                    elif v > 0:
                        pe.wait_ge(s_kevd, 7 * b + v)
                    elif not first:
                        pe.wait_ge(s_keva, 8 * b)
                    item(s, got[pos])

                def scores(i, u):
                    ii, uu = (i, u) if u < UNITS else (i + 1, u - UNITS)
                    s, p = uu // PAIRS, uu % PAIRS
                    m = p // 4
                    if p == 0:
                        b = 2 * ii + s
                        pe.wait_ge(s_keva, 8 * b + 4)
                        pe.wait_ge(s_kevd, 7 * b + 4)
                        pe.wait_ge(s_qb, b + 1)
                    for c in range(4):
                        n = 4 * uu + c
                        if n >= 3:
                            pe.wait_ge(s_ttr, 64 * ii + n - 2)
                        elif not (isinstance(ii, int) and ii == 0):
                            pe.wait_ge(s_ttr, 64 * ii - {0: 0, 1: 2, 2: 1}[n])
                        pe.matmul(bank_s[n % 3][:, 0:CH[c]],
                                  qb[s][:, m, 2 * (p % 4):2 * (p % 4) + 2].rearrange("p h n -> p (h n)"),
                                  kt[s][:, m, CO[c]:CO[c] + CH[c]], start=True, stop=True).then_inc(s_sc, 1)

                def turn(i, u):
                    pe.wait_ge(s_exp, UNITS * i + u + 1)
                    for g in range(4):
                        uses = 2 * (UNITS * i + u) + g // 2
                        if not (isinstance(i, int) and i == 0 and u == 0 and g < 2):
                            pe.wait_ge(s_ta if g % 2 == 0 else s_td, uses)
                        for q, lt in enumerate(range(4 * g, min(4 * g + 4, LT))):
                            rows = LAST if lt == LT - 1 else P
                            mm = pe.transpose(bank_t[g % 2][0:rows, q * P:(q + 1) * P], sm[u % 2][:, lt * P:lt * P + rows],
                                              ident_f[:, :])
                        mm.then_inc(s_t, 1)

                def pv(i, u):
                    s, m = u // PAIRS, (u % PAIRS) // 4
                    half_no = (UNITS * i + u + 1)
                    pe.wait_ge(s_ta, 2 * half_no)
                    pe.wait_ge(s_td, 2 * half_no)
                    if m == 0:
                        b = 2 * i + s
                        pe.wait_ge(s_keva, 8 * b + 8)
                        pe.wait_ge(s_kevd, 7 * b + 7)
                        if not (isinstance(i, int) and i == 0 and s == 0):
                            pe.wait_ge(s_of, b)
                    for lt in range(LT):
                        rows = LAST if lt == LT - 1 else P
                        for g in range(2):
                            slot = (2 * (u // 4) + g) % 4
                            mm = pe.matmul(bank_o[g * 64:(g + 1) * 64, m * C:(m + 1) * C],
                                           vt[s][0:rows, lt, m * P + g * 64:m * P + (g + 1) * 64],
                                           pt[slot][0:rows, lt, :, :].rearrange("p j n -> p (j n)"),
                                           start=(lt == 0), stop=(lt == LT - 1), skip_group_check=True)
                    mm.then_inc(s_pv, 1)

                def out_turn(i):
                    pe.wait_ge(s_fin, FINS * i + FINS - 1)
                    for m in range(KC):
                        mm = pe.transpose(bank_c[:, m * P:(m + 1) * P], ot[:, m, :], ident_f[:, :])
                    mm.then_inc(ev("o_turned"), 1)

                def tile(i, last):
                    for u in range(UNITS):
                        s, v = u // PAIRS, u % PAIRS
                        ahead = not (last and s == 1)
                        turn(i, u)
                        if ahead:
                            kv_step(2 * i + s + 1, 1 - s, i + s + 1, v, 0)
                        if not (last and u + 2 >= UNITS):
                            scores(i, u + 2)
                        if ahead:
                            kv_step(2 * i + s + 1, 1 - s, i + s + 1, v, 1)
                        if u % 4 == 3:
                            pv(i, u)
                    out_turn(i)

                pe.wait_ge(s_wkv, 48)
                for v in range(PAIRS):
                    kv_step(0, 0, 1, v, 0)
                    kv_step(0, 0, 1, v, 1)
                scores(0, 0)
                scores(0, 1)
                tile(0, False)
                with pe.Fori(1, LASTI) as i:
                    tile(i, False)
                tile(LASTI, True)

            @blk.scalar
            def _(act):
                def kv_out(b, s, v):
                    act.wait_ge(s_item, ITEMS * b + 2 * v + 1)
                    n = 2 * v
                    if n < 8:
                        m, c = n // 4, n % 4
                        act.activation(kt[s][:, m, CO[c]:CO[c] + CH[c]], bank_x[:, 0:CH[c]], ACT.Identity,
                                       bias=bks[:, m:m + 1]).then_inc(s_keva, 1)
                    else:
                        lt = 2 * (n - 8)
                        if lt == LT - 1:
                            act.activation(vt[s][0:LAST, lt, :], bank_x[0:LAST, 0:C], ACT.Copy).then_inc(s_keva, 1)
                        else:
                            act.activation(vt[s][:, lt:lt + 2, :].rearrange("p t c -> p (t c)"), bank_x[:, :],
                                           ACT.Copy).then_inc(s_keva, 1)

                def exp(i, u):
                    ii, uu = (i, u) if u < UNITS else (i + 1, u - UNITS)
                    s, p = uu // PAIRS, uu % PAIRS
                    act.wait_ge(s_ttr, 64 * ii + 4 * uu + 4)
                    if p == 0 and not (isinstance(ii, int) and ii == 0):
                        act.wait_ge(s_rs, 2 * ii + s - 1)
                    hold(act)
                    act.activation(sm[uu % 2][:, :], sm[uu % 2][:, :], ACT.Exp, bias=nmax[:, uu % 2, 3:4], scale=-1.0,
                                   accum_out=sums[s][:, p:p + 1]).then_inc(s_exp, 1)

                def turned_out(i, u, g):
                    act.wait_ge(s_t, 4 * (UNITS * i + u) + g + 1)
                    dst = pt[(u // 2) % 4][:, 4 * g:4 * g + 4, u % 2, :]
                    if u % 4 == 0 and g == 0 and not (isinstance(i, int) and i == 0 and u < 8):
                        act.wait_ge(s_pv, 4 * i + u // 4 - 1)
                    act.activation(dst, bank_t[0][:, :].rearrange("p (t n) -> p t n", t=4), ACT.Copy).then_inc(s_ta, 1)

                def tile(i, last):
                    for u in range(UNITS):
                        s, v = u // PAIRS, u % PAIRS
                        turned_out(i, u, 0)
                        turned_out(i, u, 2)
                        if not (last and s == 1):
                            kv_out(2 * i + s + 1, 1 - s, v)
                        if not (last and u + 1 >= UNITS):
                            exp(i, u + 1)

                act.wait_ge(s_wkv, 48)
                for v in range(PAIRS):
                    kv_out(0, 0, v)
                exp(0, 0)
                tile(0, False)
                with act.Fori(1, LASTI) as i:
                    tile(i, False)
                tile(LASTI, True)

            @blk.vector
            def _(dve):
                fins = [0]

                def kv_out(b, s, v):
                    n = 2 * v + 1
                    if n >= ITEMS:
                        return
                    dve.wait_ge(s_item, ITEMS * b + 2 * v + 2)
                    if n < 8:
                        m, c = n // 4, n % 4
                        dve.tensor_scalar(kt[s][:, m, CO[c]:CO[c] + CH[c]], bank_x[:, 0:CH[c]], bks[:, m:m + 1], None,
                                          ALU.add).then_inc(s_kevd, 1)
                    else:
                        lt = 2 * (n - 8)
                        dve.tensor_copy(vt[s][:, lt:lt + 2, :].rearrange("p t c -> p (t c)"),
                                        bank_x[:, :]).then_inc(s_kevd, 1)

                def masked(i, u):
                    ii, uu = (i, u) if u < UNITS else (i + 1, u - UNITS)
                    s = uu // PAIRS
                    if uu % PAIRS == 0:
                        dve.wait_ge(s_mk[s], 32 * (ii + 1))
                        hold(dve)
                    for c in range(4):
                        if c:
                            dve.wait_ge(s_ttr, 64 * ii + 4 * uu + c)
                            hold(dve)
                        elif not (isinstance(ii, int) and ii == 0 and uu < 2):
                            dve.wait_ge(s_t, 4 * (UNITS * ii + uu - 1))
                            hold(dve)
                        dve.wait_ge(s_sc, 64 * ii + 4 * uu + c + 1)
                        hold(dve)
                        dve.tensor_tensor_reduce(
                            out=sm[uu % 2][:, CO[c]:CO[c] + CH[c]], in0=bank_s[(4 * uu + c) % 3][:, 0:CH[c]],
                            in1=mk[s][:, CO[c]:CO[c] + CH[c]], scale=-1.0,
                            scalar=nmax[:, uu % 2, c - 1:c] if c else BIG, op0=ALU.add, op1=ALU.min,
                            accum_out=nmax[:, uu % 2, c:c + 1]).then_inc(s_ttr, 1)

                def turned_out(i, u, g):
                    dve.wait_ge(s_t, 4 * (UNITS * i + u) + g + 1)
                    if u % 4 == 0 and g == 1 and not (isinstance(i, int) and i == 0 and u < 8):
                        dve.wait_ge(s_pv, 4 * i + u // 4 - 1)
                    rows, k = (LAST, 1) if g == 3 else (P, 4)
                    dve.tensor_copy(pt[(u // 2) % 4][0:rows, 4 * g:4 * g + k, u % 2, :],
                                    bank_t[1][0:rows, 0:k * P].rearrange("p (t n) -> p t n", t=k)).then_inc(s_td, 1)

                def step(i, ins):
                    fins[0] += 1
                    ins.then_inc(s_fin, 1)
                    dve.wait_ge(s_fin, FINS * i + fins[0])
                    hold(dve)

                def attn_out(i, s):
                    b = 2 * i + s
                    dve.wait_ge(s_pv, 2 * (b + 1))
                    dve.tensor_tensor(ot4[:, :, :, :], bank_o[:, :].rearrange("p (m g n) -> p m g n", m=KC, g=4),
                                      group[:, :].unsqueeze(1).unsqueeze(3).to_broadcast([P, KC, 4, N]),
                                      ALU.mult).then_inc(s_of, 1)
                    dve.wait_ge(s_of, b + 1)
                    if s == 0 and not (isinstance(i, int) and i == 0):
                        need(dve, "o_turned", i - 1)
                    step(i, dve.tensor_reduce(ot[:, :, s * N:(s + 1) * N], ot4[:, :, :, :].rearrange("p m g n -> p m n g"),
                                              AX.X, ALU.add))
                    dve.wait_ge(s_exp, PAIRS * (b + 1))
                    dve.reciprocal(rsum[:, :], sums[s][:, :]).then_inc(s_rs, 1)
                    dve.wait_ge(s_rs, b + 1)
                    for j in range(2):
                        step(i, dve.tensor_copy(rtok[s * N:(s + 1) * N, :, j], rsum[j * N:(j + 1) * N, :]))

                def tile(i, last):
                    fins[0] = 0
                    for u in range(UNITS):
                        s, v = u // PAIRS, u % PAIRS
                        turned_out(i, u, 1)
                        turned_out(i, u, 3)
                        if not (last and u + 2 >= UNITS):
                            masked(i, u + 2)
                        if not (last and s == 1):
                            kv_out(2 * i + s + 1, 1 - s, v)
                        if v == PAIRS - 1:
                            attn_out(i, s)
                    need(dve, "o_turned", i)
                    step(i, dve.tensor_tensor(o_all[:, bass.ds(i, 1), :].rearrange("p t (h d) -> p (t h) d", d=D),
                                              bank_c[:, 0:C].rearrange("p (h d) -> p h d", d=D),
                                              rtok[:, :, :].rearrange("p a j -> p (a j)").unsqueeze(2).to_broadcast([P, H, D]),
                                              ALU.mult))
                    assert fins[0] == FINS

                dve.wait_ge(s_wkv, 48)
                for v in range(PAIRS):
                    kv_out(0, 0, v)
                masked(0, 0)
                masked(0, 1)
                tile(0, False)
                with dve.Fori(1, LASTI) as i:
                    tile(i, False)
                tile(LASTI, True)

        chain_and_experts(nc, ctx, sb, sem, ev, need, hold, bank_s, bank_t, bank_x, bank_c, bank_o, ident_f, ident_b,
                          o_all, half, half_exp, wo_qt, swo_b, x, bo_b, bv_b, w_qkvg, w_o, gnw_b, gnb_b, gate_t,
                          w_gu, w_dn, cos_t, sin_t, decay, tri, expand, out)


def chain_and_experts(nc, ctx, sb, sem, ev, need, hold, bank_s, bank_t, bank_x, bank_c, bank_o, ident_f, ident_b,
                      o_all, half, half_exp, wo_qt, swo_b, x, bo_b, bv_b, w_qkvg, w_o, gnw_b, gnb_b, gate_t,
                      w_gu, w_dn, cos_t, sin_t, decay, tri, expand, out):
    with ExitStack() as keep:
        x3t = sb(keep, "x3t", [P, KC, TILES * P])
        comb = sb(keep, "comb", [3 * E + 1, TILES * P], BF16)

        with ExitStack() as ph:
            xb = sb(ph, "xb", [P, TILES, C])
            bo = sb(ph, "bo", [P, C])
            bv = sb(ph, "bv", [P, C])
            wr = sb(ph, "wr", [P, KC, 4 * C])
            wor = sb(ph, "wor", [P, KC, C])
            gnw = sb(ph, "gnw", [P, C])
            gnb = sb(ph, "gnb", [P, C])
            gw = sb(ph, "gw", [P, KC, E])
            cost = sb(ph, "cost", [P, 2, D])
            sint = sb(ph, "sint", [P, 2, D])
            dec = sb(ph, "dec", [P, H, N])
            lower = sb(ph, "lower", [P, E, E])
            oc = sb(ph, "oc", [P, C])
            oq = sb(ph, "oq", [P, C])
            oi = sb(ph, "oi", [P, C], BF16)
            sc = sb(ph, "sc", [P, 4])
            oqt = sb(ph, "oqt", [P, KC, P], BF16)
            x1 = sb(ph, "x1", [P, C])
            stats = sb(ph, "stats", [P, 6])
            mv = sb(ph, "mv", [P, 2])
            rstd = sb(ph, "rstd", [P, 2])
            xn = sb(ph, "xn", [P, C])
            xnt = sb(ph, "xnt", [P, KC, P])
            ra = sb(ph, "ra", [P, 2 * H, D])
            rb = sb(ph, "rb", [P, 2 * H, D])
            rqt = sb(ph, "rqt", [P, KC, P])
            rkt = sb(ph, "rkt", [P, KC, P])
            rqb = sb(ph, "rqb", [P, KC, 2, HH, N])
            rv = sb(ph, "rv", [P, C])
            gs = sb(ph, "gs", [P, C])
            ret = sb(ph, "ret", [P, KC, HH * N])
            yc = sb(ph, "yc", [P, H, D])
            ysq = sb(ph, "ysq", [P, H, D])
            gst = sb(ph, "gst", [P, 4, H])
            ht = sb(ph, "ht", [P, KC, P])
            x2 = sb(ph, "x2", [P, C])
            x3s = sb(ph, "x3s", [P, KC, P])
            rt = sb(ph, "rt", [P, 8])
            es = sb(ph, "es", [P, E])
            ps = sb(ph, "ps", [P, E])
            rank = sb(ph, "rank", [P, 2, E, E])
            rk = sb(ph, "rk", [P, 2, E])
            cw = sb(ph, "cw", [P, E])
            cr = sb(ph, "cr", [P, 2, E])
            c3 = sb(ph, "c3", [P, 3 * E], BF16)
            s_ld = sem("chain_loaded")
            s_step, s_pre = sem("chain_dve"), sem("chain_pre")
            LINKS = 39
            blk = ph.enter_context(nc.Block())

            @blk.sync
            def _(sp):
                sp.dma_start(xb[:, :, :], x.rearrange("(t p) c -> p t c", p=P)).then_inc(s_ld, 16)
                for dst, src in ((bo, bo_b), (bv, bv_b), (gnw, gnw_b), (gnb, gnb_b)):
                    sp.dma_start(dst[:, :], src).then_inc(s_ld, 16)
                for dst, src in ((wr, w_qkvg), (wor, w_o), (gw, gate_t)):
                    sp.dma_start(dst[:, :, :], src.rearrange("(k p) n -> p k n", p=P)).then_inc(s_ld, 16)
                for dst, src in ((cost, cos_t), (sint, sin_t), (dec, decay), (lower, tri)):
                    sp.dma_start(dst[:, :, :], src).then_inc(s_ld, 16)

            @blk.gpsimd
            def _(pool):
                def root(name, t, dst, src, eps):
                    need(pool, name, t)
                    hold(pool)
                    pool.tensor_scalar(src, src, eps, None, ALU.add).then_inc(ev(name + "_eps"), 1)
                    need(pool, name + "_eps", t)
                    pool.tensor_tensor(dst, src, half_exp[:, 0:dst.shape[1]], ALU.pow).then_inc(ev(name + "_root"), 1)

                with pool.Fori(0, TILES) as t:
                    root("ln2", t, rstd[:, 0:1], mv[:, 1:2], LN_EPS)
                    need(pool, "rq_ready", t)
                    hold(pool)
                    for m in range(KC):
                        for s in range(2):
                            q = rqt[:, m, s * N:(s + 1) * N].unsqueeze(1).to_broadcast([P, HH, N])
                            tt = pool.tensor_tensor(rqb[:, m, s], q, half[:, :].unsqueeze(2).to_broadcast([P, HH, N]),
                                                    ALU.mult)
                    tt.then_inc(ev("rqb_ready"), 1)
                    root("gn", t, gst[:, 2, :], gst[:, 1, :], GN_EPS)
                    root("ln3", t, rstd[:, 1:2], mv[:, 1:2], LN_EPS)

            @blk.vector
            def _(dve):
                pre = [0]

                def link(ins):
                    pre[0] += 1
                    ins.then_inc(s_pre, 1)
                    dve.wait_ge(s_pre, pre[0])

                dve.wait_ge(s_ld, 16 * 12)
                link(dve.tensor_tensor(xb[:, :, :], xb[:, :, :], bo[:, :].unsqueeze(1).to_broadcast([P, TILES, C]), ALU.add))
                link(dve.memset(comb[32:3 * E + 1, :], 1.0))
                with dve.Fori(0, TILES) as t:
                    n = [0]

                    def step(ins):
                        n[0] += 1
                        ins.then_inc(s_step, 1)
                        dve.wait_ge(s_step, LINKS * t + n[0])

                    def heads(ap):
                        return ap.rearrange("p (h d) -> p h d", d=D)

                    def by_head(ap):
                        return ap.unsqueeze(2).to_broadcast([P, H, D])

                    step(dve.tensor_tensor(oc[:, :], o_all[:, t, :], bv[:, :], ALU.add))
                    step(dve.tensor_reduce(sc[:, 0:1], oc[:, :], AX.X, ALU.max, apply_absolute_value=True))
                    step(dve.tensor_scalar(sc[:, 1:2], sc[:, 0:1], 1.0 / 127.0, Q_EPS, ALU.mult, ALU.max))
                    step(dve.reciprocal(sc[:, 2:3], sc[:, 1:2]))
                    step(dve.tensor_scalar(oc[:, :], oc[:, :], sc[:, 2:3], 127.0, ALU.mult, ALU.min))
                    step(dve.tensor_scalar(oq[:, :], oc[:, :], -127.0, ROUND, ALU.max, ALU.add))
                    dve.tensor_scalar(oi[:, :], oq[:, :], -ROUND, None, ALU.add).then_inc(ev("oi_ready"), 1)
                    need(dve, "y_done", t)
                    hold(dve)
                    step(dve.scalar_tensor_tensor(oq[:, :], bank_c[:, 0:C], sc[:, 1:2], swo_b[:, :], ALU.mult, ALU.mult))
                    step(dve.tensor_tensor(x1[:, :], oq[:, :], xb[:, t, :], ALU.add))

                    def norm(src, name, root):
                        step(dve.bn_stats(stats[:, :], src))
                        hold(dve)
                        dve.bn_aggr(mv[:, :], stats[:, :]).then_inc(ev(name), 1)
                        need(dve, name + "_root", t)
                        hold(dve)
                        return dve.tensor_scalar(xn[:, :], src, mv[:, 0:1], root, ALU.subtract, ALU.mult)

                    norm(x1[:, :], "ln2", rstd[:, 0:1]).then_inc(ev("xn2_ready"), 1)
                    need(dve, "qk_done", t)
                    hold(dve)
                    qk = bank_c[:, :].rearrange("p (a h d) -> p a h d", a=2, d=D)
                    ra4 = ra[:, :, :].rearrange("p (a h) d -> p a h d", a=2)
                    rb4 = rb[:, :, :].rearrange("p (a h) d -> p a h d", a=2)
                    dve.tensor_tensor(ra4, qk, cost[:, :, :].unsqueeze(2).to_broadcast([P, 2, H, D]), ALU.mult)\
                       .then_inc(ev("rope_cos"), 1)
                    for z in range(2):
                        zs, zo = slice(8 * z, 8 * z + 8), slice(8 - 8 * z, 16 - 8 * z)
                        step(dve.tensor_tensor(rb4[:, :, :, zs], qk[:, :, :, zo],
                                               sint[:, :, zs].unsqueeze(2).to_broadcast([P, 2, H, D // 2]), ALU.mult))
                    need(dve, "rope_cos", t)
                    dve.tensor_tensor(ra[:, :, :], ra[:, :, :], rb[:, :, :], ALU.add).then_inc(ev("qk_rot"), 1)
                    for m in range(KC):
                        need(dve, f"ret_done{m}", t)
                        dve.tensor_tensor(ret[:, m, :], bank_c[:, :], dec[:, m * HH:(m + 1) * HH, :].rearrange("p h n -> p (h n)"),
                                          ALU.mult).then_inc(ev(f"ret_ready{m}"), 1)
                    need(dve, "yr_done", t)
                    y = heads(bank_c[:, 0:C])
                    step(dve.tensor_reduce(gst[:, 0, :], y, AX.X, ALU.add))
                    step(dve.tensor_scalar(gst[:, 0, :], gst[:, 0, :], 1.0 / D, None, ALU.mult))
                    step(dve.tensor_tensor(yc[:, :, :], y, by_head(gst[:, 0, :]), ALU.subtract))
                    step(dve.tensor_tensor(ysq[:, :, :], yc[:, :, :], yc[:, :, :], ALU.mult))
                    step(dve.tensor_reduce(gst[:, 3, :], ysq[:, :, :], AX.X, ALU.add))
                    dve.tensor_scalar(gst[:, 1, :], gst[:, 3, :], 1.0 / D, None, ALU.mult).then_inc(ev("gn"), 1)
                    need(dve, "gn_root", t)
                    step(dve.tensor_tensor(yc[:, :, :], yc[:, :, :], by_head(gst[:, 2, :]), ALU.mult))
                    ycf = yc[:, :, :].rearrange("p h d -> p (h d)")
                    step(dve.tensor_tensor(ycf, ycf, gnw[:, :], ALU.mult))
                    step(dve.tensor_tensor(ycf, ycf, gnb[:, :], ALU.add))
                    need(dve, "gate_ready", t)
                    dve.tensor_tensor(ycf, ycf, gs[:, :], ALU.mult).then_inc(ev("h_ready"), 1)
                    need(dve, "wo_done", t)
                    step(dve.tensor_tensor(x2[:, :], x1[:, :], bank_c[:, 0:C], ALU.add))
                    step(dve.tensor_scalar(o_all[:, t, :], x2[:, :], 1.0, None, ALU.mult))
                    norm(x2[:, :], "ln3", rstd[:, 1:2]).then_inc(ev("xn3_ready"), 1)
                    need(dve, "logits_done", t)
                    dve.tensor_reduce(rt[:, 0:1], bank_c[:, 0:E], AX.X, ALU.max, negate=True).then_inc(ev("rt_max"), 1)
                    need(dve, "rt_exp", t)
                    step(dve.reciprocal(rt[:, 2:3], rt[:, 1:2]))
                    step(dve.tensor_scalar(ps[:, :], es[:, :], rt[:, 2:3], None, ALU.mult))
                    by_f = ps[:, :].unsqueeze(1).to_broadcast([P, E, E])
                    by_e = ps[:, :].unsqueeze(2).to_broadcast([P, E, E])
                    step(dve.tensor_tensor(rank[:, 0], by_f, by_e, ALU.is_gt))
                    step(dve.tensor_tensor(rank[:, 1], by_f, by_e, ALU.is_equal))
                    step(dve.tensor_tensor(rank[:, 1], rank[:, 1], lower[:, :, :], ALU.mult))
                    step(dve.tensor_reduce(rk[:, :, :], rank[:, :, :, :], AX.X, ALU.add))
                    step(dve.tensor_tensor(cw[:, :], rk[:, 0], rk[:, 1], ALU.add))
                    step(dve.tensor_scalar(cw[:, :], cw[:, :], TOPK - 0.5, None, ALU.is_lt))
                    step(dve.tensor_tensor(cw[:, :], cw[:, :], ps[:, :], ALU.mult))
                    step(dve.tensor_reduce(rt[:, 3:4], cw[:, :], AX.X, ALU.add))
                    step(dve.reciprocal(rt[:, 4:5], rt[:, 3:4]))
                    step(dve.tensor_scalar(cw[:, :], cw[:, :], rt[:, 4:5], None, ALU.mult))
                    step(dve.tensor_copy(c3[:, 0:E], cw[:, :]))
                    step(dve.tensor_tensor(cr[:, 0], cw[:, :], c3[:, 0:E], ALU.subtract))
                    step(dve.tensor_copy(c3[:, E:2 * E], cr[:, 0]))
                    step(dve.tensor_tensor(cr[:, 1], cr[:, 0], c3[:, E:2 * E], ALU.subtract))
                    dve.tensor_copy(c3[:, 2 * E:3 * E], cr[:, 1]).then_inc(ev("c3_ready"), 1)
                    need(dve, "c3_turned", t)
                    hold(dve)
                    step(dve.tensor_copy(comb[0:3 * E, bass.ds(t * P, P)], bank_c[:, :].bitcast(BF16)[0:3 * E, 0:P]))
                    assert n[0] == LINKS, n[0]

            @blk.scalar
            def _(act):
                def out_of(name, t, dst, src, func, done):
                    need(act, name, t)
                    act.activation(dst, src, func).then_inc(ev(done), 1)

                with act.Fori(0, TILES) as t:
                    flat = lambda a: a[:, :, :].rearrange("p k n -> p (k n)")
                    out_of("oi_turned", t, flat(oqt), bank_c[:, :].bitcast(BF16)[:, 0:C], ACT.Copy, "oqt_ready")
                    out_of("xn2_turned", t, flat(xnt), bank_c[:, 0:C], ACT.Copy, "xnt_ready")
                    need(act, "qk_turned", t)
                    act.activation(flat(rqt), bank_c[:, 0:C], ACT.Copy).then_inc(ev("rq_ready"), 1)
                    act.activation(flat(rkt), bank_c[:, C:2 * C], ACT.Copy).then_inc(ev("rk_ready"), 1)
                    need(act, "vg_done", t)
                    act.activation(rv[:, :], bank_c[:, 0:C], ACT.Copy).then_inc(ev("rv_ready"), 1)
                    act.activation(gs[:, :], bank_c[:, C:2 * C], ACT.Silu).then_inc(ev("gate_ready"), 1)
                    out_of("h_turned", t, flat(ht), bank_c[:, 0:C], ACT.Copy, "ht_ready")
                    need(act, "xn3_turned", t)
                    act.activation(x3t[:, :, bass.ds(t * P, P)], bank_c[:, 0:C].rearrange("p (k n) -> p k n", k=KC),
                                   ACT.Copy).then_inc(ev("x3t_ready"), 1)
                    act.activation(flat(x3s), bank_c[:, 0:C], ACT.Copy).then_inc(ev("x3s_ready"), 1)
                    need(act, "rt_max", t)
                    act.activation(es[:, :], bank_c[:, 0:E], ACT.Exp, bias=rt[:, 0:1],
                                   accum_out=rt[:, 1:2]).then_inc(ev("rt_exp"), 1)

            @blk.tensor
            def _(pe):
                def turn(src, ident, bank, done):
                    for k in range(KC):
                        mm = pe.transpose(bank[:, k * P:(k + 1) * P], src[:, k * P:(k + 1) * P], ident)
                    mm.then_inc(ev(done), 1)

                def project(dst, lhs, rhs, done):
                    for k in range(KC):
                        mm = pe.matmul(dst, lhs[:, k, :], rhs(k), start=(k == 0), stop=(k == KC - 1))
                    mm.then_inc(ev(done), 1)

                with pe.Fori(0, TILES) as t:
                    need(pe, "oi_ready", t)
                    turn(oi, ident_b[:, :], bank_c[:, :].bitcast(BF16), "oi_turned")
                    need(pe, "oqt_ready", t)
                    project(bank_c[:, 0:C], oqt, lambda k: wo_qt[:, k, :], "y_done")
                    need(pe, "xn2_ready", t)
                    turn(xn, ident_f[:, :], bank_c, "xn2_turned")
                    need(pe, "xnt_ready", t)
                    project(bank_c[:, :], xnt, lambda k: wr[:, k, 0:2 * C], "qk_done")
                    need(pe, "qk_rot", t)
                    for k in range(2 * KC):
                        mm = pe.transpose(bank_c[:, k * P:(k + 1) * P],
                                          ra[:, :, :].rearrange("p h d -> p (h d)")[:, k * P:(k + 1) * P], ident_f[:, :])
                    mm.then_inc(ev("qk_turned"), 1)
                    need(pe, "rk_ready", t)
                    project(bank_c[:, :], xnt, lambda k: wr[:, k, 2 * C:4 * C], "vg_done")
                    need(pe, "gate_ready", t)
                    need(pe, "rqb_ready", t)
                    for m in range(KC):
                        if m:
                            need(pe, f"ret_ready{m - 1}", t)
                        for s in range(2):
                            mm = pe.matmul(bank_c[s * N:(s + 1) * N, :], rkt[:, m, s * N:(s + 1) * N],
                                           rqb[:, m, s].rearrange("p h n -> p (h n)"), start=True, stop=True)
                        mm.then_inc(ev(f"ret_done{m}"), 1)
                    need(pe, f"ret_ready{KC - 1}", t)
                    hold(pe)
                    for s in range(2):
                        for h in range(H):
                            mm = pe.matmul(bank_c[s * N:(s + 1) * N, h * D:(h + 1) * D],
                                           ret[s * N:(s + 1) * N, h // HH, (h % HH) * N:(h % HH + 1) * N],
                                           rv[s * N:(s + 1) * N, h * D:(h + 1) * D], start=True, stop=True)
                    mm.then_inc(ev("yr_done"), 1)
                    need(pe, "h_ready", t)
                    turn(yc[:, :, :].rearrange("p h d -> p (h d)"), ident_f[:, :], bank_c, "h_turned")
                    need(pe, "ht_ready", t)
                    project(bank_c[:, 0:C], ht, lambda k: wor[:, k, :], "wo_done")
                    need(pe, "xn3_ready", t)
                    turn(xn, ident_f[:, :], bank_c, "xn3_turned")
                    need(pe, "x3s_ready", t)
                    project(bank_c[:, 0:E], x3s, lambda k: gw[:, k, :], "logits_done")
                    need(pe, "c3_ready", t)
                    hold(pe)
                    pe.transpose(bank_c[:, :].bitcast(BF16)[0:3 * E, 0:P], c3[:, :], ident_b[:, :]).then_inc(ev("c3_turned"), 1)

        with ExitStack() as ph:
            wgu = [sb(ph, f"wgu{n}", [P, 2, KC, P]) for n in range(2)]
            wdn = [sb(ph, f"wdn{n}", [P, C]) for n in range(2)]
            wex = [sb(ph, f"wex{n}", [3 * E + 1, P], BF16) for n in range(2)]
            sg = [sb(ph, f"silu{n}", [P, 512]) for n in range(2)]
            su = [sb(ph, f"gated{n}", [P, 512]) for n in range(2)]
            aw = [sb(ph, f"acts{n}", [P, 512]) for n in range(2)]
            yout = sb(ph, "yout", [P, TILES, C])
            bank_y = [bank_s[0], bank_s[1], bank_s[2], bank_o]
            bank_g, bank_u, bank_w = bank_t[0], bank_t[1], bank_x
            s_wl = [sem(f"expert_w{n}") for n in range(2)]
            s_gd, s_ud, s_cd = sem("gate_mm"), sem("up_mm"), sem("weight_mm")
            s_sg, s_su, s_aw = sem("silu_done"), sem("gated_done"), sem("acts_done")
            s_dn, s_yo, s_out = sem("down_done"), sem("y_added"), sem("out_stored")
            NB = TILES * P // 512
            blk = ph.enter_context(nc.Block())

            def tiles_loop(e, body):
                body(0, 0, 0)
                body(1, 1, 0)
                body(2, 0, 1)
                with e.Fori(1, (JT - 1) // 2) as r:
                    body(2 * r + 1, 1, r)
                    body(2 * r + 2, 0, r + 1)

            @blk.sync
            def _(sp):
                def body(j, b, r):
                    if not (isinstance(j, int) and j < 2):
                        sp.wait_ge(s_dn, NB * (j - 1))
                    sp.dma_start(wgu[b][:, :, :, :], w_gu[j]).then_inc(s_wl[b], 16)
                    sp.dma_start(wdn[b][:, :], w_dn[j]).then_inc(s_wl[b], 16)
                    sp.dma_start(wex[b][:, :], expand[j].bitcast(BF16)).then_inc(s_wl[b], 16)

                tiles_loop(sp, body)
                for q in range(2):
                    sp.wait_ge(s_yo, 2 * (q + 1))
                    sp.dma_start(out.rearrange("(t p) c -> p t c", p=P)[:, 4 * q:4 * q + 4, :],
                                 yout[:, 4 * q:4 * q + 4, :]).then_inc(s_out, 16)
                sp.wait_ge(s_out, 32)

            @blk.tensor
            def _(pe):
                def down(jn, b, n, first, last):
                    pe.wait_ge(s_aw, jn + 1)
                    for q in range(4):
                        tt = 4 * n + q
                        mm = pe.matmul(bank_y[tt // 2][:, (tt % 2) * C:(tt % 2 + 1) * C], aw[n][:, q * P:(q + 1) * P],
                                       wdn[b][:, :], start=(first and tt % 2 == 0), stop=last, skip_group_check=True)
                    mm.then_inc(s_dn, 1)

                def body(j, b, r):
                    first = isinstance(j, int) and j == 0
                    pe.wait_ge(s_wl[b], 48 * (r + 1))
                    for n in range(NB):
                        jn = NB * j + n
                        cols = slice(n * 512, (n + 1) * 512)
                        for g, (bank, free, done) in enumerate(((bank_g, s_sg, s_gd), (bank_u, s_su, s_ud))):
                            if not (first and n == 0):
                                pe.wait_ge(free, jn)
                            for k in range(KC):
                                mm = pe.matmul(bank[:, :], wgu[b][:, g, k, :], x3t[:, k, cols], start=(k == 0), stop=(k == KC - 1))
                            mm.then_inc(done, 1)
                        if not (first and n == 0):
                            pe.wait_ge(s_aw, jn)
                        pe.matmul(bank_w[:, :], wex[b][:, :], comb[:, cols], start=True, stop=True).then_inc(s_cd, 1)
                        down(jn, b, n, first, False)

                tiles_loop(pe, body)

            @blk.scalar
            def _(act):
                def body(j, b, r):
                    for n in range(NB):
                        act.wait_ge(s_gd, NB * j + n + 1)
                        if not (isinstance(j, int) and j == 0):
                            act.wait_ge(s_su, NB * j + n - 1)
                        act.activation(sg[n][:, :], bank_g[:, :], ACT.Silu).then_inc(s_sg, 1)

                tiles_loop(act, body)

            @blk.vector
            def _(dve):
                def body(j, b, r):
                    for n in range(NB):
                        jn = NB * j + n
                        dve.wait_ge(s_sg, jn + 1)
                        dve.wait_ge(s_ud, jn + 1)
                        dve.tensor_tensor(su[n][:, :], sg[n][:, :], bank_u[:, :], ALU.mult).then_inc(s_su, 1)
                        dve.wait_ge(s_su, jn + 1)
                        dve.wait_ge(s_cd, jn + 1)
                        if not (isinstance(j, int) and j == 0):
                            dve.wait_ge(s_dn, jn - 1)
                        dve.tensor_tensor(aw[n][:, :], su[n][:, :], bank_w[:, :], ALU.mult).then_inc(s_aw, 1)

                tiles_loop(dve, body)
                dve.wait_ge(s_dn, NB * JT)
                for q in range(4):
                    dve.tensor_tensor(yout[:, 2 * q:2 * q + 2, :].rearrange("p t c -> p (t c)"),
                                      o_all[:, 2 * q:2 * q + 2, :].rearrange("p t c -> p (t c)"), bank_y[q][:, :],
                                      ALU.add).then_inc(s_yo, 1)


def shape_tables():
    import numpy as np

    p = np.arange(P)
    f = np.float32
    ident = np.eye(P, dtype=f)
    half = (p[:, None] // D == np.arange(HH)[None]).astype(f)
    group = (p[:, None] // D % 4 == np.arange(4)[None]).astype(f)
    pos = (p % N).astype(f)
    hd = D // 2
    xscale = (np.arange(0, D, 2, dtype=f) + f(0.4 * D)) / f(1.4 * D)
    scale = xscale[None, :] ** (pos[:, None] / f(64))
    inv_freq = f(1.0) / f(10000.0) ** (np.arange(hd, dtype=f) / f(hd))
    sinu = pos[:, None] * inv_freq[None, :]
    cos_t = np.zeros((P, 2, D), f)
    sin_t = np.zeros((P, 2, D), f)
    for a, sc in enumerate((scale, f(1.0) / scale)):
        cos_t[:, a, :hd] = cos_t[:, a, hd:] = np.cos(sinu) * sc
        sin_t[:, a, :hd] = -np.sin(sinu) * sc
        sin_t[:, a, hd:] = np.sin(sinu) * sc
    gammas = 1.0 - np.exp(np.linspace(np.log(1.0 / 32), np.log(1.0 / 64), H)).astype(f)
    gammas = gammas.astype(f)
    m = (p % N)[:, None, None]
    n = np.arange(N)[None, None, :]
    decay = np.where(n >= m, gammas[None, :, None] ** np.maximum(n - m, 0).astype(f), 0.0).astype(f)
    tri = np.broadcast_to((np.arange(E)[None, :] < np.arange(E)[:, None]).astype(f), (P, E, E))
    rows = np.arange(JT * P)
    expand = np.zeros((3 * E + 1, JT * P), f)
    for part in range(3):
        for e in range(E):
            expand[part * E + e] = rows // I == e
    expand[3 * E] = rows >= E * I
    expand = expand.reshape(3 * E + 1, JT, P).transpose(1, 0, 2).astype(np.uint16) * np.uint16(0x3F80)
    return dict(ident=ident, half_sel=half, group_sel=group, cos_t=cos_t, sin_t=sin_t, decay=decay,
                tri=np.ascontiguousarray(tri), expand=expand)


def kernel(**inputs):
    import numpy as np
    import concourse.bacc as bacc
    from concourse import mybir as _mybir
    from concourse.bass_utils import run_bass_kernel_spmd as run

    g = {k: np.asarray(v) for k, v in inputs.items()}
    row = lambda a: np.ascontiguousarray(np.broadcast_to(a[None, :], (P, a.shape[0])))

    def heads(w, evens_first):
        w = w.transpose(1, 0, 2)
        if evens_first:
            w = np.concatenate([w[..., 0::2], w[..., 1::2]], -1)
        return w.reshape(C, H * D)

    def hidden(w):
        w = np.concatenate([w, np.zeros((C, JT * P - w.shape[1]), w.dtype)], 1)
        return w.reshape(KC, P, JT, P).transpose(2, 1, 0, 3)

    w_g = hidden(np.concatenate([g["L0_ffn_w_gate"].transpose(1, 0, 2).reshape(C, E * I), g["L0_ffn_sw_gate"]], 1))
    w_u = hidden(np.concatenate([g["L0_ffn_w_up"].transpose(1, 0, 2).reshape(C, E * I), g["L0_ffn_sw_up"]], 1))
    w_d = np.concatenate([g["L0_ffn_w_down"].reshape(E * I, C), g["L0_ffn_sw_down"]], 0)
    w_d = np.concatenate([w_d, np.zeros((JT * P - w_d.shape[0], C), w_d.dtype)], 0).reshape(JT, P, C)
    arrays = dict(
        x=g["x"].reshape(B * N, C), ctx_t=g["ctx_2048"].transpose(0, 2, 1), mask=g["mask_BxSxS2_ff0"],
        wq=g["L0_xattn_wq"], wk_t=g["L0_xattn_wk"].T, wv_t=g["L0_xattn_wv"].T, wo=g["L0_xattn_wo"],
        bq=g["L0_xattn_bq"].reshape(KC, P).T, bo_b=row(g["L0_xattn_bo"]), bv_b=row(g["L0_xattn_bv"]),
        w_qkvg=np.concatenate([heads(g["L0_attn_W_Q"], True), heads(g["L0_attn_W_K"], True),
                               heads(g["L0_attn_W_V"], False), g["L0_attn_W_G"]], 1),
        w_o=g["L0_attn_W_O"], gnw_b=row(g["L0_attn_gn_weight"]), gnb_b=row(g["L0_attn_gn_bias"]),
        gate_t=g["L0_ffn_gate_w"].T, w_gu=np.stack([w_g, w_u], 2), w_dn=w_d,
        bk=g["L0_xattn_bk"].reshape(KC, P).T, **shape_tables())
    arrays = {f"in_{k}": np.ascontiguousarray(v) for k, v in arrays.items()}
    nc = bacc.Bacc("TRN2", target_bir_lowering=False, num_devices=1)
    args = {k[3:]: nc.dram_tensor(k, a.shape, _mybir.dt.from_np(a.dtype), kind="ExternalInput").ap()
            for k, a in arrays.items()}
    out = nc.dram_tensor("out_0", (B * N, C), _mybir.dt.float32, kind="ExternalOutput").ap()
    perceiver_program(nc, out=out, **args)
    r = run(nc, [arrays], core_ids=[0])
    return r.results[0]["out_0"].reshape(B, N, C)
```

```python
from contextlib import ExitStack

import concourse.bass as bass
from concourse import mybir
from concourse.alu_op_type import AluOpType as ALU

F32 = mybir.dt.float32
BF16 = mybir.dt.bfloat16
F32R = mybir.dt.float32r
ACT = mybir.ActivationFunctionType
AX = mybir.AxisListType

P = 128
B, N, C = 16, 64, 256
L = 1601
H, D = 16, 16
KC = C // P
HH = H // KC
TILES = B * N // P
PAIRS = H // 2
UNITS = 2 * PAIRS
LT = -(-L // P)
LAST = L - (LT - 1) * P
NC4 = 4
CH = [384, 384, 384, 449]
CM = [384, 384, 384, 450]
LM = L + L % 2
CO = [0, 384, 768, 1152]
G4 = 64
NG = H * D // G4
E, I, TOPK = 16, 176, 4
IS = 2 * I
MT = E * I // P
ST = -(-IS // P)
JT = MT + ST
LANES = 4
ROUND = 12582912.0
BIG = 3.0e38
LN_EPS, Q_EPS, GN_EPS = 1e-5, 1e-8, 1e-5


def perceiver_program(nc, x, ctx_t, mask, wq, wk_t, wv_t, wo, bq, bo_b, bv_b, w_qkvg, w_o, gnw_b, gnb_b,
                      gate_t, w_gu, w_dn, ident, half_sel, group_sel, fold_sel, cos_t, sin_t, decay, tri, expand, bk, out):
    with ExitStack() as ctx:
        def sem(name):
            return ctx.enter_context(nc.semaphore(name))

        def sb(stack, name, shape, dt=F32):
            return stack.enter_context(nc.sbuf_tensor(name, shape, dt))

        events = {}

        def ev(name):
            if name not in events:
                events[name] = sem(name)
            return events[name]

        def need(e, name, t):
            e.wait_ge(ev(name), t + 1)

        def hold(e):
            e.nop(nofuse=True)

        bank_s = [ctx.enter_context(nc.psum_tensor(f"scores{n}", [P, 512], F32)) for n in range(3)]
        bank_t = [ctx.enter_context(nc.psum_tensor(f"turned{n}", [P, 512], F32)) for n in range(2)]
        bank_x = ctx.enter_context(nc.psum_tensor("kv_proj", [P, 512], F32))
        bank_c = ctx.enter_context(nc.psum_tensor("chain", [P, 512], F32))
        bank_o = ctx.enter_context(nc.psum_tensor("attn_out", [P, 512], F32))

        ident_f = sb(ctx, "ident_f", [P, P])
        ident_b = sb(ctx, "ident_b", [P, P], BF16)
        o_all = sb(ctx, "o_all", [P, TILES, C])
        qt_all = sb(ctx, "qt_all", [P, NG, TILES * P])
        wo_qt = sb(ctx, "wo_qt", [P, KC, C], BF16)
        swo_b = sb(ctx, "swo_b", [P, C])
        half = sb(ctx, "half", [P, HH])
        fold = sb(ctx, "fold", [P, G4])
        group = sb(ctx, "group", [P, 4])
        half_exp = sb(ctx, "power", [P, H])

        with ExitStack() as ph:
            xs = sb(ph, "xs", [P, TILES, C])
            w_in = sb(ph, "w_in", [P, 2, KC, C])
            w_q = sb(ph, "w_quant", [P, 2, KC, C])
            w_i = sb(ph, "w_int", [P, 2, KC, C], BF16)
            w_amax = sb(ph, "w_amax", [P, 2 * KC])
            w_s = sb(ph, "w_scale", [P, 2 * KC])
            w_r = sb(ph, "w_rscale", [P, 2 * KC])
            wq_qt = sb(ph, "wq_qt", [P, KC, C], BF16)
            diag = sb(ph, "diag", [P, KC, P])
            ones = sb(ph, "ones", [P, P])
            bq_s = sb(ph, "bq_s", [P, NG])
            bq4 = sb(ph, "bq4", [P, NG])
            swq4 = sb(ph, "swq4", [P, KC, 2])
            stats = sb(ph, "q_stats", [P, 6])
            mv = sb(ph, "q_mv", [P, 2])
            rstd = sb(ph, "q_rstd", [P, 2])
            xn = sb(ph, "q_xn", [P, C])
            sc = sb(ph, "q_sc", [P, 4])
            xq = sb(ph, "q_xq", [P, C])
            xi = sb(ph, "q_xi", [P, C], BF16)
            xit = sb(ph, "q_xit", [P, KC, P], BF16)
            qtok = sb(ph, "q_tok", [P, NG, 2, G4])
            s_in, s_w, s_wdve = sem("in_loaded"), sem("w_in_loaded"), sem("w_dve")
            s_link = sem("q_dve")
            blk = ph.enter_context(nc.Block())

            @blk.sync
            def _(sp):
                sp.dma_start(w_in[:, 0], wq.rearrange("(a p) c -> p a c", p=P)).then_inc(s_w, 16)
                sp.dma_start(w_in[:, 1], wo.rearrange("(a p) c -> p a c", p=P)).then_inc(s_w, 16)
                sp.dma_start(ident_f[:, :], ident).then_inc(s_w, 16)
                sp.dma_start(bq_s[:, :], bq).then_inc(s_w, 16)
                sp.dma_start(xs[:, :, :], x.rearrange("(t p) c -> p t c", p=P)).then_inc(s_in, 16)
                sp.dma_start(half[:, :], half_sel).then_inc(s_in, 16)
                sp.dma_start(group[:, :], group_sel).then_inc(s_in, 16)
                sp.dma_start(fold[:, :], fold_sel).then_inc(s_in, 16)

            @blk.gpsimd
            def _(pool):
                pool.memset(half_exp[:, :], -0.5).then_inc(ev("consts_set"), 1)
                pool.memset(ones[:, :], 1.0).then_inc(ev("consts_set"), 1)
                pool.wait_ge(ev("consts_set"), 2)
                with pool.Fori(0, TILES) as t:
                    need(pool, "q_mv_ready", t)
                    hold(pool)
                    pool.tensor_scalar(rstd[:, 0:1], mv[:, 1:2], LN_EPS, None, ALU.add).then_inc(ev("q_veps"), 1)
                    need(pool, "q_veps", t)
                    pool.tensor_tensor(rstd[:, 1:2], rstd[:, 0:1], half_exp[:, 0:1], ALU.pow).then_inc(ev("q_rstd_ready"), 1)

            @blk.vector
            def _(dve):
                done = [0]

                def link(ins):
                    done[0] += 1
                    ins.then_inc(s_wdve, 1)
                    dve.wait_ge(s_wdve, done[0])

                dve.wait_ge(s_w, 64)
                link(dve.tensor_copy(ident_b[:, :], ident_f[:, :]))
                link(dve.tensor_reduce(w_amax[:, :], w_in[:, :, :, :].rearrange("p m a c -> p (m a) c"), AX.X, ALU.max,
                                       apply_absolute_value=True))
                link(dve.tensor_scalar(w_s[:, :], w_amax[:, :], 1.0 / 127.0, Q_EPS, ALU.mult, ALU.max))
                link(dve.reciprocal(w_r[:, :], w_s[:, :]))
                for m in range(2):
                    for a in range(KC):
                        link(dve.tensor_scalar(w_q[:, m, a], w_in[:, m, a], w_r[:, KC * m + a:KC * m + a + 1], 127.0,
                                               ALU.mult, ALU.min))
                link(dve.tensor_scalar(w_q[:, :, :, :], w_q[:, :, :, :], -127.0, ROUND, ALU.max, ALU.add))
                dve.tensor_scalar(w_i[:, :, :, :], w_q[:, :, :, :], -ROUND, None, ALU.add).then_inc(ev("w_int_ready"), 1)
                for a in range(KC):
                    link(dve.tensor_scalar(diag[:, a], ident_f[:, :], w_s[:, KC + a:KC + a + 1], None, ALU.mult))
                for d in range(2):
                    for r in range(2):
                        link(dve.tensor_scalar(swq4[d * G4:(d + 1) * G4, :, r], w_s[r * G4:(r + 1) * G4, 0:KC],
                                               float(D) ** -0.5, None, ALU.mult))
                dve.tensor_scalar(bq4[:, :], bq_s[:, :], float(D) ** -0.5, None, ALU.mult).then_inc(ev("diag_ready"), 1)
                for m, dst in enumerate((wq_qt, wo_qt)):
                    dve.wait_ge(ev("w_turned"), m + 1)
                    dve.tensor_copy(dst[:, :, :].rearrange("p k o -> p (k o)"),
                                    bank_t[m][:, :].bitcast(BF16)[:, 0:KC * C]).then_inc(ev("w_copied"), 1)
                dve.wait_ge(ev("swo_rows"), 1)
                dve.tensor_copy(swo_b[:, :], bank_x[:, 0:C]).then_inc(ev("w_copied"), 1)

                dve.wait_ge(s_in, 64)
                with dve.Fori(0, TILES) as t:
                    n = [0]
                    links = 7 + NG

                    def step(ins):
                        n[0] += 1
                        ins.then_inc(s_link, 1)
                        dve.wait_ge(s_link, t * links + n[0])

                    step(dve.bn_stats(stats[:, :], xs[:, t, :]))
                    hold(dve)
                    dve.bn_aggr(mv[:, :], stats[:, :]).then_inc(ev("q_mv_ready"), 1)
                    need(dve, "q_rstd_ready", t)
                    hold(dve)
                    step(dve.tensor_scalar(xn[:, :], xs[:, t, :], mv[:, 0:1], rstd[:, 1:2], ALU.subtract, ALU.mult))
                    step(dve.tensor_reduce(sc[:, 0:1], xn[:, :], AX.X, ALU.max, apply_absolute_value=True))
                    step(dve.tensor_scalar(sc[:, 1:2], sc[:, 0:1], 1.0 / 127.0, Q_EPS, ALU.mult, ALU.max))
                    step(dve.reciprocal(sc[:, 2:3], sc[:, 1:2]))
                    step(dve.tensor_scalar(xn[:, :], xn[:, :], sc[:, 2:3], 127.0, ALU.mult, ALU.min))
                    step(dve.tensor_scalar(xq[:, :], xn[:, :], -127.0, ROUND, ALU.max, ALU.add))
                    dve.tensor_scalar(xi[:, :], xq[:, :], -ROUND, None, ALU.add).then_inc(ev("q_int_ready"), 1)
                    need(dve, "q_proj_done", t)
                    dve.tensor_scalar(qtok[:, :, :, :], bank_c[:, 0:C].rearrange("p (j c) -> p j c", j=NG).unsqueeze(2)
                                      .to_broadcast([P, NG, 2, G4]), sc[:, 1:2], None, ALU.mult).then_inc(ev("q_tok_ready"), 1)
                    need(dve, "q_turned", t)
                    hold(dve)
                    for j in range(NG):
                        step(dve.tensor_scalar(qt_all[:, j, bass.ds(t * P, P)], bank_c[:, j * P:(j + 1) * P],
                                               swq4[:, j // 2, j % 2:j % 2 + 1], bq4[:, j:j + 1], ALU.mult, ALU.add))
                    assert n[0] == links

            @blk.scalar
            def _(act):
                with act.Fori(0, TILES) as t:
                    need(act, "q_int_turned", t)
                    act.activation(xit[:, :, :].rearrange("p k n -> p (k n)"), bank_c[:, :].bitcast(BF16)[:, 0:C],
                                   ACT.Copy).then_inc(ev("q_xit_ready"), 1)

            @blk.tensor
            def _(pe):
                pe.wait_ge(ev("w_int_ready"), 1)
                for m in range(2):
                    tb = bank_t[m][:, :].bitcast(BF16)
                    for k in range(KC):
                        for a in range(KC):
                            mm = pe.transpose(tb[:, k * C + a * P:k * C + a * P + P], w_i[:, m, a, k * P:(k + 1) * P], ident_b[:, :])
                    mm.then_inc(ev("w_turned"), 1)
                pe.wait_ge(ev("diag_ready"), 1)
                pe.wait_ge(ev("consts_set"), 2)
                pe.matmul(bank_x[:, 0:C], ones[:, :], diag[:, :, :].rearrange("p a o -> p (a o)"),
                          start=True, stop=True).then_inc(ev("swo_rows"), 1)
                pe.wait_ge(ev("w_copied"), 3)
                with pe.Fori(0, TILES) as t:
                    need(pe, "q_int_ready", t)
                    cb = bank_c[:, :].bitcast(BF16)
                    for k in range(KC):
                        mm = pe.transpose(cb[:, k * P:(k + 1) * P], xi[:, k * P:(k + 1) * P], ident_b[:, :])
                    mm.then_inc(ev("q_int_turned"), 1)
                    need(pe, "q_xit_ready", t)
                    for k in range(KC):
                        mm = pe.matmul(bank_c[:, 0:C], xit[:, k, :], wq_qt[:, k, :], start=(k == 0), stop=(k == KC - 1))
                    mm.then_inc(ev("q_proj_done"), 1)
                    need(pe, "q_tok_ready", t)
                    for j in range(NG):
                        mm = pe.transpose(bank_c[:, j * P:(j + 1) * P], qtok[:, j, :, :].rearrange("p r c -> p (r c)"),
                                          ident_f[:, :])
                    mm.then_inc(ev("q_turned"), 1)

        with ExitStack() as ph:
            raw = [sb(ph, f"ctx_raw{n}", [P, KC, CM[3]]) for n in range(2)]
            cx = [sb(ph, f"ctx_parts{c}", [P, 2, KC, CM[c]], F32R) for c in range(NC4)]
            mk = [sb(ph, f"mask{s}", [P, L]) for s in range(2)]
            kt = sb(ph, "keys", [P, NG, LM], F32R)
            vt = [sb(ph, f"values{s}", [P, LT, C]) for s in range(2)]
            qb = [sb(ph, f"queries{s}", [P, PAIRS, 2, 2, N], F32R) for s in range(2)]
            qm = sb(ph, "queries_masked", [P, PAIRS, 2, N])
            sm = [sb(ph, f"probs{s}", [P, L]) for s in range(2)]
            pt = [sb(ph, f"probs_t{n}", [P, LT, 2, P]) for n in range(2)]
            w_raw = sb(ph, "w_raw", [P, 2, KC, C])
            w_kv = sb(ph, "w_kv", [P, 2, 2, KC, C], F32R)
            bks = sb(ph, "bks", [P, KC])
            nmax = sb(ph, "neg_max_chunks", [P, 2, NC4])
            nmin = sb(ph, "neg_max", [P, 2])
            sums = [sb(ph, f"sums{s}", [P, PAIRS]) for s in range(2)]
            rsum = sb(ph, "rsum", [P, PAIRS])
            rtok = sb(ph, "rtok", [P, PAIRS, 2])
            ot4 = sb(ph, "ot4", [P, 2, 4, N])
            ot = sb(ph, "ot", [P, NG, P])
            s_wkv, s_wsp = sem("wkv_loaded"), sem("wkv_split")
            s_raw = [sem(f"ctx_loaded{n}") for n in range(2)]
            s_hi, s_split = sem("ctx_high"), sem("ctx_split")
            s_mk = [sem(f"mask_loaded{s}") for s in range(2)]
            s_k, s_v = sem("k_item_done"), sem("v_item_done")
            s_khi, s_klo, s_vo = sem("keys_high"), sem("keys_low"), sem("values_out")
            s_sc = sem("scores_done")
            s_ttr = sem("scores_masked")
            s_nm = sem("neg_max_ready")
            s_exp = sem("exp_done")
            s_t = sem("turned")
            s_ta, s_td = sem("turned_out_act"), sem("turned_out_dve")
            s_pv = sem("pv_done")
            s_of = sem("attn_out_read")
            s_qm, s_qh, s_qb = sem("queries_masked_done"), sem("queries_high"), sem("queries_set")
            s_rs = sem("sums_read")
            s_fin = sem("attn_dve")
            FINS = 9
            blk = ph.enter_context(nc.Block())
            LASTI = TILES - 1

            def k_item(v):
                return (v + 6) % 8

            def v_item(v):
                return None if v == 1 else (6 if v == 0 else v - 2)

            def start(i, u):
                return isinstance(i, int) and i == 0 and u <= 0

            @blk.sync
            def _(sp):
                sp.dma_start(w_raw[:, 0], wk_t.rearrange("(k p) o -> p k o", p=P)).then_inc(s_wkv, 16)
                sp.dma_start(w_raw[:, 1], wv_t.rearrange("(k p) o -> p k o", p=P)).then_inc(s_wkv, 16)
                sp.dma_start(bks[:, :], bk).then_inc(s_wkv, 16)

                def load(b, c):
                    if not (isinstance(b, int) and b == 0 and c < 2):
                        sp.wait_ge(s_split, 4 * b + c - 1)
                    sp.dma_start(raw[c % 2][:, :, 0:CM[c]],
                                 ctx_t[b].rearrange("(k p) l -> p k l", p=P)[:, :, CO[c]:CO[c] + CM[c]]).then_inc(s_raw[c % 2], 16)

                def load_mask(b, s):
                    for j in range(2):
                        sp.dma_start(mk[s][j * N:(j + 1) * N, :], mask[b]).then_inc(s_mk[s], 16)

                for c in range(NC4):
                    load(0, c)
                load_mask(0, 0)
                load_mask(1, 1)
                for c in range(NC4):
                    load(1, c)
                with sp.Fori(0, LASTI) as i:
                    for s in range(2):
                        for c in range(NC4):
                            load(2 * i + 2 + s, c)
                        sp.wait_ge(s_ttr, 4 * PAIRS * (2 * i + s + 1))
                        load_mask(2 * i + 2 + s, s)

            @blk.gpsimd
            def _(pool):
                def split(b, c):
                    n = 4 * b + c
                    pool.wait_ge(s_raw[c % 2], 16 * (2 * b + c // 2 + 1))
                    if not (isinstance(b, int) and b == 0):
                        pool.wait_ge(s_k, 8 * b - 3 + c)
                    hold(pool)
                    pool.tensor_copy(cx[c][:, 0], raw[c % 2][:, :, 0:CM[c]]).then_inc(s_hi, 1)
                    pool.wait_ge(s_hi, n + 1)
                    pool.tensor_tensor(cx[c][:, 1], raw[c % 2][:, :, 0:CM[c]], cx[c][:, 0].bitcast(F32),
                                       ALU.subtract).then_inc(s_split, 1)

                def spread(b, s):
                    if not (isinstance(b, int) and b < 2):
                        pool.wait_ge(s_sc, 4 * PAIRS * (b - 1))
                        hold(pool)
                    q = qt_all[:, :, bass.ds(b * N, N)].unsqueeze(2).to_broadcast([P, NG, 4, N])
                    pool.tensor_tensor(qm[:, :, :, :].rearrange("p (j a) h n -> p j (a h) n", j=NG), q,
                                       group[:, :].unsqueeze(1).unsqueeze(3).to_broadcast([P, NG, 4, N]), ALU.mult).then_inc(s_qm, 1)
                    pool.wait_ge(s_qm, b + 1)
                    hold(pool)
                    pool.tensor_copy(qb[s][:, :, 0], qm[:, :, :, :]).then_inc(s_qh, 1)
                    pool.wait_ge(s_qh, b + 1)
                    pool.tensor_tensor(qb[s][:, :, 1], qm[:, :, :, :], qb[s][:, :, 0].bitcast(F32), ALU.subtract).then_inc(s_qb, 1)

                pool.wait_ge(s_wkv, 48)
                pool.tensor_copy(w_kv[:, :, 0], w_raw[:, :]).then_inc(s_wsp, 1)
                pool.wait_ge(s_wsp, 1)
                pool.tensor_tensor(w_kv[:, :, 1], w_raw[:, :], w_kv[:, :, 0].bitcast(F32), ALU.subtract).then_inc(s_wsp, 1)
                for c in range(NC4):
                    split(0, c)
                spread(0, 0)

                def ahead(i):
                    for s in range(2):
                        for c in range(NC4):
                            split(2 * i + s + 1, c)
                        spread(2 * i + s + 1, 1 - s)

                ahead(0)
                with pool.Fori(1, LASTI) as i:
                    ahead(i)
                for c in range(NC4):
                    split(2 * LASTI + 1, c)
                spread(2 * LASTI + 1, 1)

            @blk.tensor
            def _(pe):
                PARTS = [(0, 0), (0, 1), (1, 0)]

                def keys(b, n):
                    m, c = n // 4, n % 4
                    if m == 0:
                        pe.wait_ge(s_split, 4 * b + c + 1)
                    for k, (a, z, h) in enumerate((a, z, h) for a in range(KC) for z, h in PARTS):
                        mm = pe.matmul(bank_x[:, 0:CM[c]], w_kv[:, 0, h, a, m * P:(m + 1) * P], cx[c][:, z, a, :],
                                       start=(k == 0), stop=(k == 3 * KC - 1))
                    mm.then_inc(s_k, 1)

                def values(n):
                    for h, lt in enumerate(range(2 * n, min(2 * n + 2, LT))):
                        rows = LAST if lt == LT - 1 else P
                        c = min(lt // 3, NC4 - 1)
                        at = lt * P - CO[c]
                        for k, (a, z, w) in enumerate((a, z, w) for a in range(KC) for z, w in PARTS):
                            o = C * (h + (n == 6))
                            mm = pe.matmul(bank_c[0:rows, o:o + C], cx[c][:, z, a, at:at + rows],
                                           w_kv[:, 1, w, a, :], start=(k == 0), stop=(k == 3 * KC - 1))
                    mm.then_inc(s_v, 1)

                def scores_of(i, u):
                    ii, uu = (i, u) if u < UNITS else (i + 1, u - UNITS)
                    s, p = uu // PAIRS, uu % PAIRS
                    b = 2 * ii + s
                    if p == 0:
                        pe.wait_ge(s_qb, b + 1)
                    if p % 4 == 0:
                        pe.wait_ge(s_klo, 8 * b + p + 4)

                    def chunk(c):
                        n = 4 * uu + c
                        if n >= 3:
                            pe.wait_ge(s_ttr, 64 * ii + n - 2)
                        elif not (isinstance(ii, int) and ii == 0):
                            pe.wait_ge(s_ttr, 64 * ii - {0: 0, 1: 2, 2: 1}[n])
                        for h in range(2):
                            mm = pe.matmul(bank_s[n % 3][:, 0:CM[c]], qb[s][:, p, h].rearrange("p h n -> p (h n)"),
                                           kt[:, p // 2, CO[c]:CO[c] + CM[c]], start=(h == 0), stop=(h == 1))
                        mm.then_inc(s_sc, 1)

                    return chunk

                def turn(i, u, groups):
                    if groups[0] == 0:
                        pe.wait_ge(s_exp, UNITS * i + u + 1)
                    for g in groups:
                        if g == 3:
                            pe.wait_ge(s_td, UNITS * i + u + 1)
                        elif not (isinstance(i, int) and i == 0 and u == 0 and g < 2):
                            pe.wait_ge(s_ta, 3 * (UNITS * i + u) + (-1, 0, 1)[g])
                        for q, lt in enumerate(range(4 * g, min(4 * g + 4, LT))):
                            rows = LAST if lt == LT - 1 else P
                            mm = pe.transpose(bank_t[g % 2][0:rows, q * P:(q + 1) * P], sm[u % 2][:, lt * P:lt * P + rows],
                                              ident_f[:, :])
                        mm.then_inc(s_t, 1)

                def pv(i, u):
                    s, g = u // PAIRS, (u % PAIRS) // 2
                    b = 2 * i + s
                    pe.wait_ge(s_ta, 3 * (UNITS * i + u + 1))
                    pe.wait_ge(s_td, UNITS * i + u + 1)
                    if g == 0:
                        pe.wait_ge(s_vo, 7 * b + 7)
                    if g % 2 == 0 and not (isinstance(i, int) and i == 0 and u == 1):
                        pe.wait_ge(s_of, 4 * i + u // 4)
                    for lt in range(LT):
                        rows = LAST if lt == LT - 1 else P
                        z = lt % 2
                        mm = pe.matmul(bank_o[z * G4:(z + 1) * G4, (g % 2) * C:(g % 2 + 1) * C],
                                       vt[s][0:rows, lt, g * G4:(g + 1) * G4],
                                       pt[(u // 2) % 2][0:rows, lt, :, :].rearrange("p j n -> p (j n)"),
                                       start=(lt < 2), stop=(lt >= LT - 2), skip_group_check=True)
                    mm.then_inc(s_pv, 1)

                def out_turn(i):
                    pe.wait_ge(s_fin, FINS * i + FINS - 1)
                    for g in range(NG):
                        mm = pe.matmul(bank_c[:, g * G4:(g + 1) * G4], ot[:, g, :], fold[:, :], start=True, stop=True)
                    mm.then_inc(ev("o_turned"), 1)

                def tile(i, last):
                    for u in range(UNITS):
                        s, v = u // PAIRS, u % PAIRS
                        b = 2 * i + s
                        project = v < 2 or not (last and s == 1)
                        turn(i, u, (0, 1))
                        if project:
                            pe.wait_ge(s_klo, 8 * b + 6 + v)
                            keys(b if v < 2 else b + 1, k_item(v))
                        turn(i, u, (2, 3))
                        chunk = None if last and u + 2 >= UNITS else scores_of(i, u + 2)
                        for c in range(3):
                            if chunk:
                                chunk(c)
                        if project and v != 1:
                            pe.wait_ge(s_vo, 7 * b + (6 if v == 0 else 5 + v))
                            if u == 2 and not start(i, 0):
                                pe.wait_ge(s_fin, FINS * i)
                            values(v_item(v))
                        if chunk:
                            chunk(3)
                        if u == 1 and not (isinstance(i, int) and i == 0):
                            pe.wait_ge(s_vo, 14 * i + 7)
                            out_turn(i - 1)
                        if u % 2 == 1:
                            pv(i, u)

                pe.wait_ge(s_wsp, 2)
                for n in range(6):
                    if n:
                        pe.wait_ge(s_klo, n)
                    keys(0, n)
                    if n:
                        pe.wait_ge(s_vo, n)
                    values(n)
                for u in range(2):
                    chunk = scores_of(0, u)
                    for c in range(NC4):
                        chunk(c)
                tile(0, False)
                with pe.Fori(1, LASTI) as i:
                    tile(i, False)
                tile(LASTI, True)
                out_turn(LASTI)

            @blk.scalar
            def _(act):
                def keys_high(b, n, before):
                    m, c = n // 4, n % 4
                    act.wait_ge(s_k, before + 1)
                    for z in range(2):
                        r = slice(z * G4, (z + 1) * G4)
                        ins = act.activation(kt[r, 2 * m + z, CO[c]:CO[c] + CM[c]], bank_x[r, 0:CM[c]], ACT.Identity,
                                             bias=bks[r, m:m + 1])
                    ins.then_inc(s_khi, 1)

                def values_out(s, n, before):
                    act.wait_ge(s_v, before + 1)
                    if n == 6:
                        ins = act.activation(vt[s][0:LAST, LT - 1, :], bank_c[0:LAST, C:2 * C], ACT.Copy)
                    else:
                        ins = act.activation(vt[s][:, 2 * n:2 * n + 2, :].rearrange("p t c -> p (t c)"), bank_c[:, :], ACT.Copy)
                    ins.then_inc(s_vo, 1)

                def exp(i, u):
                    ii, uu = (i, u) if u < UNITS else (i + 1, u - UNITS)
                    s, p = uu // PAIRS, uu % PAIRS
                    act.wait_ge(s_nm, UNITS * ii + uu + 1)
                    if p == 0 and not (isinstance(ii, int) and ii == 0):
                        act.wait_ge(s_rs, 2 * ii + s - 1)
                    hold(act)
                    act.activation(sm[uu % 2][:, :], sm[uu % 2][:, :], ACT.Exp, bias=nmin[:, uu % 2:uu % 2 + 1], scale=-1.0,
                                   accum_out=sums[s][:, p:p + 1]).then_inc(s_exp, 1)

                def turned_out(i, u, g):
                    act.wait_ge(s_t, 4 * (UNITS * i + u) + g + 1)
                    if u % 2 == 0 and g == 0 and not (isinstance(i, int) and i == 0 and u < 4):
                        act.wait_ge(s_pv, 8 * i + u // 2 - 1)
                    rows, k = (LAST, 1) if g == 3 else (P, 4)
                    act.activation(pt[(u // 2) % 2][0:rows, 4 * g:4 * g + k, u % 2, :],
                                   bank_t[g % 2][0:rows, 0:k * P].rearrange("p (t n) -> p t n", t=k), ACT.Copy).then_inc(s_ta, 1)

                def tile(i, last):
                    for u in range(UNITS):
                        s, v = u // PAIRS, u % PAIRS
                        b = 2 * i + s
                        project = v < 2 or not (last and s == 1)
                        turned_out(i, u, 0)
                        if not (last and u + 1 >= UNITS):
                            exp(i, u + 1)
                        if project:
                            keys_high(b, k_item(v), 8 * b + 6 + v)
                        turned_out(i, u, 2)
                        turned_out(i, u, 3)
                        if project and v != 1:
                            values_out(s if v == 0 else 1 - s, v_item(v), 7 * b + (6 if v == 0 else 5 + v))

                act.wait_ge(s_wkv, 48)
                for n in range(6):
                    keys_high(0, n, n)
                    values_out(0, n, n)
                exp(0, 0)
                tile(0, False)
                with act.Fori(1, LASTI) as i:
                    tile(i, False)
                tile(LASTI, True)

            @blk.vector
            def _(dve):
                def keys_low(n, before):
                    m, c = n // 4, n % 4
                    dve.wait_ge(s_khi, before + 1)
                    hold(dve)
                    for z in range(2):
                        r, o = slice(z * G4, (z + 1) * G4), slice((1 - z) * G4, (2 - z) * G4)
                        cols = slice(CO[c], CO[c] + CM[c])
                        ins = dve.scalar_tensor_tensor(kt[o, 2 * m + z, cols], bank_x[r, 0:CM[c]], bks[r, m:m + 1],
                                                       kt[r, 2 * m + z, cols].bitcast(F32), ALU.add, ALU.subtract)
                    ins.then_inc(s_klo, 1)

                def masked(i, u, chunks):
                    ii, uu = (i, u) if u < UNITS else (i + 1, u - UNITS)
                    s = uu // PAIRS
                    for c in chunks:
                        if c == 0:
                            if uu % PAIRS == 0:
                                dve.wait_ge(s_mk[s], 32 * (ii + 1))
                                hold(dve)
                            if not (isinstance(ii, int) and ii == 0 and uu < 2):
                                dve.wait_ge(s_t, 4 * (UNITS * ii + uu - 1))
                                hold(dve)
                        dve.wait_ge(s_sc, 64 * ii + 4 * uu + c + 1)
                        hold(dve)
                        dve.tensor_tensor_reduce(
                            out=sm[uu % 2][:, CO[c]:CO[c] + CH[c]], in0=bank_s[(4 * uu + c) % 3][:, 0:CH[c]],
                            in1=mk[s][:, CO[c]:CO[c] + CH[c]], scale=-1.0, scalar=BIG, op0=ALU.add, op1=ALU.min,
                            accum_out=nmax[:, uu % 2, c:c + 1]).then_inc(s_ttr, 1)
                        if c == NC4 - 1:
                            dve.wait_ge(s_ttr, 64 * ii + 4 * uu + 4)
                            dve.tensor_reduce(nmin[:, uu % 2:uu % 2 + 1], nmax[:, uu % 2, :], AX.X, ALU.min).then_inc(s_nm, 1)

                def turned_out(i, u):
                    dve.wait_ge(s_t, 4 * (UNITS * i + u) + 2)
                    if u % 2 == 0 and not (isinstance(i, int) and i == 0 and u < 4):
                        dve.wait_ge(s_pv, 8 * i + u // 2 - 1)
                    dve.tensor_copy(pt[(u // 2) % 2][:, 4:8, u % 2, :],
                                    bank_t[1][:, :].rearrange("p (t n) -> p t n", t=4)).then_inc(s_td, 1)

                def step(i, n, ins):
                    ins.then_inc(s_fin, 1)
                    dve.wait_ge(s_fin, FINS * i + n)
                    hold(dve)

                def half_out(i, h):
                    n = 4 * i + h + 1
                    dve.wait_ge(s_pv, 2 * n)
                    dve.tensor_tensor(ot4[:, :, :, :], bank_o[:, :].rearrange("p (m g n) -> p m g n", m=2, g=4),
                                      group[:, :].unsqueeze(1).unsqueeze(3).to_broadcast([P, 2, 4, N]),
                                      ALU.mult).then_inc(s_of, 1)
                    dve.wait_ge(s_of, n)
                    if h == 0 and not (isinstance(i, int) and i == 0):
                        need(dve, "o_turned", i - 1)
                    s = h // 2
                    step(i, (1, 2, 5, 6)[h],
                         dve.tensor_reduce(ot[:, 2 * (h % 2):2 * (h % 2) + 2, s * N:(s + 1) * N],
                                           ot4[:, :, :, :].rearrange("p m g n -> p m n g"), AX.X, ALU.add))
                    if h % 2:
                        dve.wait_ge(s_exp, PAIRS * (2 * i + s + 1))
                        dve.reciprocal(rsum[:, :], sums[s][:, :]).then_inc(s_rs, 1)
                        dve.wait_ge(s_rs, 2 * i + s + 1)
                        for j in range(2):
                            step(i, 4 * s + 3 + j, dve.tensor_copy(rtok[s * N:(s + 1) * N, :, j], rsum[j * N:(j + 1) * N, :]))

                def tokens_out(i):
                    need(dve, "o_turned", i)
                    step(i, FINS, dve.tensor_tensor(o_all[:, bass.ds(i, 1), :].rearrange("p t (h d) -> p (t h) d", d=D),
                                                    bank_c[:, 0:C].rearrange("p (h d) -> p h d", d=D),
                                                    rtok[:, :, :].rearrange("p a j -> p (a j)").unsqueeze(2)
                                                    .to_broadcast([P, H, D]), ALU.mult))

                def tile(i, last):
                    for u in range(UNITS):
                        s, v = u // PAIRS, u % PAIRS
                        b = 2 * i + s
                        if not start(i, u):
                            if u == 0:
                                half_out(i - 1, 3)
                            elif u % 4 == 0:
                                half_out(i, u // 4 - 1)
                        turned_out(i, u)
                        scored = not (last and u + 2 >= UNITS)
                        if scored:
                            masked(i, u + 2, range(3))
                        if v < 2 or not (last and s == 1):
                            keys_low(k_item(v), 8 * b + 6 + v)
                        if scored:
                            masked(i, u + 2, range(3, NC4))
                        if u == 1 and not start(i, 0):
                            tokens_out(i - 1)

                dve.wait_ge(s_wkv, 48)
                for n in range(6):
                    keys_low(n, n)
                masked(0, 0, range(NC4))
                masked(0, 1, range(NC4))
                tile(0, False)
                with dve.Fori(1, LASTI) as i:
                    tile(i, False)
                tile(LASTI, True)
                half_out(LASTI, 3)
                tokens_out(LASTI)

        chain_and_experts(nc, ctx, sb, sem, ev, need, hold, bank_s, bank_t, bank_x, bank_c, bank_o, ident_f, ident_b,
                          o_all, half, half_exp, wo_qt, swo_b, x, bo_b, bv_b, w_qkvg, w_o, gnw_b, gnb_b, gate_t,
                          w_gu, w_dn, cos_t, sin_t, decay, tri, expand, out)


def chain_and_experts(nc, ctx, sb, sem, ev, need, hold, bank_s, bank_t, bank_x, bank_c, bank_o, ident_f, ident_b,
                      o_all, half, half_exp, wo_qt, swo_b, x, bo_b, bv_b, w_qkvg, w_o, gnw_b, gnb_b, gate_t,
                      w_gu, w_dn, cos_t, sin_t, decay, tri, expand, out):
    with ExitStack() as keep:
        x3h = sb(keep, "x3_high", [P, KC, TILES * P], F32R)
        x3l = sb(keep, "x3_low", [P, KC, TILES * P], F32R)
        comb = sb(keep, "comb", [3 * E + 1, TILES * P], BF16)
        wex = sb(keep, "expand", [3 * E + 1, JT, P], BF16)
        wgu = [sb(keep, f"wgu{n}", [P, 2, KC, P]) for n in range(2)]
        wdn = [sb(keep, f"wdn{n}", [P, C]) for n in range(2)]
        wgu_p = [sb(keep, f"wgu_parts{n}", [P, 2, 2, KC, P], F32R) for n in range(2)]
        wdn_p = [sb(keep, f"wdn_parts{n}", [P, 2, C], F32R) for n in range(2)]
        s_wex, s_wl = sem("expand_loaded"), [sem(f"expert_w{n}") for n in range(2)]
        s_guh, s_gu, s_dh, s_dp = sem("wgu_high"), sem("wgu_split"), sem("wdn_high"), sem("wdn_split")
        s_ud, s_dn = sem("up_mm"), sem("down_done")

        def load_weights(sp, j, b):
            if not (isinstance(j, int) and j < 2):
                sp.wait_ge(s_dp, j - 1)
            sp.dma_start(wgu[b][:, :, :, :], w_gu[j]).then_inc(s_wl[b], 16)
            sp.dma_start(wdn[b][:, :], w_dn[j]).then_inc(s_wl[b], 16)

        def split_weights(pool, j, b, r):
            later = not (isinstance(j, int) and j < 2)
            pool.wait_ge(s_wl[b], 32 * (r + 1))
            if later:
                pool.wait_ge(s_ud, 2 * (j - 1))
            hold(pool)
            pool.tensor_copy(wgu_p[b][:, 0], wgu[b][:, :, :, :]).then_inc(s_guh, 1)
            pool.wait_ge(s_guh, j + 1)
            pool.tensor_tensor(wgu_p[b][:, 1], wgu[b][:, :, :, :], wgu_p[b][:, 0].bitcast(F32), ALU.subtract).then_inc(s_gu, 1)
            if later:
                pool.wait_ge(s_dn, 2 * (j - 1))
                hold(pool)
            pool.tensor_copy(wdn_p[b][:, 0], wdn[b][:, :]).then_inc(s_dh, 1)
            pool.wait_ge(s_dh, j + 1)
            pool.tensor_tensor(wdn_p[b][:, 1], wdn[b][:, :], wdn_p[b][:, 0].bitcast(F32), ALU.subtract).then_inc(s_dp, 1)

        with ExitStack() as ph:
            def lane_sb(name, shape, dt=F32, n=LANES):
                return [sb(ph, f"{name}{a}", shape, dt) for a in range(n)]

            xb = sb(ph, "xb", [P, TILES, C])
            bo = sb(ph, "bo", [P, C])
            bv = sb(ph, "bv", [P, C])
            wr = sb(ph, "wr", [P, KC, 4 * C])
            wor = sb(ph, "wor", [P, KC, C])
            gnw = sb(ph, "gnw", [P, C])
            gnb = sb(ph, "gnb", [P, C])
            gw = sb(ph, "gw", [P, KC, E])
            cost = sb(ph, "cost", [P, 2, D])
            sint = sb(ph, "sint", [P, 2, D])
            dec = sb(ph, "dec", [P, H, N])
            lower = sb(ph, "lower", [P, E, E])
            oc = lane_sb("o_clipped", [P, C])
            oq = lane_sb("o_scaled", [P, C])
            oi = lane_sb("o_int", [P, C], BF16)
            oqt = lane_sb("o_int_t", [P, KC, P], BF16)
            sc = lane_sb("o_scales", [P, 4])
            x1 = lane_sb("x1", [P, C])
            stats = lane_sb("ln_stats", [P, 6])
            mv = lane_sb("ln_mean_var", [P, 2])
            rstd = lane_sb("ln_rstd", [P, 2])
            xn = lane_sb("x_normed", [P, C])
            xnt = lane_sb("x_normed_t", [P, KC, P])
            ra = lane_sb("rotated", [P, 2 * H, D])
            rb = lane_sb("rot_sin", [P, 2 * H, D])
            rqt = lane_sb("ret_q_t", [P, KC, P])
            rkt = lane_sb("ret_k_t", [P, KC, P])
            rqb = lane_sb("ret_q_blocks", [P, KC, 2, HH, N], n=2)
            rv = lane_sb("ret_v", [P, C])
            gs = lane_sb("gate", [P, C])
            ret = lane_sb("ret_scores", [P, KC, HH * N], n=2)
            yc = lane_sb("ret_out", [P, H, D])
            ysq = lane_sb("ret_out_sq", [P, H, D])
            gst = lane_sb("gn_stats", [P, 4, H])
            ht = lane_sb("gated_t", [P, KC, P])
            x3s = lane_sb("x3_lane", [P, KC, P])
            rt = lane_sb("route_row", [P, 8])
            es = lane_sb("route_exp", [P, E])
            ps = lane_sb("route_probs", [P, E])
            rank = lane_sb("rank_pairs", [P, 2, E, E])
            rk = lane_sb("ranks", [P, 2, E])
            cw = lane_sb("combine", [P, E])
            cr = lane_sb("combine_rest", [P, 2, E])
            c3 = lane_sb("combine_parts", [P, 3 * E], BF16)
            bank_a = [bank_t[0], bank_t[1], bank_x, bank_c]
            bank_b = [bank_s[0], bank_s[1], bank_s[2], bank_o]
            s_ld = sem("chain_loaded")
            s_step, s_pre = [sem(f"chain_dve{a}") for a in range(LANES)], sem("chain_pre")
            LINKS = 39
            lanes = range(LANES)
            blk = ph.enter_context(nc.Block())

            @blk.sync
            def _(sp):
                sp.dma_start(xb[:, :, :], x.rearrange("(t p) c -> p t c", p=P)).then_inc(s_ld, 16)
                for dst, src in ((bo, bo_b), (bv, bv_b), (gnw, gnw_b), (gnb, gnb_b)):
                    sp.dma_start(dst[:, :], src).then_inc(s_ld, 16)
                for dst, src in ((wr, w_qkvg), (wor, w_o), (gw, gate_t)):
                    sp.dma_start(dst[:, :, :], src.rearrange("(k p) n -> p k n", p=P)).then_inc(s_ld, 16)
                for dst, src in ((cost, cos_t), (sint, sin_t), (dec, decay), (lower, tri)):
                    sp.dma_start(dst[:, :, :], src).then_inc(s_ld, 16)
                sp.dma_start(wex[:, :, :], expand.bitcast(BF16)).then_inc(s_wex, 16)
                for j in range(2):
                    load_weights(sp, j, j)

            def spread_heads(e, a, m, s):
                q = rqt[a][:, m, s * N:(s + 1) * N].unsqueeze(1).to_broadcast([P, HH, N])
                return e.tensor_tensor(rqb[a % 2][:, m, s], q, half[:, :].unsqueeze(2).to_broadcast([P, HH, N]), ALU.mult)

            @blk.gpsimd
            def _(pool):
                def root(name, r, dst, src, eps):
                    for a in lanes:
                        need(pool, name, LANES * r + a)
                        hold(pool)
                        pool.tensor_scalar(src(a), src(a), eps, None, ALU.add).then_inc(ev(name + "_eps"), 1)
                        need(pool, name + "_eps", LANES * r + a)
                        pool.tensor_tensor(dst(a), src(a), half_exp[:, 0:dst(a).shape[1]], ALU.pow)\
                            .then_inc(ev(name + "_root"), 1)

                with pool.Fori(0, TILES // LANES) as r:
                    root("ln2", r, lambda a: rstd[a][:, 0:1], lambda a: mv[a][:, 1:2], LN_EPS)
                    for a in lanes:
                        t = LANES * r + a
                        need(pool, "rq_ready", t)
                        if a >= 2:
                            need(pool, "ret_done1", t - 2)
                        hold(pool)
                        for s in range(2):
                            tt = spread_heads(pool, a, 0, s)
                        tt.then_inc(ev("rqb0_ready"), 1)
                    root("gn", r, lambda a: gst[a][:, 2, :], lambda a: gst[a][:, 1, :], GN_EPS)
                    root("ln3", r, lambda a: rstd[a][:, 1:2], lambda a: mv[a][:, 1:2], LN_EPS)
                    for a in lanes:
                        t = LANES * r + a
                        need(pool, "x3h_ready", t)
                        hold(pool)
                        high = x3h[:, :, bass.ds(t * P, P)]
                        pool.tensor_tensor(x3l[:, :, bass.ds(t * P, P)], x3s[a][:, :, :], high.bitcast(F32),
                                           ALU.subtract).then_inc(ev("x3l_ready"), 1)
                for j in range(2):
                    split_weights(pool, j, j, 0)

            @blk.vector
            def _(dve):
                pre = [0]

                def link(ins):
                    pre[0] += 1
                    ins.then_inc(s_pre, 1)
                    dve.wait_ge(s_pre, pre[0])

                dve.wait_ge(s_ld, 16 * 12)
                link(dve.tensor_tensor(xb[:, :, :], xb[:, :, :], bo[:, :].unsqueeze(1).to_broadcast([P, TILES, C]), ALU.add))
                link(dve.memset(comb[32:3 * E + 1, :], 1.0))
                with dve.Fori(0, TILES // LANES) as r:
                    n = [0] * LANES

                    def each(instruction, after=None, name=None, on=lanes):
                        for a in on:
                            if n[a]:
                                dve.wait_ge(s_step[a], LINKS * r + n[a])
                            if after:
                                need(dve, after, LANES * r + a)
                            hold(dve)
                            instruction(a).then_inc(ev(name) if name else s_step[a], 1)
                            if not name:
                                n[a] += 1

                    def heads(ap):
                        return ap.rearrange("p (h d) -> p h d", d=D)

                    def flat(ap):
                        return ap.rearrange("p h d -> p (h d)")

                    def by_head(ap):
                        return ap.unsqueeze(2).to_broadcast([P, H, D])

                    each(lambda a: dve.tensor_tensor(oc[a][:, :], o_all[:, LANES * r + a, :], bv[:, :], ALU.add))
                    each(lambda a: dve.tensor_reduce(sc[a][:, 0:1], oc[a][:, :], AX.X, ALU.max, apply_absolute_value=True))
                    each(lambda a: dve.tensor_scalar(sc[a][:, 1:2], sc[a][:, 0:1], 1.0 / 127.0, Q_EPS, ALU.mult, ALU.max))
                    each(lambda a: dve.reciprocal(sc[a][:, 2:3], sc[a][:, 1:2]))
                    each(lambda a: dve.tensor_scalar(oc[a][:, :], oc[a][:, :], sc[a][:, 2:3], 127.0, ALU.mult, ALU.min))
                    each(lambda a: dve.tensor_scalar(oq[a][:, :], oc[a][:, :], -127.0, ROUND, ALU.max, ALU.add))
                    each(lambda a: dve.tensor_scalar(oi[a][:, :], oq[a][:, :], -ROUND, None, ALU.add), name="oi_ready")
                    each(lambda a: dve.scalar_tensor_tensor(oq[a][:, :], bank_a[a][:, 0:C], sc[a][:, 1:2], swo_b[:, :],
                                                            ALU.mult, ALU.mult), after="y_done")
                    each(lambda a: dve.tensor_tensor(x1[a][:, :], oq[a][:, :], xb[:, LANES * r + a, :], ALU.add))

                    def norm(src, name, col, done):
                        each(lambda a: dve.bn_stats(stats[a][:, :], src(a)))
                        each(lambda a: dve.bn_aggr(mv[a][:, :], stats[a][:, :]), name=name)
                        each(lambda a: dve.tensor_scalar(xn[a][:, :], src(a), mv[a][:, 0:1], rstd[a][:, col:col + 1],
                                                         ALU.subtract, ALU.mult), after=name + "_root", name=done)

                    norm(lambda a: x1[a][:, :], "ln2", 0, "xn2_ready")

                    def qk(a):
                        return bank_a[a][:, :].rearrange("p (a h d) -> p a h d", a=2, d=D)

                    def sin_part(a, z):
                        zs, zo = slice(8 * z, 8 * z + 8), slice(8 - 8 * z, 16 - 8 * z)
                        return dve.tensor_tensor(rb[a][:, :, zs].rearrange("p (a h) d -> p a h d", a=2), qk(a)[:, :, :, zo],
                                                 sint[:, :, zs].unsqueeze(2).to_broadcast([P, 2, H, D // 2]), ALU.mult)

                    each(lambda a: dve.tensor_tensor(ra[a][:, :, :].rearrange("p (a h) d -> p a h d", a=2), qk(a),
                                                     cost[:, :, :].unsqueeze(2).to_broadcast([P, 2, H, D]), ALU.mult),
                         after="qk_done")
                    each(lambda a: sin_part(a, 0))
                    each(lambda a: sin_part(a, 1))
                    each(lambda a: dve.tensor_tensor(ra[a][:, :, :], ra[a][:, :, :], rb[a][:, :, :], ALU.add), name="qk_rot")
                    for one in range(LANES + 1):
                        if one < LANES:
                            need(dve, "rq_ready", LANES * r + one)
                            if one >= 2:
                                need(dve, "ret_done1", LANES * r + one - 2)
                            hold(dve)
                            for s in range(2):
                                tt = spread_heads(dve, one, 1, s)
                            tt.then_inc(ev("rqb1_ready"), 1)
                        if one:
                            for m, bank in enumerate((bank_a, bank_b)):
                                each(lambda a: dve.tensor_tensor(ret[a % 2][:, m, :], bank[a][:, :],
                                                                 flat(dec[:, m * HH:(m + 1) * HH, :]), ALU.mult),
                                     after=f"ret_done{m}", name=f"ret_ready{m}", on=[one - 1])
                    for one in lanes:
                        on = [one]
                        each(lambda a: dve.tensor_reduce(gst[a][:, 0, :], heads(bank_a[a][:, 0:C]), AX.X, ALU.add),
                             after="yr_done", on=on)
                        each(lambda a: dve.tensor_scalar(gst[a][:, 0, :], gst[a][:, 0, :], 1.0 / D, None, ALU.mult), on=on)
                        each(lambda a: dve.tensor_tensor(yc[a][:, :, :], heads(bank_a[a][:, 0:C]), by_head(gst[a][:, 0, :]),
                                                         ALU.subtract), on=on)
                        each(lambda a: dve.tensor_tensor(ysq[a][:, :, :], yc[a][:, :, :], yc[a][:, :, :], ALU.mult), on=on)
                        each(lambda a: dve.tensor_reduce(gst[a][:, 3, :], ysq[a][:, :, :], AX.X, ALU.add), on=on)
                        each(lambda a: dve.tensor_scalar(gst[a][:, 1, :], gst[a][:, 3, :], 1.0 / D, None, ALU.mult),
                             name="gn", on=on)
                    each(lambda a: dve.tensor_tensor(yc[a][:, :, :], yc[a][:, :, :], by_head(gst[a][:, 2, :]), ALU.mult),
                         after="gn_root")
                    each(lambda a: dve.tensor_tensor(flat(yc[a][:, :, :]), flat(yc[a][:, :, :]), gnw[:, :], ALU.mult))
                    each(lambda a: dve.tensor_tensor(flat(yc[a][:, :, :]), flat(yc[a][:, :, :]), gnb[:, :], ALU.add))
                    each(lambda a: dve.tensor_tensor(flat(yc[a][:, :, :]), flat(yc[a][:, :, :]), gs[a][:, :], ALU.mult),
                         after="gate_ready", name="h_ready")
                    each(lambda a: dve.tensor_tensor(o_all[:, LANES * r + a, :], x1[a][:, :], bank_a[a][:, 0:C], ALU.add),
                         after="wo_done")
                    norm(lambda a: o_all[:, LANES * r + a, :], "ln3", 1, "xn3_ready")
                    each(lambda a: dve.tensor_reduce(rt[a][:, 0:1], bank_a[a][:, 0:E], AX.X, ALU.max, negate=True),
                         after="logits_done", name="rt_max")
                    each(lambda a: dve.reciprocal(rt[a][:, 2:3], rt[a][:, 1:2]), after="rt_exp")
                    each(lambda a: dve.tensor_scalar(ps[a][:, :], es[a][:, :], rt[a][:, 2:3], None, ALU.mult))

                    def rivals(a):
                        return ps[a][:, :].unsqueeze(1).to_broadcast([P, E, E]), ps[a][:, :].unsqueeze(2).to_broadcast([P, E, E])

                    each(lambda a: dve.tensor_tensor(rank[a][:, 0], *rivals(a), ALU.is_gt))
                    each(lambda a: dve.tensor_tensor(rank[a][:, 1], *rivals(a), ALU.is_equal))
                    each(lambda a: dve.tensor_tensor(rank[a][:, 1], rank[a][:, 1], lower[:, :, :], ALU.mult))
                    each(lambda a: dve.tensor_reduce(rk[a][:, :, :], rank[a][:, :, :, :], AX.X, ALU.add))
                    each(lambda a: dve.tensor_tensor(cw[a][:, :], rk[a][:, 0], rk[a][:, 1], ALU.add))
                    each(lambda a: dve.tensor_scalar(cw[a][:, :], cw[a][:, :], TOPK - 0.5, None, ALU.is_lt))
                    each(lambda a: dve.tensor_tensor(cw[a][:, :], cw[a][:, :], ps[a][:, :], ALU.mult))
                    each(lambda a: dve.tensor_reduce(rt[a][:, 3:4], cw[a][:, :], AX.X, ALU.add))
                    each(lambda a: dve.reciprocal(rt[a][:, 4:5], rt[a][:, 3:4]))
                    each(lambda a: dve.tensor_scalar(cw[a][:, :], cw[a][:, :], rt[a][:, 4:5], None, ALU.mult))
                    each(lambda a: dve.tensor_copy(c3[a][:, 0:E], cw[a][:, :]))
                    each(lambda a: dve.tensor_tensor(cr[a][:, 0], cw[a][:, :], c3[a][:, 0:E], ALU.subtract))
                    each(lambda a: dve.tensor_copy(c3[a][:, E:2 * E], cr[a][:, 0]))
                    each(lambda a: dve.tensor_tensor(cr[a][:, 1], cr[a][:, 0], c3[a][:, E:2 * E], ALU.subtract))
                    each(lambda a: dve.tensor_copy(c3[a][:, 2 * E:3 * E], cr[a][:, 1]), name="c3_ready")
                    each(lambda a: dve.tensor_copy(comb[0:3 * E, bass.ds((LANES * r + a) * P, P)],
                                                   bank_a[a][:, :].bitcast(BF16)[0:3 * E, 0:P]), after="c3_turned")
                    assert n == [LINKS] * LANES

            @blk.scalar
            def _(act):
                with act.Fori(0, TILES // LANES) as r:
                    flat = lambda b: b[:, :, :].rearrange("p k n -> p (k n)")

                    def each(after, dst, src, func, done):
                        for a in lanes:
                            need(act, after, LANES * r + a)
                            act.activation(dst(a), src(a), func).then_inc(ev(done), 1)

                    each("oi_turned", lambda a: flat(oqt[a]), lambda a: bank_a[a][:, :].bitcast(BF16)[:, 0:C], ACT.Copy, "oqt_ready")
                    each("xn2_turned", lambda a: flat(xnt[a]), lambda a: bank_a[a][:, 0:C], ACT.Copy, "xnt_ready")
                    each("vg_done", lambda a: rv[a][:, :], lambda a: bank_b[a][:, 0:C], ACT.Copy, "rv_ready")
                    each("vg_done", lambda a: gs[a][:, :], lambda a: bank_b[a][:, C:2 * C], ACT.Silu, "gate_ready")
                    each("qk_turned", lambda a: flat(rqt[a]), lambda a: bank_a[a][:, 0:C], ACT.Copy, "rq_ready")
                    each("qk_turned", lambda a: flat(rkt[a]), lambda a: bank_a[a][:, C:2 * C], ACT.Copy, "rk_ready")
                    each("h_turned", lambda a: flat(ht[a]), lambda a: bank_a[a][:, 0:C], ACT.Copy, "ht_ready")
                    each("xn3_turned", lambda a: flat(x3s[a]), lambda a: bank_a[a][:, 0:C], ACT.Copy, "x3s_ready")
                    for a in lanes:
                        need(act, "x3s_ready", LANES * r + a)
                        act.activation(x3h[:, :, bass.ds((LANES * r + a) * P, P)], x3s[a][:, :, :],
                                       ACT.Copy).then_inc(ev("x3h_ready"), 1)
                    for a in lanes:
                        need(act, "rt_max", LANES * r + a)
                        act.activation(es[a][:, :], bank_a[a][:, 0:E], ACT.Exp, bias=rt[a][:, 0:1],
                                       accum_out=rt[a][:, 1:2]).then_inc(ev("rt_exp"), 1)

            @blk.tensor
            def _(pe):
                with pe.Fori(0, TILES // LANES) as r:
                    def turn(after, src, ident, bank, done):
                        for a in lanes:
                            need(pe, after, LANES * r + a)
                            for k in range(KC):
                                mm = pe.transpose(bank(a)[:, k * P:(k + 1) * P], src(a)[:, k * P:(k + 1) * P], ident)
                            mm.then_inc(ev(done), 1)

                    def project(after, dst, lhs, rhs, done):
                        for a in lanes:
                            need(pe, after, LANES * r + a)
                            for k in range(KC):
                                mm = pe.matmul(dst(a), lhs[a][:, k, :], rhs(k), start=(k == 0), stop=(k == KC - 1))
                            mm.then_inc(ev(done), 1)

                    turn("oi_ready", lambda a: oi[a], ident_b[:, :], lambda a: bank_a[a][:, :].bitcast(BF16), "oi_turned")
                    project("oqt_ready", lambda a: bank_a[a][:, 0:C], oqt, lambda k: wo_qt[:, k, :], "y_done")
                    turn("xn2_ready", lambda a: xn[a], ident_f[:, :], lambda a: bank_a[a], "xn2_turned")
                    project("xnt_ready", lambda a: bank_a[a][:, :], xnt, lambda k: wr[:, k, 0:2 * C], "qk_done")
                    project("xnt_ready", lambda a: bank_b[a][:, :], xnt, lambda k: wr[:, k, 2 * C:4 * C], "vg_done")
                    for a in lanes:
                        need(pe, "qk_rot", LANES * r + a)
                        rot = ra[a][:, :, :].rearrange("p h d -> p (h d)")
                        for k in range(2 * KC):
                            mm = pe.transpose(bank_a[a][:, k * P:(k + 1) * P], rot[:, k * P:(k + 1) * P], ident_f[:, :])
                        mm.then_inc(ev("qk_turned"), 1)
                    def ret_scores(a):
                        t = LANES * r + a
                        need(pe, "rk_ready", t)
                        for m, bank in enumerate((bank_a, bank_b)):
                            need(pe, f"rqb{m}_ready", t)
                            if m:
                                need(pe, "gate_ready", t)
                            for s in range(2):
                                mm = pe.matmul(bank[a][s * N:(s + 1) * N, :], rkt[a][:, m, s * N:(s + 1) * N],
                                               rqb[a % 2][:, m, s].rearrange("p h n -> p (h n)"), start=True, stop=True)
                            mm.then_inc(ev(f"ret_done{m}"), 1)

                    def ret_values(a):
                        t = LANES * r + a
                        need(pe, "ret_ready0", t)
                        need(pe, "ret_ready1", t)
                        need(pe, "rv_ready", t)
                        hold(pe)
                        for s in range(2):
                            for h in range(H):
                                mm = pe.matmul(bank_a[a][s * N:(s + 1) * N, h * D:(h + 1) * D],
                                               ret[a % 2][s * N:(s + 1) * N, h // HH, (h % HH) * N:(h % HH + 1) * N],
                                               rv[a][s * N:(s + 1) * N, h * D:(h + 1) * D], start=True, stop=True)
                        mm.then_inc(ev("yr_done"), 1)

                    ret_scores(0)
                    for a in lanes:
                        if a + 1 < LANES:
                            ret_scores(a + 1)
                        ret_values(a)
                    turn("h_ready", lambda a: yc[a][:, :, :].rearrange("p h d -> p (h d)"), ident_f[:, :],
                         lambda a: bank_a[a], "h_turned")
                    project("ht_ready", lambda a: bank_a[a][:, 0:C], ht, lambda k: wor[:, k, :], "wo_done")
                    turn("xn3_ready", lambda a: xn[a], ident_f[:, :], lambda a: bank_a[a], "xn3_turned")
                    project("x3s_ready", lambda a: bank_a[a][:, 0:E], x3s, lambda k: gw[:, k, :], "logits_done")
                    for a in lanes:
                        need(pe, "c3_ready", LANES * r + a)
                        hold(pe)
                        pe.transpose(bank_a[a][:, :].bitcast(BF16)[0:3 * E, 0:P], c3[a][:, :],
                                     ident_b[:, :]).then_inc(ev("c3_turned"), 1)

        with ExitStack() as ph:
            sg = [sb(ph, f"silu{n}", [P, 512]) for n in range(2)]
            su = [sb(ph, f"gated{n}", [P, 512]) for n in range(2)]
            aw = [sb(ph, f"acts{n}", [P, 512]) for n in range(2)]
            ah = [sb(ph, f"acts_high{n}", [P, 512], F32R) for n in range(2)]
            al = [sb(ph, f"acts_low{n}", [P, 512], F32R) for n in range(2)]
            yout = sb(ph, "yout", [P, TILES, C])
            bank_y = [bank_s[0], bank_s[1], bank_s[2], bank_o]
            bank_g, bank_u, bank_w = bank_t[0], bank_t[1], bank_x
            s_gd, s_cd = sem("gate_mm"), sem("weight_mm")
            s_sg, s_su, s_aw, s_ah, s_al = (sem(n) for n in ("silu_done", "gated_done", "acts_done", "acts_high_done", "acts_low_done"))
            s_yo, s_out = sem("y_added"), sem("out_stored")
            NB = TILES * P // 512
            blk = ph.enter_context(nc.Block())

            def tiles_loop(e, body):
                body(0, 0, 0)
                body(1, 1, 0)
                body(2, 0, 1)
                with e.Fori(1, (JT - 1) // 2) as r:
                    body(2 * r + 1, 1, r)
                    body(2 * r + 2, 0, r + 1)

            @blk.sync
            def _(sp):
                def body(j, b, r):
                    if not (isinstance(j, int) and j < 2):
                        load_weights(sp, j, b)

                tiles_loop(sp, body)
                for q in range(2):
                    sp.wait_ge(s_yo, 2 * (q + 1))
                    sp.dma_start(out.rearrange("(t p) c -> p t c", p=P)[:, 4 * q:4 * q + 4, :],
                                 yout[:, 4 * q:4 * q + 4, :]).then_inc(s_out, 16)
                sp.wait_ge(s_out, 32)

            @blk.gpsimd
            def _(pool):
                def body(j, b, r):
                    if not (isinstance(j, int) and j < 2):
                        split_weights(pool, j, b, r)

                tiles_loop(pool, body)

            @blk.tensor
            def _(pe):
                def down(jn, b, n, j, first):
                    pe.wait_ge(s_al, jn + 1)
                    if n == 0:
                        pe.wait_ge(s_dp, j + 1)
                    for q in range(4):
                        tt = 4 * n + q
                        cols = slice(q * P, (q + 1) * P)
                        for k, (acts, w) in enumerate(((ah, 0), (ah, 1), (al, 0))):
                            mm = pe.matmul(bank_y[tt // 2][:, (tt % 2) * C:(tt % 2 + 1) * C], acts[n][:, cols],
                                           wdn_p[b][:, w, :], start=(first and tt % 2 == 0 and k == 0), stop=False,
                                           skip_group_check=True)
                    mm.then_inc(s_dn, 1)

                def body(j, b, r):
                    first = isinstance(j, int) and j == 0
                    pe.wait_ge(s_gu, j + 1)
                    for n in range(NB):
                        jn = NB * j + n
                        cols = slice(n * 512, (n + 1) * 512)
                        for g, (bank, free, done) in enumerate(((bank_g, s_sg, s_gd), (bank_u, s_su, s_ud))):
                            if not (first and n == 0):
                                pe.wait_ge(free, jn)
                            for k, (a, x3, w) in enumerate((a, x3, w) for a in range(KC)
                                                           for x3, w in ((x3h, 0), (x3h, 1), (x3l, 0))):
                                mm = pe.matmul(bank[:, :], wgu_p[b][:, w, g, a, :], x3[:, a, cols],
                                               start=(k == 0), stop=(k == 3 * KC - 1))
                            mm.then_inc(done, 1)
                        if not (first and n == 0):
                            pe.wait_ge(s_aw, jn)
                            hold(pe)
                        pe.matmul(bank_w[:, :], wex[:, j, :], comb[:, cols], start=True, stop=True).then_inc(s_cd, 1)
                        if n == 1:
                            down(jn - 1, b, 0, j, first)
                        elif not first:
                            down(jn - 1, 1 - b, 1, j - 1, isinstance(j, int) and j == 1)

                pe.wait_ge(s_wex, 16)
                tiles_loop(pe, body)
                down(NB * JT - 1, (JT - 1) % 2, 1, JT - 1, False)

            @blk.scalar
            def _(act):
                def body(j, b, r):
                    for n in range(NB):
                        jn = NB * j + n
                        later = not (isinstance(j, int) and j == 0)
                        act.wait_ge(s_gd, jn + 1)
                        if later:
                            act.wait_ge(s_su, jn - 1)
                        act.activation(sg[n][:, :], bank_g[:, :], ACT.Silu).then_inc(s_sg, 1)
                        act.wait_ge(s_aw, jn + 1)
                        if later:
                            act.wait_ge(s_dn, jn - 1)
                        act.activation(ah[n][:, :], aw[n][:, :], ACT.Copy).then_inc(s_ah, 1)

                tiles_loop(act, body)

            @blk.vector
            def _(dve):
                def body(j, b, r):
                    for n in range(NB):
                        jn = NB * j + n
                        dve.wait_ge(s_sg, jn + 1)
                        dve.wait_ge(s_ud, jn + 1)
                        dve.tensor_tensor(su[n][:, :], sg[n][:, :], bank_u[:, :], ALU.mult).then_inc(s_su, 1)
                        dve.wait_ge(s_su, jn + 1)
                        dve.wait_ge(s_cd, jn + 1)
                        dve.tensor_tensor(aw[n][:, :], su[n][:, :], bank_w[:, :], ALU.mult).then_inc(s_aw, 1)
                        dve.wait_ge(s_aw, jn + 1)
                        dve.wait_ge(s_ah, jn + 1)
                        dve.tensor_tensor(al[n][:, :], aw[n][:, :], ah[n][:, :].bitcast(F32), ALU.subtract).then_inc(s_al, 1)

                tiles_loop(dve, body)
                dve.wait_ge(s_dn, NB * JT)
                for q in range(4):
                    dve.tensor_tensor(yout[:, 2 * q:2 * q + 2, :].rearrange("p t c -> p (t c)"),
                                      o_all[:, 2 * q:2 * q + 2, :].rearrange("p t c -> p (t c)"), bank_y[q][:, :],
                                      ALU.add).then_inc(s_yo, 1)


def shape_tables():
    import numpy as np

    p = np.arange(P)
    f = np.float32
    ident = np.eye(P, dtype=f)
    half = (p[:, None] // D == np.arange(HH)[None]).astype(f)
    fold = (p[:, None] % G4 == np.arange(G4)[None]).astype(f)
    group = (p[:, None] // D % 4 == np.arange(4)[None]).astype(f)
    pos = (p % N).astype(f)
    hd = D // 2
    xscale = (np.arange(0, D, 2, dtype=f) + f(0.4 * D)) / f(1.4 * D)
    scale = xscale[None, :] ** (pos[:, None] / f(64))
    inv_freq = f(1.0) / f(10000.0) ** (np.arange(hd, dtype=f) / f(hd))
    sinu = pos[:, None] * inv_freq[None, :]
    cos_t = np.zeros((P, 2, D), f)
    sin_t = np.zeros((P, 2, D), f)
    for a, sc in enumerate((scale, f(1.0) / scale)):
        cos_t[:, a, :hd] = cos_t[:, a, hd:] = np.cos(sinu) * sc
        sin_t[:, a, :hd] = -np.sin(sinu) * sc
        sin_t[:, a, hd:] = np.sin(sinu) * sc
    gammas = 1.0 - np.exp(np.linspace(np.log(1.0 / 32), np.log(1.0 / 64), H)).astype(f)
    gammas = gammas.astype(f)
    m = (p % N)[:, None, None]
    n = np.arange(N)[None, None, :]
    decay = np.where(n >= m, gammas[None, :, None] ** np.maximum(n - m, 0).astype(f), 0.0).astype(f)
    tri = np.broadcast_to((np.arange(E)[None, :] < np.arange(E)[:, None]).astype(f), (P, E, E))
    rows = np.arange(JT * P)
    expand = np.zeros((3 * E + 1, JT * P), f)
    for part in range(3):
        for e in range(E):
            expand[part * E + e] = rows // I == e
    expand[3 * E] = rows >= E * I
    expand = expand.reshape(3 * E + 1, JT, P).astype(np.uint16) * np.uint16(0x3F80)
    return dict(ident=ident, half_sel=half, group_sel=group, fold_sel=fold, cos_t=cos_t, sin_t=sin_t, decay=decay,
                tri=np.ascontiguousarray(tri), expand=expand)


def kernel(**inputs):
    import numpy as np
    import concourse.bacc as bacc
    from concourse import mybir as _mybir
    from concourse.bass_utils import run_bass_kernel_spmd as run

    g = {k: np.asarray(v) for k, v in inputs.items()}
    row = lambda a: np.ascontiguousarray(np.broadcast_to(a[None, :], (P, a.shape[0])))

    def heads(w, evens_first):
        w = w.transpose(1, 0, 2)
        if evens_first:
            w = np.concatenate([w[..., 0::2], w[..., 1::2]], -1)
        return w.reshape(C, H * D)

    def hidden(w):
        w = np.concatenate([w, np.zeros((C, JT * P - w.shape[1]), w.dtype)], 1)
        return w.reshape(KC, P, JT, P).transpose(2, 1, 0, 3)

    w_g = hidden(np.concatenate([g["L0_ffn_w_gate"].transpose(1, 0, 2).reshape(C, E * I), g["L0_ffn_sw_gate"]], 1))
    w_u = hidden(np.concatenate([g["L0_ffn_w_up"].transpose(1, 0, 2).reshape(C, E * I), g["L0_ffn_sw_up"]], 1))
    w_d = np.concatenate([g["L0_ffn_w_down"].reshape(E * I, C), g["L0_ffn_sw_down"]], 0)
    w_d = np.concatenate([w_d, np.zeros((JT * P - w_d.shape[0], C), w_d.dtype)], 0).reshape(JT, P, C)
    arrays = dict(
        x=g["x"].reshape(B * N, C), ctx_t=np.pad(g["ctx_2048"].transpose(0, 2, 1), ((0, 0), (0, 0), (0, LM - L))), mask=g["mask_BxSxS2_ff0"],
        wq=g["L0_xattn_wq"], wk_t=g["L0_xattn_wk"].T, wv_t=g["L0_xattn_wv"].T, wo=g["L0_xattn_wo"],
        bq=np.tile(g["L0_xattn_bq"].reshape(NG, G4).T, (2, 1)), bo_b=row(g["L0_xattn_bo"]), bv_b=row(g["L0_xattn_bv"]),
        w_qkvg=np.concatenate([heads(g["L0_attn_W_Q"], True), heads(g["L0_attn_W_K"], True),
                               heads(g["L0_attn_W_V"], False), g["L0_attn_W_G"]], 1),
        w_o=g["L0_attn_W_O"], gnw_b=row(g["L0_attn_gn_weight"]), gnb_b=row(g["L0_attn_gn_bias"]),
        gate_t=g["L0_ffn_gate_w"].T, w_gu=np.stack([w_g, w_u], 2), w_dn=w_d,
        bk=g["L0_xattn_bk"].reshape(KC, P).T, **shape_tables())
    arrays = {f"in_{k}": np.ascontiguousarray(v) for k, v in arrays.items()}
    nc = bacc.Bacc("TRN2", target_bir_lowering=False, num_devices=1)
    args = {k[3:]: nc.dram_tensor(k, a.shape, _mybir.dt.from_np(a.dtype), kind="ExternalInput").ap()
            for k, a in arrays.items()}
    out = nc.dram_tensor("out_0", (B * N, C), _mybir.dt.float32, kind="ExternalOutput").ap()
    perceiver_program(nc, out=out, **args)
    r = run(nc, [arrays], core_ids=[0])
    return r.results[0]["out_0"].reshape(B, N, C)
```

```python
from contextlib import ExitStack

import concourse.bass as bass
from concourse import mybir
from concourse.alu_op_type import AluOpType as ALU

F32 = mybir.dt.float32
BF16 = mybir.dt.bfloat16
F32R = mybir.dt.float32r
ACT = mybir.ActivationFunctionType
AX = mybir.AxisListType

P = 128
B, N, C = 16, 64, 256
L = 1601
H, D = 16, 16
KC = C // P
HH = H // KC
TILES = B * N // P
PAIRS = H // 2
UNITS = 2 * PAIRS
LT = -(-L // P)
LAST = L - (LT - 1) * P
NC4 = 4
CT = LT // NC4
CO = [c * CT * P for c in range(NC4)]
CH = [CT * P] * (NC4 - 1) + [L - CO[-1]]
LM = L + L % 2
CM = CH[:-1] + [LM - CO[-1]]
G4 = 4 * D
NG = H * D // G4
E, I, TOPK = 16, 176, 4
IS = 2 * I
MT = E * I // P
ST = -(-IS // P)
JT = MT + ST
LANES = 4
ROUND = 12582912.0
BIG = 3.0e38
LN_EPS, Q_EPS, GN_EPS = 1e-5, 1e-8, 1e-5


def perceiver_program(nc, x, ctx_t, mask, wq, wk_t, wv_t, wo, bq, bo_b, bv_b, w_qkvg, w_o, gnw_b, gnb_b,
                      gate_t, w_gu, w_dn, ident, half_sel, group_sel, fold_sel, cos_t, sin_t, decay, tri, expand, bk, out):
    with ExitStack() as ctx:
        def sem(name):
            return ctx.enter_context(nc.semaphore(name))

        def sb(stack, name, shape, dt=F32):
            return stack.enter_context(nc.sbuf_tensor(name, shape, dt))

        events = {}

        def ev(name):
            if name not in events:
                events[name] = sem(name)
            return events[name]

        def need(e, name, t):
            e.wait_ge(ev(name), t + 1)

        def hold(e):
            e.nop(nofuse=True)

        bank_s = [ctx.enter_context(nc.psum_tensor(f"scores{n}", [P, 512], F32)) for n in range(3)]
        bank_t = [ctx.enter_context(nc.psum_tensor(f"turned{n}", [P, 512], F32)) for n in range(2)]
        bank_x = ctx.enter_context(nc.psum_tensor("kv_proj", [P, 512], F32))
        bank_c = ctx.enter_context(nc.psum_tensor("chain", [P, 512], F32))
        bank_o = ctx.enter_context(nc.psum_tensor("attn_out", [P, 512], F32))

        ident_f = sb(ctx, "ident_f", [P, P])
        ident_b = sb(ctx, "ident_b", [P, P], BF16)
        o_all = sb(ctx, "o_all", [P, TILES, C])
        qt_all = sb(ctx, "qt_all", [P, NG, TILES * P])
        wo_qt = sb(ctx, "wo_qt", [P, KC, C], BF16)
        swo_b = sb(ctx, "swo_b", [P, C])
        half = sb(ctx, "half", [P, HH])
        fold = sb(ctx, "fold", [P, G4])
        group = sb(ctx, "group", [P, 4])
        half_exp = sb(ctx, "power", [P, H])

        with ExitStack() as ph:
            raw = [sb(ph, f"ctx_raw{n}", [P, KC, CM[3]]) for n in range(2)]
            cx = [sb(ph, f"ctx_parts{c}", [P, 2, KC, CM[c]], F32R) for c in range(NC4)]
            mk = [sb(ph, f"mask{s}", [P, L]) for s in range(2)]
            kt = sb(ph, "keys", [P, NG, LM], F32R)
            vt = [sb(ph, f"values{s}", [P, LT, C]) for s in range(2)]
            qb = [sb(ph, f"queries{s}", [P, PAIRS, 2, 2, N], F32R) for s in range(2)]
            qm = sb(ph, "queries_masked", [P, PAIRS, 2, N])
            w_raw = sb(ph, "w_raw", [P, 2, KC, C])
            w_kv = sb(ph, "w_kv", [P, 2, 2, KC, C], F32R)
            bks = sb(ph, "bks", [P, KC])
            s_wkv, s_wsp = sem("wkv_loaded"), sem("wkv_split")
            s_raw = [sem(f"ctx_loaded{n}") for n in range(2)]
            s_hi, s_split = sem("ctx_high"), sem("ctx_split")
            s_mk = [sem(f"mask_loaded{s}") for s in range(2)]
            s_k, s_v = sem("k_item_done"), sem("v_item_done")
            s_khi, s_klo, s_vo = sem("keys_high"), sem("keys_low"), sem("values_out")
            s_sc = sem("scores_done")
            s_ttr = sem("scores_masked")
            s_nm = sem("neg_max_ready")
            s_exp = sem("exp_done")
            s_t = sem("turned")
            s_ta, s_td = sem("turned_out_act"), sem("turned_out_dve")
            s_pv = sem("pv_done")
            s_of = sem("attn_out_read")
            s_qm, s_qh, s_qb = sem("queries_masked_done"), sem("queries_high"), sem("queries_set")
            s_rs = sem("sums_read")
            s_fin = sem("attn_dve")
            FINS = 9
            LASTI = TILES - 1

            def k_item(v):
                return (v + 6) % 8

            def v_item(v):
                return None if v == 1 else (6 if v == 0 else v - 2)

            def start(i, u):
                return isinstance(i, int) and i == 0 and u <= 0

            def load(sp, b, c):
                if not (isinstance(b, int) and b == 0 and c < 2):
                    sp.wait_ge(s_split, 4 * b + c - 1)
                sp.dma_start(raw[c % 2][:, :, 0:CM[c]],
                             ctx_t[b].rearrange("(k p) l -> p k l", p=P)[:, :, CO[c]:CO[c] + CM[c]]).then_inc(s_raw[c % 2], 16)

            def load_mask(sp, b, s):
                for j in range(2):
                    sp.dma_start(mk[s][j * N:(j + 1) * N, :], mask[b]).then_inc(s_mk[s], 16)

            def split(pool, b, c):
                n = 4 * b + c
                pool.wait_ge(s_raw[c % 2], 16 * (2 * b + c // 2 + 1))
                if not (isinstance(b, int) and b == 0):
                    pool.wait_ge(s_k, 8 * b - 3 + c)
                hold(pool)
                pool.tensor_copy(cx[c][:, 0], raw[c % 2][:, :, 0:CM[c]]).then_inc(s_hi, 1)
                pool.wait_ge(s_hi, n + 1)
                pool.tensor_tensor(cx[c][:, 1], raw[c % 2][:, :, 0:CM[c]], cx[c][:, 0].bitcast(F32),
                                   ALU.subtract).then_inc(s_split, 1)

            def spread(pool, b, s):
                if not (isinstance(b, int) and b < 2):
                    pool.wait_ge(s_sc, 4 * PAIRS * (b - 1))
                    hold(pool)
                q = qt_all[:, :, bass.ds(b * N, N)].unsqueeze(2).to_broadcast([P, NG, 4, N])
                pool.tensor_tensor(qm[:, :, :, :].rearrange("p (j a) h n -> p j (a h) n", j=NG), q,
                                   group[:, :].unsqueeze(1).unsqueeze(3).to_broadcast([P, NG, 4, N]), ALU.mult).then_inc(s_qm, 1)
                pool.wait_ge(s_qm, b + 1)
                hold(pool)
                pool.tensor_copy(qb[s][:, :, 0], qm[:, :, :, :]).then_inc(s_qh, 1)
                pool.wait_ge(s_qh, b + 1)
                pool.tensor_tensor(qb[s][:, :, 1], qm[:, :, :, :], qb[s][:, :, 0].bitcast(F32), ALU.subtract).then_inc(s_qb, 1)

            PARTS = [(0, 0), (0, 1), (1, 0)]

            def keys(pe, b, n, bank=bank_x):
                m, c = n // 4, n % 4
                if m == 0:
                    pe.wait_ge(s_split, 4 * b + c + 1)
                for k, (a, z, h) in enumerate((a, z, h) for a in range(KC) for z, h in PARTS):
                    mm = pe.matmul(bank[:, 0:CM[c]], w_kv[:, 0, h, a, m * P:(m + 1) * P], cx[c][:, z, a, :],
                                   start=(k == 0), stop=(k == 3 * KC - 1))
                mm.then_inc(s_k, 1)

            def values(pe, n):
                for h, lt in enumerate(range(2 * n, min(2 * n + 2, LT))):
                    rows = LAST if lt == LT - 1 else P
                    c = min(lt // CT, NC4 - 1)
                    at = lt * P - CO[c]
                    for k, (a, z, w) in enumerate((a, z, w) for a in range(KC) for z, w in PARTS):
                        o = C * (h + (n == 6))
                        mm = pe.matmul(bank_c[0:rows, o:o + C], cx[c][:, z, a, at:at + rows],
                                       w_kv[:, 1, w, a, :], start=(k == 0), stop=(k == 3 * KC - 1))
                mm.then_inc(s_v, 1)

            def keys_high(act, n, before, bank=bank_x):
                m, c = n // 4, n % 4
                act.wait_ge(s_k, before + 1)
                for z in range(2):
                    r = slice(z * G4, (z + 1) * G4)
                    ins = act.activation(kt[r, 2 * m + z, CO[c]:CO[c] + CM[c]], bank[r, 0:CM[c]], ACT.Identity,
                                         bias=bks[r, m:m + 1])
                ins.then_inc(s_khi, 1)

            def values_out(act, s, n, before):
                act.wait_ge(s_v, before + 1)
                if n == 6:
                    ins = act.activation(vt[s][0:LAST, LT - 1, :], bank_c[0:LAST, C:2 * C], ACT.Copy)
                else:
                    ins = act.activation(vt[s][:, 2 * n:2 * n + 2, :].rearrange("p t c -> p (t c)"), bank_c[:, :], ACT.Copy)
                ins.then_inc(s_vo, 1)

            def keys_low(dve, n, before, bank=bank_x):
                m, c = n // 4, n % 4
                dve.wait_ge(s_khi, before + 1)
                hold(dve)
                for z in range(2):
                    r, o = slice(z * G4, (z + 1) * G4), slice((1 - z) * G4, (2 - z) * G4)
                    cols = slice(CO[c], CO[c] + CM[c])
                    ins = dve.scalar_tensor_tensor(kt[o, 2 * m + z, cols], bank[r, 0:CM[c]], bks[r, m:m + 1],
                                                   kt[r, 2 * m + z, cols].bitcast(F32), ALU.add, ALU.subtract)
                ins.then_inc(s_klo, 1)

            with ExitStack() as first:
                xs = o_all
                w_in = sb(first, "w_in", [P, 2, KC, C])
                w_q = sb(first, "w_quant", [P, 2, KC, C])
                w_i = sb(first, "w_int", [P, 2, KC, C], BF16)
                w_amax = sb(first, "w_amax", [P, 2 * KC])
                w_s = sb(first, "w_scale", [P, 2 * KC])
                w_r = sb(first, "w_rscale", [P, 2 * KC])
                wq_qt = sb(first, "wq_qt", [P, KC, C], BF16)
                diag = sb(first, "diag", [P, KC, P])
                ones = sb(first, "ones", [P, P])
                bq_s = sb(first, "bq_s", [P, NG])
                bq4 = sb(first, "bq4", [P, NG])
                swq4 = sb(first, "swq4", [P, KC, 2])
                lanes = range(LANES)

                def lane_sb(name, shape, dt=F32):
                    return [sb(first, f"{name}{a}", shape, dt) for a in lanes]

                stats = lane_sb("q_stats", [P, 6])
                mv = lane_sb("q_mv", [P, 2])
                veps = lane_sb("q_var_eps", [P, 1])
                rstd = lane_sb("q_rstd", [P, 1])
                xn = lane_sb("q_xn", [P, C])
                sc = lane_sb("q_sc", [P, 4])
                xq = lane_sb("q_xq", [P, C])
                xi = lane_sb("q_xi", [P, C], BF16)
                xit = lane_sb("q_xit", [P, KC, P], BF16)
                qtok = lane_sb("q_tok", [P, NG, 2, G4])
                bank_q = [bank_s[0], bank_s[1], bank_s[2], bank_o]
                s_in, s_w, s_wdve = sem("in_loaded"), sem("w_in_loaded"), sem("w_dve")
                s_link = [sem(f"q_dve{a}") for a in lanes]
                LINKS = 7
                blk = first.enter_context(nc.Block())

                @blk.sync
                def _(sp):
                    sp.dma_start(w_in[:, 0], wq.rearrange("(a p) c -> p a c", p=P)).then_inc(s_w, 16)
                    sp.dma_start(w_in[:, 1], wo.rearrange("(a p) c -> p a c", p=P)).then_inc(s_w, 16)
                    sp.dma_start(ident_f[:, :], ident).then_inc(s_w, 16)
                    sp.dma_start(bq_s[:, :], bq).then_inc(s_w, 16)
                    sp.dma_start(xs[:, :, :], x.rearrange("(t p) c -> p t c", p=P)).then_inc(s_in, 16)
                    sp.dma_start(half[:, :], half_sel).then_inc(s_in, 16)
                    sp.dma_start(group[:, :], group_sel).then_inc(s_in, 16)
                    sp.dma_start(fold[:, :], fold_sel).then_inc(s_in, 16)
                    sp.dma_start(w_raw[:, 0], wk_t.rearrange("(k p) o -> p k o", p=P)).then_inc(s_wkv, 16)
                    sp.dma_start(w_raw[:, 1], wv_t.rearrange("(k p) o -> p k o", p=P)).then_inc(s_wkv, 16)
                    sp.dma_start(bks[:, :], bk).then_inc(s_wkv, 16)
                    for c in range(NC4):
                        load(sp, 0, c)
                    load_mask(sp, 0, 0)
                    load_mask(sp, 1, 1)
                    for c in range(2):
                        load(sp, 1, c)

                @blk.gpsimd
                def _(pool):
                    pool.memset(half_exp[:, :], -0.5).then_inc(ev("consts_set"), 1)
                    pool.memset(ones[:, :], 1.0).then_inc(ev("consts_set"), 1)
                    pool.wait_ge(ev("consts_set"), 2)
                    pool.wait_ge(s_wkv, 48)
                    pool.tensor_copy(w_kv[:, :, 0], w_raw[:, :]).then_inc(s_wsp, 1)
                    pool.wait_ge(s_wsp, 1)
                    pool.tensor_tensor(w_kv[:, :, 1], w_raw[:, :], w_kv[:, :, 0].bitcast(F32), ALU.subtract).then_inc(s_wsp, 1)
                    for r in range(TILES // LANES):
                        for a in lanes:
                            t = LANES * r + a
                            need(pool, "q_mv_ready", t)
                            pool.tensor_scalar(veps[a][:, :], mv[a][:, 1:2], LN_EPS, None, ALU.add).then_inc(ev("q_veps"), 1)
                            need(pool, "q_veps", t)
                            pool.tensor_tensor(rstd[a][:, :], veps[a][:, :], half_exp[:, 0:1], ALU.pow)\
                                .then_inc(ev("q_rstd_ready"), 1)
                        for c in range(2 * r, 2 * r + 2):
                            split(pool, 0, c)
                    need(pool, "q_set", TILES - 1)
                    spread(pool, 0, 0)

                @blk.vector
                def _(dve):
                    done = [0]

                    def link(ins):
                        done[0] += 1
                        ins.then_inc(s_wdve, 1)
                        dve.wait_ge(s_wdve, done[0])

                    dve.wait_ge(s_w, 64)
                    link(dve.tensor_copy(ident_b[:, :], ident_f[:, :]))
                    link(dve.tensor_reduce(w_amax[:, :], w_in[:, :, :, :].rearrange("p m a c -> p (m a) c"), AX.X, ALU.max,
                                           apply_absolute_value=True))
                    link(dve.tensor_scalar(w_s[:, :], w_amax[:, :], 1.0 / 127.0, Q_EPS, ALU.mult, ALU.max))
                    link(dve.reciprocal(w_r[:, :], w_s[:, :]))
                    for m in range(2):
                        for a in range(KC):
                            link(dve.tensor_scalar(w_q[:, m, a], w_in[:, m, a], w_r[:, KC * m + a:KC * m + a + 1], 127.0,
                                                   ALU.mult, ALU.min))
                    link(dve.tensor_scalar(w_q[:, :, :, :], w_q[:, :, :, :], -127.0, ROUND, ALU.max, ALU.add))
                    dve.tensor_scalar(w_i[:, :, :, :], w_q[:, :, :, :], -ROUND, None, ALU.add).then_inc(ev("w_int_ready"), 1)
                    for a in range(KC):
                        link(dve.tensor_scalar(diag[:, a], ident_f[:, :], w_s[:, KC + a:KC + a + 1], None, ALU.mult))
                    for d in range(2):
                        for r in range(2):
                            link(dve.tensor_scalar(swq4[d * G4:(d + 1) * G4, :, r], w_s[r * G4:(r + 1) * G4, 0:KC],
                                                   float(D) ** -0.5, None, ALU.mult))
                    dve.tensor_scalar(bq4[:, :], bq_s[:, :], float(D) ** -0.5, None, ALU.mult).then_inc(ev("diag_ready"), 1)
                    for m, dst in enumerate((wq_qt, wo_qt)):
                        dve.wait_ge(ev("w_turned"), m + 1)
                        dve.tensor_copy(dst[:, :, :].rearrange("p k o -> p (k o)"),
                                        bank_t[m][:, :].bitcast(BF16)[:, 0:KC * C]).then_inc(ev("w_copied"), 1)
                    dve.wait_ge(ev("swo_rows"), 1)
                    dve.tensor_copy(swo_b[:, :], bank_x[:, 0:C]).then_inc(ev("w_copied"), 1)

                    dve.wait_ge(s_in, 64)
                    with dve.Fori(0, TILES // LANES) as r:
                        n = [0]

                        def each(instruction, after=None, name=None):
                            for a in lanes:
                                if n[0]:
                                    dve.wait_ge(s_link[a], LINKS * r + n[0])
                                if after:
                                    need(dve, after, LANES * r + a)
                                hold(dve)
                                instruction(a).then_inc(ev(name) if name else s_link[a], 1)
                            if not name:
                                n[0] += 1

                        each(lambda a: dve.bn_stats(stats[a][:, :], xs[:, LANES * r + a, :]))
                        each(lambda a: dve.bn_aggr(mv[a][:, :], stats[a][:, :]), name="q_mv_ready")
                        each(lambda a: dve.tensor_scalar(xn[a][:, :], xs[:, LANES * r + a, :], mv[a][:, 0:1], rstd[a][:, :],
                                                         ALU.subtract, ALU.mult), after="q_rstd_ready")
                        each(lambda a: dve.tensor_reduce(sc[a][:, 0:1], xn[a][:, :], AX.X, ALU.max, apply_absolute_value=True))
                        each(lambda a: dve.tensor_scalar(sc[a][:, 1:2], sc[a][:, 0:1], 1.0 / 127.0, Q_EPS, ALU.mult, ALU.max))
                        each(lambda a: dve.reciprocal(sc[a][:, 2:3], sc[a][:, 1:2]))
                        each(lambda a: dve.tensor_scalar(xn[a][:, :], xn[a][:, :], sc[a][:, 2:3], 127.0, ALU.mult, ALU.min))
                        each(lambda a: dve.tensor_scalar(xq[a][:, :], xn[a][:, :], -127.0, ROUND, ALU.max, ALU.add))
                        each(lambda a: dve.tensor_scalar(xi[a][:, :], xq[a][:, :], -ROUND, None, ALU.add), name="q_int_ready")
                        each(lambda a: dve.tensor_scalar(qtok[a][:, :, :, :], bank_q[a][:, 0:C]
                                                         .rearrange("p (j c) -> p j c", j=NG).unsqueeze(2)
                                                         .to_broadcast([P, NG, 2, G4]), sc[a][:, 1:2], None, ALU.mult),
                             after="q_proj_done", name="q_tok_ready")
                        assert n[0] == LINKS, n[0]
                    for n in range(6):
                        keys_low(dve, n, n, (bank_x, bank_t[0])[n % 2])

                @blk.scalar
                def _(act):
                    with act.Fori(0, TILES // LANES) as r:
                        for a in lanes:
                            need(act, "q_int_turned", LANES * r + a)
                            act.activation(xit[a][:, :, :].rearrange("p k n -> p (k n)"),
                                           bank_q[a][:, :].bitcast(BF16)[:, 0:C], ACT.Copy).then_inc(ev("q_xit_ready"), 1)
                        for a in lanes:
                            t = LANES * r + a
                            need(act, "q_turned", t)
                            hold(act)
                            for j in range(NG):
                                ins = act.activation(qt_all[:, j, bass.ds(t * P, P)], bank_q[a][:, j * P:(j + 1) * P],
                                                     ACT.Identity, bias=bq4[:, j:j + 1], scale=swq4[:, j // 2, j % 2:j % 2 + 1])
                            ins.then_inc(ev("q_set"), 1)
                    act.wait_ge(s_wkv, 48)
                    for n in range(6):
                        keys_high(act, n, n, (bank_x, bank_t[0])[n % 2])
                        values_out(act, 0, n, n)

                @blk.tensor
                def _(pe):
                    pe.wait_ge(ev("w_int_ready"), 1)
                    for m in range(2):
                        tb = bank_t[m][:, :].bitcast(BF16)
                        for k in range(KC):
                            for a in range(KC):
                                mm = pe.transpose(tb[:, k * C + a * P:k * C + a * P + P], w_i[:, m, a, k * P:(k + 1) * P], ident_b[:, :])
                        mm.then_inc(ev("w_turned"), 1)
                    pe.wait_ge(ev("diag_ready"), 1)
                    pe.wait_ge(ev("consts_set"), 2)
                    pe.matmul(bank_x[:, 0:C], ones[:, :], diag[:, :, :].rearrange("p a o -> p (a o)"),
                              start=True, stop=True).then_inc(ev("swo_rows"), 1)
                    pe.wait_ge(ev("w_copied"), 3)
                    with pe.Fori(0, TILES // LANES) as r:
                        for a in lanes:
                            t = LANES * r + a
                            need(pe, "q_int_ready", t)
                            for k in range(KC):
                                mm = pe.transpose(bank_q[a][:, :].bitcast(BF16)[:, k * P:(k + 1) * P],
                                                  xi[a][:, k * P:(k + 1) * P], ident_b[:, :])
                            mm.then_inc(ev("q_int_turned"), 1)
                        for a in lanes:
                            need(pe, "q_xit_ready", LANES * r + a)
                            for k in range(KC):
                                mm = pe.matmul(bank_q[a][:, 0:C], xit[a][:, k, :], wq_qt[:, k, :],
                                               start=(k == 0), stop=(k == KC - 1))
                            mm.then_inc(ev("q_proj_done"), 1)
                        for a in lanes:
                            need(pe, "q_tok_ready", LANES * r + a)
                            for j in range(NG):
                                mm = pe.transpose(bank_q[a][:, j * P:(j + 1) * P],
                                                  qtok[a][:, j, :, :].rearrange("p r c -> p (r c)"), ident_f[:, :])
                            mm.then_inc(ev("q_turned"), 1)
                        need(pe, "q_set", LANES * r + LANES - 1)
                    pe.wait_ge(s_wsp, 2)
                    for n in range(6):
                        if n > 1:
                            pe.wait_ge(s_klo, n - 1)
                        keys(pe, 0, n, (bank_x, bank_t[0])[n % 2])
                        if n:
                            pe.wait_ge(s_vo, n)
                        values(pe, n)

            sm = [sb(ph, f"probs{s}", [P, L]) for s in range(2)]
            pt = [sb(ph, f"probs_t{n}", [P, LT, 2, P]) for n in range(2)]
            nmax = sb(ph, "neg_max_chunks", [P, 2, NC4])
            nmin = sb(ph, "neg_max", [P, 2])
            sums = [sb(ph, f"sums{s}", [P, PAIRS]) for s in range(2)]
            rsum = sb(ph, "rsum", [P, PAIRS])
            rtok = sb(ph, "rtok", [P, PAIRS, 2])
            ot4 = sb(ph, "ot4", [P, 2, 4, N])
            ot = sb(ph, "ot", [P, NG, P])
            blk = ph.enter_context(nc.Block())

            @blk.sync
            def _(sp):
                for c in range(2, NC4):
                    load(sp, 1, c)
                with sp.Fori(0, LASTI) as i:
                    for s in range(2):
                        for c in range(NC4):
                            load(sp, 2 * i + 2 + s, c)
                        sp.wait_ge(s_ttr, 4 * PAIRS * (2 * i + s + 1))
                        load_mask(sp, 2 * i + 2 + s, s)

            @blk.gpsimd
            def _(pool):
                def ahead(i):
                    for s in range(2):
                        for c in range(NC4):
                            split(pool, 2 * i + s + 1, c)
                        spread(pool, 2 * i + s + 1, 1 - s)

                ahead(0)
                with pool.Fori(1, LASTI) as i:
                    ahead(i)
                for c in range(NC4):
                    split(pool, 2 * LASTI + 1, c)
                spread(pool, 2 * LASTI + 1, 1)

            @blk.tensor
            def _(pe):
                def scores_of(i, u):
                    ii, uu = (i, u) if u < UNITS else (i + 1, u - UNITS)
                    s, p = uu // PAIRS, uu % PAIRS
                    b = 2 * ii + s
                    if p == 0:
                        pe.wait_ge(s_qb, b + 1)
                    if p % 4 == 0:
                        pe.wait_ge(s_klo, 8 * b + p + 4)

                    def chunk(c):
                        n = 4 * uu + c
                        if n >= 3:
                            pe.wait_ge(s_ttr, 64 * ii + n - 2)
                        elif not (isinstance(ii, int) and ii == 0):
                            pe.wait_ge(s_ttr, 64 * ii - {0: 0, 1: 2, 2: 1}[n])
                        for h in range(2):
                            mm = pe.matmul(bank_s[n % 3][:, 0:CM[c]], qb[s][:, p, h].rearrange("p h n -> p (h n)"),
                                           kt[:, p // 2, CO[c]:CO[c] + CM[c]], start=(h == 0), stop=(h == 1))
                        mm.then_inc(s_sc, 1)

                    return chunk

                def turn(i, u, groups):
                    if groups[0] == 0:
                        pe.wait_ge(s_exp, UNITS * i + u + 1)
                    for g in groups:
                        if g == 3:
                            pe.wait_ge(s_td, UNITS * i + u + 1)
                        elif not (isinstance(i, int) and i == 0 and u == 0 and g < 2):
                            pe.wait_ge(s_ta, 3 * (UNITS * i + u) + (-1, 0, 1)[g])
                        for q, lt in enumerate(range(4 * g, min(4 * g + 4, LT))):
                            rows = LAST if lt == LT - 1 else P
                            mm = pe.transpose(bank_t[g % 2][0:rows, q * P:(q + 1) * P], sm[u % 2][:, lt * P:lt * P + rows],
                                              ident_f[:, :])
                        mm.then_inc(s_t, 1)

                def pv(i, u):
                    s, g = u // PAIRS, (u % PAIRS) // 2
                    b = 2 * i + s
                    pe.wait_ge(s_ta, 3 * (UNITS * i + u + 1))
                    pe.wait_ge(s_td, UNITS * i + u + 1)
                    if g == 0:
                        pe.wait_ge(s_vo, 7 * b + 7)
                    if g % 2 == 0 and not (isinstance(i, int) and i == 0 and u == 1):
                        pe.wait_ge(s_of, 4 * i + u // 4)
                    for lt in range(LT):
                        rows = LAST if lt == LT - 1 else P
                        z = lt % 2
                        mm = pe.matmul(bank_o[z * G4:(z + 1) * G4, (g % 2) * C:(g % 2 + 1) * C],
                                       vt[s][0:rows, lt, g * G4:(g + 1) * G4],
                                       pt[(u // 2) % 2][0:rows, lt, :, :].rearrange("p j n -> p (j n)"),
                                       start=(lt < 2), stop=(lt >= LT - 2), skip_group_check=True)
                    mm.then_inc(s_pv, 1)

                def out_turn(i):
                    pe.wait_ge(s_fin, FINS * i + FINS - 1)
                    for g in range(NG):
                        mm = pe.matmul(bank_c[:, g * G4:(g + 1) * G4], ot[:, g, :], fold[:, :], start=True, stop=True)
                    mm.then_inc(ev("o_turned"), 1)

                def tile(i, last):
                    for u in range(UNITS):
                        s, v = u // PAIRS, u % PAIRS
                        b = 2 * i + s
                        project = v < 2 or not (last and s == 1)
                        turn(i, u, (0, 1))
                        if project:
                            pe.wait_ge(s_klo, 8 * b + 6 + v)
                            keys(pe, b if v < 2 else b + 1, k_item(v))
                        turn(i, u, (2, 3))
                        chunk = None if last and u + 2 >= UNITS else scores_of(i, u + 2)
                        for c in range(3):
                            if chunk:
                                chunk(c)
                        if project and v != 1:
                            pe.wait_ge(s_vo, 7 * b + (6 if v == 0 else 5 + v))
                            if u == 2 and not start(i, 0):
                                pe.wait_ge(s_fin, FINS * i)
                            values(pe, v_item(v))
                        if chunk:
                            chunk(3)
                        if u == 1 and not (isinstance(i, int) and i == 0):
                            pe.wait_ge(s_vo, 14 * i + 7)
                            out_turn(i - 1)
                        if u % 2 == 1:
                            pv(i, u)

                for u in range(2):
                    chunk = scores_of(0, u)
                    for c in range(NC4):
                        chunk(c)
                tile(0, False)
                with pe.Fori(1, LASTI) as i:
                    tile(i, False)
                tile(LASTI, True)
                out_turn(LASTI)

            @blk.scalar
            def _(act):
                def exp(i, u):
                    ii, uu = (i, u) if u < UNITS else (i + 1, u - UNITS)
                    s, p = uu // PAIRS, uu % PAIRS
                    act.wait_ge(s_nm, UNITS * ii + uu + 1)
                    if p == 0 and not (isinstance(ii, int) and ii == 0):
                        act.wait_ge(s_rs, 2 * ii + s - 1)
                    hold(act)
                    act.activation(sm[uu % 2][:, :], sm[uu % 2][:, :], ACT.Exp, bias=nmin[:, uu % 2:uu % 2 + 1], scale=-1.0,
                                   accum_out=sums[s][:, p:p + 1]).then_inc(s_exp, 1)

                def turned_out(i, u, g):
                    act.wait_ge(s_t, 4 * (UNITS * i + u) + g + 1)
                    if u % 2 == 0 and g == 0 and not (isinstance(i, int) and i == 0 and u < 4):
                        act.wait_ge(s_pv, 8 * i + u // 2 - 1)
                    rows, k = (LAST, 1) if g == 3 else (P, 4)
                    act.activation(pt[(u // 2) % 2][0:rows, 4 * g:4 * g + k, u % 2, :],
                                   bank_t[g % 2][0:rows, 0:k * P].rearrange("p (t n) -> p t n", t=k), ACT.Copy).then_inc(s_ta, 1)

                def tile(i, last):
                    for u in range(UNITS):
                        s, v = u // PAIRS, u % PAIRS
                        b = 2 * i + s
                        project = v < 2 or not (last and s == 1)
                        turned_out(i, u, 0)
                        if not (last and u + 1 >= UNITS):
                            exp(i, u + 1)
                        if project and v != 1:
                            keys_high(act, k_item(v), 8 * b + 6 + v)
                        turned_out(i, u, 2)
                        turned_out(i, u, 3)
                        if v == 1:
                            keys_high(act, k_item(v), 8 * b + 6 + v)
                        if project and v != 1:
                            values_out(act, s if v == 0 else 1 - s, v_item(v), 7 * b + (6 if v == 0 else 5 + v))

                exp(0, 0)
                tile(0, False)
                with act.Fori(1, LASTI) as i:
                    tile(i, False)
                tile(LASTI, True)

            @blk.vector
            def _(dve):
                def masked(i, u, chunks):
                    ii, uu = (i, u) if u < UNITS else (i + 1, u - UNITS)
                    s = uu // PAIRS
                    for c in chunks:
                        if c == 0:
                            if uu % PAIRS == 0:
                                dve.wait_ge(s_mk[s], 32 * (ii + 1))
                                hold(dve)
                            if not (isinstance(ii, int) and ii == 0 and uu < 2):
                                dve.wait_ge(s_t, 4 * (UNITS * ii + uu - 1))
                                hold(dve)
                        dve.wait_ge(s_sc, 64 * ii + 4 * uu + c + 1)
                        hold(dve)
                        dve.tensor_tensor_reduce(
                            out=sm[uu % 2][:, CO[c]:CO[c] + CH[c]], in0=bank_s[(4 * uu + c) % 3][:, 0:CH[c]],
                            in1=mk[s][:, CO[c]:CO[c] + CH[c]], scale=-1.0, scalar=BIG, op0=ALU.add, op1=ALU.min,
                            accum_out=nmax[:, uu % 2, c:c + 1]).then_inc(s_ttr, 1)
                        if c == NC4 - 1:
                            dve.wait_ge(s_ttr, 64 * ii + 4 * uu + 4)
                            dve.tensor_reduce(nmin[:, uu % 2:uu % 2 + 1], nmax[:, uu % 2, :], AX.X, ALU.min).then_inc(s_nm, 1)

                def turned_out(i, u):
                    dve.wait_ge(s_t, 4 * (UNITS * i + u) + 2)
                    if u % 2 == 0 and not (isinstance(i, int) and i == 0 and u < 4):
                        dve.wait_ge(s_pv, 8 * i + u // 2 - 1)
                    dve.tensor_copy(pt[(u // 2) % 2][:, 4:8, u % 2, :],
                                    bank_t[1][:, :].rearrange("p (t n) -> p t n", t=4)).then_inc(s_td, 1)

                def step(i, n, ins):
                    ins.then_inc(s_fin, 1)
                    dve.wait_ge(s_fin, FINS * i + n)
                    hold(dve)

                def half_out(i, h):
                    n = 4 * i + h + 1
                    dve.wait_ge(s_pv, 2 * n)
                    dve.tensor_tensor(ot4[:, :, :, :], bank_o[:, :].rearrange("p (m g n) -> p m g n", m=2, g=4),
                                      group[:, :].unsqueeze(1).unsqueeze(3).to_broadcast([P, 2, 4, N]),
                                      ALU.mult).then_inc(s_of, 1)
                    dve.wait_ge(s_of, n)
                    if h == 0 and not (isinstance(i, int) and i == 0):
                        need(dve, "o_turned", i - 1)
                    s = h // 2
                    step(i, (1, 2, 5, 6)[h],
                         dve.tensor_reduce(ot[:, 2 * (h % 2):2 * (h % 2) + 2, s * N:(s + 1) * N],
                                           ot4[:, :, :, :].rearrange("p m g n -> p m n g"), AX.X, ALU.add))

                def sums_out(i, s):
                    dve.wait_ge(s_exp, PAIRS * (2 * i + s + 1))
                    dve.reciprocal(rsum[:, :], sums[s][:, :]).then_inc(s_rs, 1)
                    dve.wait_ge(s_rs, 2 * i + s + 1)
                    for j in range(2):
                        step(i, 4 * s + 3 + j, dve.tensor_copy(rtok[s * N:(s + 1) * N, :, j], rsum[j * N:(j + 1) * N, :]))

                def tokens_out(i):
                    need(dve, "o_turned", i)
                    step(i, FINS, dve.tensor_tensor(o_all[:, bass.ds(i, 1), :].rearrange("p t (h d) -> p (t h) d", d=D),
                                                    bank_c[:, 0:C].rearrange("p (h d) -> p h d", d=D),
                                                    rtok[:, :, :].rearrange("p a j -> p (a j)").unsqueeze(2)
                                                    .to_broadcast([P, H, D]), ALU.mult))

                def tile(i, last):
                    for u in range(UNITS):
                        s, v = u // PAIRS, u % PAIRS
                        scored = not (last and u + 2 >= UNITS)
                        turned_out(i, u)
                        if u % 4 == 0 and not start(i, u):
                            half_out(*((i - 1, 3) if u == 0 else (i, u // 4 - 1)))
                        if v == 1 and not start(i, u - 1):
                            sums_out(*((i - 1, 1) if u == 1 else (i, 0)))
                        if scored:
                            masked(i, u + 2, range(2))
                        if v < 2 or not (last and s == 1):
                            keys_low(dve, k_item(v), 16 * i + 8 * s + 6 + v)
                        if scored:
                            masked(i, u + 2, range(2, NC4))
                        if u == 1 and not start(i, 0):
                            tokens_out(i - 1)

                masked(0, 0, range(NC4))
                masked(0, 1, range(NC4))
                tile(0, False)
                with dve.Fori(1, LASTI) as i:
                    tile(i, False)
                tile(LASTI, True)
                half_out(LASTI, 3)
                sums_out(LASTI, 1)
                tokens_out(LASTI)

        chain_and_experts(nc, ctx, sb, sem, ev, need, hold, bank_s, bank_t, bank_x, bank_c, bank_o, ident_f, ident_b,
                          o_all, half, half_exp, wo_qt, swo_b, x, bo_b, bv_b, w_qkvg, w_o, gnw_b, gnb_b, gate_t,
                          w_gu, w_dn, cos_t, sin_t, decay, tri, expand, out)


def chain_and_experts(nc, ctx, sb, sem, ev, need, hold, bank_s, bank_t, bank_x, bank_c, bank_o, ident_f, ident_b,
                      o_all, half, half_exp, wo_qt, swo_b, x, bo_b, bv_b, w_qkvg, w_o, gnw_b, gnb_b, gate_t,
                      w_gu, w_dn, cos_t, sin_t, decay, tri, expand, out):
    with ExitStack() as keep:
        x3h = sb(keep, "x3_high", [P, KC, TILES * P], F32R)
        x3l = sb(keep, "x3_low", [P, KC, TILES * P], F32R)
        comb = sb(keep, "comb", [3 * E + 1, TILES * P], BF16)
        wex = sb(keep, "expand", [3 * E + 1, JT, P], BF16)
        wgu = [sb(keep, f"wgu{n}", [P, 2, KC, P]) for n in range(2)]
        wdn = [sb(keep, f"wdn{n}", [P, C]) for n in range(2)]
        wgu_p = [sb(keep, f"wgu_parts{n}", [P, 2, 2, KC, P], F32R) for n in range(2)]
        wdn_p = [sb(keep, f"wdn_parts{n}", [P, 2, C], F32R) for n in range(2)]
        s_wex, s_wl = sem("expand_loaded"), [sem(f"expert_w{n}") for n in range(2)]
        s_guh, s_gu, s_dh, s_dp = sem("wgu_high"), sem("wgu_split"), sem("wdn_high"), sem("wdn_split")
        s_ud, s_dn = sem("up_mm"), sem("down_done")

        def load_weights(sp, j, b):
            if not (isinstance(j, int) and j < 2):
                sp.wait_ge(s_dp, j - 1)
            sp.dma_start(wgu[b][:, :, :, :], w_gu[j]).then_inc(s_wl[b], 16)
            sp.dma_start(wdn[b][:, :], w_dn[j]).then_inc(s_wl[b], 16)

        def split_weights(pool, j, b, r):
            later = not (isinstance(j, int) and j < 2)
            pool.wait_ge(s_wl[b], 32 * (r + 1))
            if later:
                pool.wait_ge(s_ud, 2 * (j - 1))
            hold(pool)
            pool.tensor_copy(wgu_p[b][:, 0], wgu[b][:, :, :, :]).then_inc(s_guh, 1)
            pool.wait_ge(s_guh, j + 1)
            pool.tensor_tensor(wgu_p[b][:, 1], wgu[b][:, :, :, :], wgu_p[b][:, 0].bitcast(F32), ALU.subtract).then_inc(s_gu, 1)
            if later:
                pool.wait_ge(s_dn, 2 * (j - 1))
                hold(pool)
            pool.tensor_copy(wdn_p[b][:, 0], wdn[b][:, :]).then_inc(s_dh, 1)
            pool.wait_ge(s_dh, j + 1)
            pool.tensor_tensor(wdn_p[b][:, 1], wdn[b][:, :], wdn_p[b][:, 0].bitcast(F32), ALU.subtract).then_inc(s_dp, 1)

        with ExitStack() as ph:
            lanes = range(TILES)

            def lane_sb(name, shape, dt=F32, n=TILES):
                return [sb(ph, f"{name}{a}", shape, dt) for a in range(n)]

            def flat(ap):
                return ap.rearrange("p h d -> p (h d)")

            def halves(ap):
                return ap.rearrange("p (k n) -> p k n", k=KC)

            def heads(ap):
                return ap.rearrange("p (h d) -> p h d", d=D)

            bo = sb(ph, "bo", [P, C])
            bv = sb(ph, "bv", [P, C])
            wr = sb(ph, "wr", [P, KC, 4 * C])
            wor = sb(ph, "wor", [P, KC, C])
            gnw = sb(ph, "gnw", [P, C])
            gnb = sb(ph, "gnb", [P, C])
            gw = sb(ph, "gw", [P, KC, E])
            cost = sb(ph, "cost", [P, 2, D])
            sint = sb(ph, "sint", [P, 2, D])
            dec = sb(ph, "dec", [P, H, N])
            lower = sb(ph, "lower", [P, E, E])
            oc = lane_sb("work", [P, C])
            xn = oc
            yc = [heads(b[:, :]) for b in oc]
            x_t = lane_sb("work_t", [P, C])
            oi = [b[:, 0:P].bitcast(BF16) for b in x_t]
            oqt = [halves(b[:, P:C].bitcast(BF16)) for b in x_t]
            xnt = [halves(b[:, :]) for b in x_t]
            xb = sb(ph, "xb_ret_v", [P, TILES, C])
            rv = [xb[:, a, :] for a in lanes]
            ra = lane_sb("rotated", [P, 2 * H, D])
            rb = lane_sb("rot_sin", [P, 2 * H, D])
            ysq = [b[:, 0:H, :] for b in ra]
            rank = [flat(b[:, :, :]).rearrange("p (c e f) -> p c e f", c=2, e=E) for b in ra]
            oq = [flat(b[:, 0:H, :]) for b in rb]
            gb = [flat(b[:, H:2 * H, :]) for b in rb]
            rqt = lane_sb("ret_q_t", [P, KC, P])
            rkt = lane_sb("ret_k_t", [P, KC, P])
            ht, x3s = rqt, rkt
            rqb = lane_sb("ret_q_blocks", [P, KC, 2, HH, N], n=2)
            ret = lane_sb("ret_scores", [P, KC, HH * N], n=2)
            gs = lane_sb("gate", [P, C])
            sc = lane_sb("o_scales", [P, 4])
            stats = lane_sb("ln_stats", [P, 6])
            mv = lane_sb("ln_mean_var", [P, 2])
            rstd = lane_sb("ln_rstd", [P, 2])
            gst = lane_sb("gn_stats", [P, 4, H])
            rt = lane_sb("route_row", [P, 8])
            es = lane_sb("route_exp", [P, E])
            ps = lane_sb("route_probs", [P, E])
            rk = lane_sb("ranks", [P, 2, E])
            cw = lane_sb("combine", [P, E])
            cr = lane_sb("combine_rest", [P, 2, E])
            c3 = lane_sb("combine_parts", [P, 3 * E], BF16)
            bank_a = [bank_t[0], bank_t[1], bank_x, bank_c, bank_s[0], bank_s[1], bank_s[2], bank_o]
            s_bv, s_xb, s_ld = sem("bv_loaded"), sem("xb_loaded"), sem("chain_loaded")
            s_step = [sem(f"chain_dve{a}") for a in lanes]
            LINKS = 36
            blk = ph.enter_context(nc.Block())

            @blk.sync
            def _(sp):
                sp.dma_start(bv[:, :], bv_b).then_inc(s_bv, 16)
                sp.dma_start(bo[:, :], bo_b).then_inc(s_xb, 16)
                sp.dma_start(xb[:, :, :], x.rearrange("(t p) c -> p t c", p=P)).then_inc(s_xb, 16)
                for dst, src in ((gnw, gnw_b), (gnb, gnb_b)):
                    sp.dma_start(dst[:, :], src).then_inc(s_ld, 16)
                for dst, src in ((wr, w_qkvg), (wor, w_o), (gw, gate_t)):
                    sp.dma_start(dst[:, :, :], src.rearrange("(k p) n -> p k n", p=P)).then_inc(s_ld, 16)
                for dst, src in ((cost, cos_t), (sint, sin_t), (dec, decay), (lower, tri)):
                    sp.dma_start(dst[:, :, :], src).then_inc(s_ld, 16)
                sp.dma_start(wex[:, :, :], expand.bitcast(BF16)).then_inc(s_wex, 16)
                for j in range(2):
                    load_weights(sp, j, j)

            def spread_heads(e, a, m, s):
                q = rqt[a][:, m, s * N:(s + 1) * N].unsqueeze(1).to_broadcast([P, HH, N])
                return e.tensor_tensor(rqb[a % 2][:, m, s], q, half[:, :].unsqueeze(2).to_broadcast([P, HH, N]), ALU.mult)

            @blk.gpsimd
            def _(pool):
                def root(name, on, dst, src, eps):
                    for a in on:
                        need(pool, name, a)
                        hold(pool)
                        pool.tensor_scalar(src(a), src(a), eps, None, ALU.add).then_inc(ev(name + "_eps"), 1)
                        need(pool, name + "_eps", a)
                        pool.tensor_tensor(dst(a), src(a), half_exp[:, 0:dst(a).shape[1]], ALU.pow)\
                            .then_inc(ev(name + "_root"), 1)

                pool.wait_ge(s_xb, 32)
                pool.tensor_tensor(xb[:, :, :], xb[:, :, :], bo[:, :].unsqueeze(1).to_broadcast([P, TILES, C]),
                                   ALU.add).then_inc(ev("xb_ready"), 1)
                pool.wait_ge(s_ld, 16 * 9)
                root("ln2", lanes, lambda a: rstd[a][:, 0:1], lambda a: mv[a][:, 1:2], LN_EPS)
                def gate_terms(a):
                    need(pool, "gate_ready", a)
                    pool.tensor_tensor(gb[a][:, :], gs[a][:, :], gnb[:, :], ALU.mult)
                    pool.tensor_tensor(gs[a][:, :], gs[a][:, :], gnw[:, :], ALU.mult).then_inc(ev("gate_wb"), 1)

                def spread_lane(a):
                    need(pool, "rq_ready", a)
                    if a >= 2:
                        need(pool, "ret_done1", a - 2)
                    spread_heads(pool, a, 0, 0).then_inc(ev("rqb_pool_ready"), 1)

                spread_lane(0)
                spread_lane(1)
                for a in lanes:
                    gate_terms(a)
                for k in range(1, TILES + 2):
                    if k + 1 < TILES:
                        spread_lane(k + 1)
                    if k >= 2:
                        root("gn", [k - 2], lambda a: gst[a][:, 2, :], lambda a: gst[a][:, 1, :], GN_EPS)
                root("ln3", lanes, lambda a: rstd[a][:, 1:2], lambda a: mv[a][:, 1:2], LN_EPS)
                for a in lanes:
                    t = a
                    need(pool, "x3h_ready", t)
                    hold(pool)
                    high = x3h[:, :, bass.ds(t * P, P)]
                    pool.tensor_tensor(x3l[:, :, bass.ds(t * P, P)], x3s[a][:, :, :], high.bitcast(F32),
                                       ALU.subtract).then_inc(ev("x3l_ready"), 1)
                for a in lanes:
                    need(pool, "equal_ready", a)
                    pool.tensor_tensor(rank[a][:, 1], rank[a][:, 1], lower[:, :, :], ALU.mult).then_inc(ev("ties_ready"), 1)
                for j in range(2):
                    split_weights(pool, j, j, 0)

            @blk.vector
            def _(dve):
                dve.memset(comb[32:3 * E + 1, :], 1.0).then_inc(ev("comb_ones"), 1)
                dve.wait_ge(ev("comb_ones"), 1)
                dve.wait_ge(s_bv, 16)
                n = [0] * TILES

                def each(instruction, after=None, name=None, on=lanes):
                    for a in on:
                        if n[a]:
                            dve.wait_ge(s_step[a], n[a])
                        if after:
                            need(dve, after, a)
                        instruction(a).then_inc(ev(name) if name else s_step[a], 1)
                        if not name:
                            n[a] += 1

                def by_head(ap):
                    return ap.unsqueeze(2).to_broadcast([P, H, D])

                each(lambda a: dve.tensor_tensor(oc[a][:, :], o_all[:, a, :], bv[:, :], ALU.add))
                each(lambda a: dve.tensor_reduce(sc[a][:, 0:1], oc[a][:, :], AX.X, ALU.max, apply_absolute_value=True))
                each(lambda a: dve.tensor_scalar(sc[a][:, 1:2], sc[a][:, 0:1], 1.0 / 127.0, Q_EPS, ALU.mult, ALU.max))
                each(lambda a: dve.reciprocal(sc[a][:, 2:3], sc[a][:, 1:2]))
                each(lambda a: dve.tensor_scalar(oc[a][:, :], oc[a][:, :], sc[a][:, 2:3], 127.0, ALU.mult, ALU.min))
                each(lambda a: dve.tensor_scalar(oq[a][:, :], oc[a][:, :], -127.0, ROUND, ALU.max, ALU.add))
                each(lambda a: dve.tensor_scalar(oi[a][:, :], oq[a][:, :], -ROUND, None, ALU.add), name="oi_ready")
                each(lambda a: dve.scalar_tensor_tensor(oq[a][:, :], bank_a[a][:, 0:C], sc[a][:, 1:2], swo_b[:, :],
                                                        ALU.mult, ALU.mult), after="y_done")
                dve.wait_ge(ev("xb_ready"), 1)
                each(lambda a: dve.tensor_tensor(o_all[:, a, :], oq[a][:, :], xb[:, a, :], ALU.add))

                def norm(src, name, col, done):
                    each(lambda a: dve.bn_stats(stats[a][:, :], src(a)))
                    each(lambda a: dve.bn_aggr(mv[a][:, :], stats[a][:, :]), name=name)
                    each(lambda a: dve.tensor_scalar(xn[a][:, :], src(a), mv[a][:, 0:1], rstd[a][:, col:col + 1],
                                                     ALU.subtract, ALU.mult), after=name + "_root", name=done)

                norm(lambda a: o_all[:, a, :], "ln2", 0, "xn2_ready")

                dve.wait_ge(s_ld, 16 * 9)

                def qk(a):
                    return bank_a[a][:, :].rearrange("p (a h d) -> p a h d", a=2, d=D)

                def sin_part(a, z):
                    zs, zo = slice(8 * z, 8 * z + 8), slice(8 - 8 * z, 16 - 8 * z)
                    return dve.tensor_tensor(rb[a][:, :, zs].rearrange("p (a h) d -> p a h d", a=2), qk(a)[:, :, :, zo],
                                             sint[:, :, zs].unsqueeze(2).to_broadcast([P, 2, H, D // 2]), ALU.mult)

                for one in range(0, TILES, 2):
                    on = [one, one + 1]
                    each(lambda a: dve.tensor_tensor(ra[a][:, :, :].rearrange("p (a h) d -> p a h d", a=2), qk(a),
                                                     cost[:, :, :].unsqueeze(2).to_broadcast([P, 2, H, D]), ALU.mult),
                         after="qk_done", on=on)
                    each(lambda a: sin_part(a, 0), on=on)
                    each(lambda a: sin_part(a, 1), on=on)
                    each(lambda a: dve.tensor_tensor(ra[a][:, :, :], ra[a][:, :, :], rb[a][:, :, :], ALU.add),
                         name="qk_rot", on=on)

                def decayed(a, m):
                    each(lambda a: dve.tensor_tensor(ret[a % 2][:, m, :], bank_a[a][:, :], flat(dec[:, m * HH:(m + 1) * HH, :]),
                                                     ALU.mult), after=f"ret_done{m}", name=f"ret_ready{m}", on=[a])

                def head_stats(a):
                    on = [a]
                    each(lambda a: dve.tensor_reduce(gst[a][:, 0, :], heads(bank_a[a][:, 0:C]), AX.X, ALU.add),
                         after="yr_done", on=on)
                    each(lambda a: dve.tensor_scalar(gst[a][:, 0, :], gst[a][:, 0, :], 1.0 / D, None, ALU.mult), on=on)
                    each(lambda a: dve.tensor_tensor(yc[a][:, :, :], heads(bank_a[a][:, 0:C]), by_head(gst[a][:, 0, :]),
                                                     ALU.subtract), on=on)
                    each(lambda a: dve.tensor_tensor(ysq[a][:, :, :], yc[a][:, :, :], yc[a][:, :, :], ALU.mult), on=on)
                    each(lambda a: dve.tensor_reduce(gst[a][:, 3, :], ysq[a][:, :, :], AX.X, ALU.add), on=on)
                    each(lambda a: dve.tensor_scalar(gst[a][:, 1, :], gst[a][:, 3, :], 1.0 / D, None, ALU.mult),
                         name="gn", on=on)

                def spread_lane(a):
                    need(dve, "rq_ready", a)
                    if a >= 2:
                        need(dve, "ret_done1", a - 2)
                    for m, s in ((0, 1), (1, 0), (1, 1)):
                        tt = spread_heads(dve, a, m, s)
                    tt.then_inc(ev("rqb_ready"), 1)

                spread_lane(0)
                for k in range(TILES + 2):
                    if 0 <= k - 1 < TILES:
                        decayed(k - 1, 1)
                    if k < TILES:
                        decayed(k, 0)
                    if k + 1 < TILES:
                        spread_lane(k + 1)
                    if k >= 2:
                        head_stats(k - 2)
                each(lambda a: dve.tensor_tensor(yc[a][:, :, :], yc[a][:, :, :], by_head(gst[a][:, 2, :]), ALU.mult),
                     after="gn_root")
                each(lambda a: dve.tensor_tensor(flat(yc[a][:, :, :]), flat(yc[a][:, :, :]), gs[a][:, :], ALU.mult),
                     after="gate_wb")
                each(lambda a: dve.tensor_tensor(flat(yc[a][:, :, :]), flat(yc[a][:, :, :]), gb[a][:, :], ALU.add),
                     name="h_ready")
                each(lambda a: dve.tensor_tensor(o_all[:, a, :], o_all[:, a, :], bank_a[a][:, 0:C], ALU.add),
                     after="wo_done")
                norm(lambda a: o_all[:, a, :], "ln3", 1, "xn3_ready")
                each(lambda a: dve.tensor_reduce(rt[a][:, 0:1], bank_a[a][:, 0:E], AX.X, ALU.max, negate=True),
                     after="logits_done", name="rt_max")
                each(lambda a: dve.reciprocal(rt[a][:, 2:3], rt[a][:, 1:2]), after="rt_exp")
                each(lambda a: dve.tensor_scalar(ps[a][:, :], es[a][:, :], rt[a][:, 2:3], None, ALU.mult))

                def rivals(a):
                    return ps[a][:, :].unsqueeze(1).to_broadcast([P, E, E]), ps[a][:, :].unsqueeze(2).to_broadcast([P, E, E])

                each(lambda a: dve.tensor_tensor(rank[a][:, 1], *rivals(a), ALU.is_equal), name="equal_ready")
                each(lambda a: dve.tensor_tensor(rank[a][:, 0], *rivals(a), ALU.is_gt))
                each(lambda a: dve.tensor_reduce(rk[a][:, :, :], rank[a][:, :, :, :], AX.X, ALU.add), after="ties_ready")
                each(lambda a: dve.tensor_tensor(cw[a][:, :], rk[a][:, 0], rk[a][:, 1], ALU.add))
                each(lambda a: dve.tensor_scalar(cw[a][:, :], cw[a][:, :], TOPK - 0.5, None, ALU.is_lt))
                each(lambda a: dve.tensor_tensor(cw[a][:, :], cw[a][:, :], ps[a][:, :], ALU.mult))
                each(lambda a: dve.tensor_reduce(rt[a][:, 3:4], cw[a][:, :], AX.X, ALU.add))
                each(lambda a: dve.reciprocal(rt[a][:, 4:5], rt[a][:, 3:4]))
                each(lambda a: dve.tensor_scalar(cw[a][:, :], cw[a][:, :], rt[a][:, 4:5], None, ALU.mult))
                each(lambda a: dve.tensor_copy(c3[a][:, 0:E], cw[a][:, :]))
                each(lambda a: dve.tensor_tensor(cr[a][:, 0], cw[a][:, :], c3[a][:, 0:E], ALU.subtract))
                each(lambda a: dve.tensor_copy(c3[a][:, E:2 * E], cr[a][:, 0]))
                each(lambda a: dve.tensor_tensor(cr[a][:, 1], cr[a][:, 0], c3[a][:, E:2 * E], ALU.subtract))
                each(lambda a: dve.tensor_copy(c3[a][:, 2 * E:3 * E], cr[a][:, 1]), name="c3_ready")
                each(lambda a: dve.tensor_copy(comb[0:3 * E, bass.ds((a) * P, P)],
                                               bank_a[a][:, :].bitcast(BF16)[0:3 * E, 0:P]), after="c3_turned")
                assert n == [LINKS] * TILES

            @blk.scalar
            def _(act):
                def each(after, dst, src, func, done, on=lanes):
                    for a in on:
                        need(act, after, a)
                        act.activation(dst(a), src(a), func).then_inc(ev(done), 1)

                each("oi_turned", lambda a: flat(oqt[a][:, :, :]), lambda a: bank_a[a][:, :].bitcast(BF16)[:, 0:C], ACT.Copy, "oqt_ready")
                each("xn2_turned", lambda a: flat(xnt[a][:, :, :]), lambda a: bank_a[a][:, 0:C], ACT.Copy, "xnt_ready")
                for k in range(TILES + 1):
                    if k < TILES:
                        each("qk_turned", lambda a: flat(rqt[a][:, :, :]), lambda a: bank_a[a][:, 0:C], ACT.Copy, "rq_ready", [k])
                        each("qk_turned", lambda a: flat(rkt[a][:, :, :]), lambda a: bank_a[a][:, C:2 * C], ACT.Copy, "rk_ready", [k])
                    if k:
                        each("vg_done", lambda a: rv[a][:, :], lambda a: bank_a[a][:, 0:C], ACT.Copy, "rv_ready", [k - 1])
                        each("vg_done", lambda a: gs[a][:, :], lambda a: bank_a[a][:, C:2 * C], ACT.Silu, "gate_ready", [k - 1])
                each("h_turned", lambda a: flat(ht[a][:, :, :]), lambda a: bank_a[a][:, 0:C], ACT.Copy, "ht_ready")
                each("xn3_turned", lambda a: flat(x3s[a][:, :, :]), lambda a: bank_a[a][:, 0:C], ACT.Copy, "x3s_ready")
                for a in lanes:
                    need(act, "x3s_ready", a)
                    act.activation(x3h[:, :, bass.ds((a) * P, P)], x3s[a][:, :, :],
                                   ACT.Copy).then_inc(ev("x3h_ready"), 1)
                for a in lanes:
                    need(act, "rt_max", a)
                    act.activation(es[a][:, :], bank_a[a][:, 0:E], ACT.Exp, bias=rt[a][:, 0:1],
                                   accum_out=rt[a][:, 1:2]).then_inc(ev("rt_exp"), 1)

            @blk.tensor
            def _(pe):
                def turn(after, src, ident, bank, done):
                    for a in lanes:
                        need(pe, after, a)
                        for k in range(KC):
                            mm = pe.transpose(bank(a)[:, k * P:(k + 1) * P], src(a)[:, k * P:(k + 1) * P], ident)
                        mm.then_inc(ev(done), 1)

                def project(after, dst, lhs, rhs, done, on=lanes):
                    for a in on:
                        need(pe, after, a)
                        for k in range(KC):
                            mm = pe.matmul(dst(a), lhs[a][:, k, :], rhs(k), start=(k == 0), stop=(k == KC - 1))
                        mm.then_inc(ev(done), 1)

                turn("oi_ready", lambda a: oi[a], ident_b[:, :], lambda a: bank_a[a][:, :].bitcast(BF16), "oi_turned")
                project("oqt_ready", lambda a: bank_a[a][:, 0:C], oqt, lambda k: wo_qt[:, k, :], "y_done")
                turn("xn2_ready", lambda a: xn[a], ident_f[:, :], lambda a: bank_a[a], "xn2_turned")
                project("xnt_ready", lambda a: bank_a[a][:, :], xnt, lambda k: wr[:, k, 0:2 * C], "qk_done")
                for k in range(TILES + 1):
                    if k < TILES:
                        need(pe, "qk_rot", k)
                        rot = flat(ra[k][:, :, :])
                        for c in range(2 * KC):
                            mm = pe.transpose(bank_a[k][:, c * P:(c + 1) * P], rot[:, c * P:(c + 1) * P], ident_f[:, :])
                        mm.then_inc(ev("qk_turned"), 1)
                    if k:
                        project("rk_ready", lambda a: bank_a[a][:, :], xnt, lambda c: wr[:, c, 2 * C:4 * C], "vg_done", [k - 1])

                def ret_scores(a, m):
                    if m == 0:
                        need(pe, "rqb_pool_ready", a)
                        need(pe, "rqb_ready", a)
                        need(pe, "gate_ready", a)
                    else:
                        need(pe, "ret_ready0", a)
                    for s in range(2):
                        mm = pe.matmul(bank_a[a][s * N:(s + 1) * N, :], rkt[a][:, m, s * N:(s + 1) * N],
                                       flat(rqb[a % 2][:, m, s]), start=True, stop=True)
                    mm.then_inc(ev(f"ret_done{m}"), 1)

                def ret_values(a):
                    need(pe, "ret_ready1", a)
                    need(pe, "rv_ready", a)
                    for s in range(2):
                        for h in range(H):
                            mm = pe.matmul(bank_a[a][s * N:(s + 1) * N, h * D:(h + 1) * D],
                                           ret[a % 2][s * N:(s + 1) * N, h // HH, (h % HH) * N:(h % HH + 1) * N],
                                           rv[a][s * N:(s + 1) * N, h * D:(h + 1) * D], start=True, stop=True)
                    mm.then_inc(ev("yr_done"), 1)

                for k in range(TILES + 1):
                    if k < TILES:
                        ret_scores(k, 0)
                    if k:
                        ret_values(k - 1)
                    if k < TILES:
                        ret_scores(k, 1)
                turn("h_ready", lambda a: yc[a][:, :, :].rearrange("p h d -> p (h d)"), ident_f[:, :],
                     lambda a: bank_a[a], "h_turned")
                project("ht_ready", lambda a: bank_a[a][:, 0:C], ht, lambda k: wor[:, k, :], "wo_done")
                turn("xn3_ready", lambda a: xn[a], ident_f[:, :], lambda a: bank_a[a], "xn3_turned")
                project("x3s_ready", lambda a: bank_a[a][:, 0:E], x3s, lambda k: gw[:, k, :], "logits_done")
                for a in lanes:
                    need(pe, "c3_ready", a)
                    hold(pe)
                    pe.transpose(bank_a[a][:, :].bitcast(BF16)[0:3 * E, 0:P], c3[a][:, :],
                                 ident_b[:, :]).then_inc(ev("c3_turned"), 1)

        with ExitStack() as ph:
            sg = [sb(ph, f"silu{n}", [P, 512]) for n in range(2)]
            su = [sb(ph, f"gated{n}", [P, 512]) for n in range(2)]
            aw = [sb(ph, f"acts{n}", [P, 512]) for n in range(2)]
            ah = [sb(ph, f"acts_high{n}", [P, 512], F32R) for n in range(2)]
            al = [sb(ph, f"acts_low{n}", [P, 512], F32R) for n in range(2)]
            yout = sb(ph, "yout", [P, TILES, C])
            bank_y = [bank_s[0], bank_s[1], bank_s[2], bank_o]
            bank_g, bank_u, bank_w = bank_t[0], bank_t[1], bank_x
            s_gd, s_cd = sem("gate_mm"), sem("weight_mm")
            s_sg, s_su, s_aw, s_ah, s_al = (sem(n) for n in ("silu_done", "gated_done", "acts_done", "acts_high_done", "acts_low_done"))
            s_yo, s_out = sem("y_added"), sem("out_stored")
            NB = TILES * P // 512
            blk = ph.enter_context(nc.Block())

            def tiles_loop(e, body):
                body(0, 0, 0)
                body(1, 1, 0)
                body(2, 0, 1)
                with e.Fori(1, (JT - 1) // 2) as r:
                    body(2 * r + 1, 1, r)
                    body(2 * r + 2, 0, r + 1)

            @blk.sync
            def _(sp):
                def body(j, b, r):
                    if not (isinstance(j, int) and j < 2):
                        load_weights(sp, j, b)

                tiles_loop(sp, body)
                for q in range(2):
                    sp.wait_ge(s_yo, 2 * (q + 1))
                    sp.dma_start(out.rearrange("(t p) c -> p t c", p=P)[:, 4 * q:4 * q + 4, :],
                                 yout[:, 4 * q:4 * q + 4, :]).then_inc(s_out, 16)
                sp.wait_ge(s_out, 32)

            @blk.gpsimd
            def _(pool):
                def body(j, b, r):
                    if not (isinstance(j, int) and j < 2):
                        split_weights(pool, j, b, r)

                tiles_loop(pool, body)

            @blk.tensor
            def _(pe):
                def down(jn, b, n, j, first):
                    pe.wait_ge(s_al, jn + 1)
                    if n == 0:
                        pe.wait_ge(s_dp, j + 1)
                    for q in range(4):
                        tt = 4 * n + q
                        cols = slice(q * P, (q + 1) * P)
                        for k, (acts, w) in enumerate(((ah, 0), (ah, 1), (al, 0))):
                            mm = pe.matmul(bank_y[tt // 2][:, (tt % 2) * C:(tt % 2 + 1) * C], acts[n][:, cols],
                                           wdn_p[b][:, w, :], start=(first and tt % 2 == 0 and k == 0), stop=False,
                                           skip_group_check=True)
                    mm.then_inc(s_dn, 1)

                def body(j, b, r):
                    first = isinstance(j, int) and j == 0
                    pe.wait_ge(s_gu, j + 1)
                    for n in range(NB):
                        jn = NB * j + n
                        cols = slice(n * 512, (n + 1) * 512)
                        for g, (bank, free, done) in enumerate(((bank_g, s_sg, s_gd), (bank_u, s_su, s_ud))):
                            if not (first and n == 0):
                                pe.wait_ge(free, jn)
                            for k, (a, x3, w) in enumerate((a, x3, w) for a in range(KC)
                                                           for x3, w in ((x3h, 0), (x3h, 1), (x3l, 0))):
                                mm = pe.matmul(bank[:, :], wgu_p[b][:, w, g, a, :], x3[:, a, cols],
                                               start=(k == 0), stop=(k == 3 * KC - 1))
                            mm.then_inc(done, 1)
                        if not (first and n == 0):
                            pe.wait_ge(s_aw, jn)
                            hold(pe)
                        pe.matmul(bank_w[:, :], wex[:, j, :], comb[:, cols], start=True, stop=True).then_inc(s_cd, 1)
                        if n == 1:
                            down(jn - 1, b, 0, j, first)
                        elif not first:
                            down(jn - 1, 1 - b, 1, j - 1, isinstance(j, int) and j == 1)

                pe.wait_ge(s_wex, 16)
                tiles_loop(pe, body)
                down(NB * JT - 1, (JT - 1) % 2, 1, JT - 1, False)

            @blk.scalar
            def _(act):
                def body(j, b, r):
                    for n in range(NB):
                        jn = NB * j + n
                        later = not (isinstance(j, int) and j == 0)
                        act.wait_ge(s_gd, jn + 1)
                        if later:
                            act.wait_ge(s_su, jn - 1)
                        act.activation(sg[n][:, :], bank_g[:, :], ACT.Silu).then_inc(s_sg, 1)
                        act.wait_ge(s_aw, jn + 1)
                        if later:
                            act.wait_ge(s_dn, jn - 1)
                        act.activation(ah[n][:, :], aw[n][:, :], ACT.Copy).then_inc(s_ah, 1)

                tiles_loop(act, body)

            @blk.vector
            def _(dve):
                def body(j, b, r):
                    for n in range(NB):
                        jn = NB * j + n
                        dve.wait_ge(s_sg, jn + 1)
                        dve.wait_ge(s_ud, jn + 1)
                        dve.tensor_tensor(su[n][:, :], sg[n][:, :], bank_u[:, :], ALU.mult).then_inc(s_su, 1)
                        dve.wait_ge(s_su, jn + 1)
                        dve.wait_ge(s_cd, jn + 1)
                        dve.tensor_tensor(aw[n][:, :], su[n][:, :], bank_w[:, :], ALU.mult).then_inc(s_aw, 1)
                        dve.wait_ge(s_aw, jn + 1)
                        dve.wait_ge(s_ah, jn + 1)
                        dve.tensor_tensor(al[n][:, :], aw[n][:, :], ah[n][:, :].bitcast(F32), ALU.subtract).then_inc(s_al, 1)

                tiles_loop(dve, body)
                dve.wait_ge(s_dn, NB * JT)
                for q in range(4):
                    dve.tensor_tensor(yout[:, 2 * q:2 * q + 2, :].rearrange("p t c -> p (t c)"),
                                      o_all[:, 2 * q:2 * q + 2, :].rearrange("p t c -> p (t c)"), bank_y[q][:, :],
                                      ALU.add).then_inc(s_yo, 1)


def shape_tables():
    import numpy as np

    p = np.arange(P)
    f = np.float32
    ident = np.eye(P, dtype=f)
    half = (p[:, None] // D == np.arange(HH)[None]).astype(f)
    fold = (p[:, None] % G4 == np.arange(G4)[None]).astype(f)
    group = (p[:, None] // D % 4 == np.arange(4)[None]).astype(f)
    pos = (p % N).astype(f)
    hd = D // 2
    xscale = (np.arange(0, D, 2, dtype=f) + f(0.4 * D)) / f(1.4 * D)
    scale = xscale[None, :] ** (pos[:, None] / f(64))
    inv_freq = f(1.0) / f(10000.0) ** (np.arange(hd, dtype=f) / f(hd))
    sinu = pos[:, None] * inv_freq[None, :]
    cos_t = np.zeros((P, 2, D), f)
    sin_t = np.zeros((P, 2, D), f)
    for a, sc in enumerate((scale, f(1.0) / scale)):
        cos_t[:, a, :hd] = cos_t[:, a, hd:] = np.cos(sinu) * sc
        sin_t[:, a, :hd] = -np.sin(sinu) * sc
        sin_t[:, a, hd:] = np.sin(sinu) * sc
    gammas = 1.0 - np.exp(np.linspace(np.log(1.0 / 32), np.log(1.0 / 64), H)).astype(f)
    gammas = gammas.astype(f)
    m = (p % N)[:, None, None]
    n = np.arange(N)[None, None, :]
    decay = np.where(n >= m, gammas[None, :, None] ** np.maximum(n - m, 0).astype(f), 0.0).astype(f)
    tri = np.broadcast_to((np.arange(E)[None, :] < np.arange(E)[:, None]).astype(f), (P, E, E))
    rows = np.arange(JT * P)
    expand = np.zeros((3 * E + 1, JT * P), f)
    for part in range(3):
        for e in range(E):
            expand[part * E + e] = rows // I == e
    expand[3 * E] = rows >= E * I
    expand = expand.reshape(3 * E + 1, JT, P).astype(np.uint16) * np.uint16(0x3F80)
    return dict(ident=ident, half_sel=half, group_sel=group, fold_sel=fold, cos_t=cos_t, sin_t=sin_t, decay=decay,
                tri=np.ascontiguousarray(tri), expand=expand)


def kernel(**inputs):
    import numpy as np
    import concourse.bacc as bacc
    from concourse import mybir as _mybir
    from concourse.bass_utils import run_bass_kernel_spmd as run

    g = {k: np.asarray(v) for k, v in inputs.items()}
    row = lambda a: np.ascontiguousarray(np.broadcast_to(a[None, :], (P, a.shape[0])))

    def heads(w, evens_first):
        w = w.transpose(1, 0, 2)
        if evens_first:
            w = np.concatenate([w[..., 0::2], w[..., 1::2]], -1)
        return w.reshape(C, H * D)

    def hidden(w):
        w = np.concatenate([w, np.zeros((C, JT * P - w.shape[1]), w.dtype)], 1)
        return w.reshape(KC, P, JT, P).transpose(2, 1, 0, 3)

    w_g = hidden(np.concatenate([g["L0_ffn_w_gate"].transpose(1, 0, 2).reshape(C, E * I), g["L0_ffn_sw_gate"]], 1))
    w_u = hidden(np.concatenate([g["L0_ffn_w_up"].transpose(1, 0, 2).reshape(C, E * I), g["L0_ffn_sw_up"]], 1))
    w_d = np.concatenate([g["L0_ffn_w_down"].reshape(E * I, C), g["L0_ffn_sw_down"]], 0)
    w_d = np.concatenate([w_d, np.zeros((JT * P - w_d.shape[0], C), w_d.dtype)], 0).reshape(JT, P, C)
    arrays = dict(
        x=g["x"].reshape(B * N, C), ctx_t=np.pad(g["ctx_2048"].transpose(0, 2, 1), ((0, 0), (0, 0), (0, LM - L))), mask=g["mask_BxSxS2_ff0"],
        wq=g["L0_xattn_wq"], wk_t=g["L0_xattn_wk"].T, wv_t=g["L0_xattn_wv"].T, wo=g["L0_xattn_wo"],
        bq=np.tile(g["L0_xattn_bq"].reshape(NG, G4).T, (2, 1)), bo_b=row(g["L0_xattn_bo"]), bv_b=row(g["L0_xattn_bv"]),
        w_qkvg=np.concatenate([heads(g["L0_attn_W_Q"], True), heads(g["L0_attn_W_K"], True),
                               heads(g["L0_attn_W_V"], False), g["L0_attn_W_G"]], 1),
        w_o=g["L0_attn_W_O"], gnw_b=row(g["L0_attn_gn_weight"]), gnb_b=row(g["L0_attn_gn_bias"]),
        gate_t=g["L0_ffn_gate_w"].T, w_gu=np.stack([w_g, w_u], 2), w_dn=w_d,
        bk=g["L0_xattn_bk"].reshape(KC, P).T, **shape_tables())
    arrays = {f"in_{k}": np.ascontiguousarray(v) for k, v in arrays.items()}
    nc = bacc.Bacc("TRN2", target_bir_lowering=False, num_devices=1)
    args = {k[3:]: nc.dram_tensor(k, a.shape, _mybir.dt.from_np(a.dtype), kind="ExternalInput").ap()
            for k, a in arrays.items()}
    out = nc.dram_tensor("out_0", (B * N, C), _mybir.dt.float32, kind="ExternalOutput").ap()
    perceiver_program(nc, out=out, **args)
    r = run(nc, [arrays], core_ids=[0])
    return r.results[0]["out_0"].reshape(B, N, C)
```
